# Optimizing a Trainium2 kernel written in Bass

```python
import numpy as np
import jax
import jax.numpy as jnp

def _softmax(x, axis=-1):
    return jax.nn.softmax(x, axis=axis)

def _gelu(x):
    return jax.nn.gelu(x, approximate=True)

def _silu(x):
    return jax.nn.silu(x)

def _sigmoid(x):
    return jax.nn.sigmoid(x)

def _layernorm(x, axis=-1, eps=1e-05):
    m = jnp.mean(x, axis=axis, keepdims=True)
    v = jnp.var(x, axis=axis, keepdims=True)
    return (x - m) / jnp.sqrt(v + eps)

def _scatter_add(tgt, idx, src, axis=0):
    return tgt.at[idx].add(src)

def _segment_sum(src, seg, n):
    return jax.ops.segment_sum(src, seg, n)
kernel_name = 'mk_early_fusion_d1_tok_img256_r4_c775e1'

def setup_inputs(seed: int=0):
    np.random.seed(seed)
    _w = jnp.asarray

    def _rec_inputs():
        import jax
        import jax.numpy as jnp
        _rk = jax.random.key(seed)
        x = -0.000395706 + 0.999959 * jax.random.normal(jax.random.fold_in(_rk, 1), (16, 1, 96, 96), jnp.float32)
        txt = -0.00371421 + 0.449605 * jax.random.normal(jax.random.fold_in(_rk, 2), (16, 128, 64), jnp.float32)
        return (x, txt)
    x, txt = _rec_inputs()

    def _L0_tok_setup():
        import jax, jax.numpy as jnp
        import numpy as np
        from jax import lax
        EMBED_DIM = 64
        key = jax.random.key(seed)
        ks = jax.random.split(key, 11)
        B, H, W = (64, 224, 224)
        D = EMBED_DIM
        x = jax.random.normal(ks[0], (B, 1, H, W), dtype=jnp.float32)
        conv_w = jax.random.normal(ks[1], (4, 1, 2, 2), dtype=jnp.float32) * 0.5
        conv_b = jax.random.normal(ks[2], (4,), dtype=jnp.float32) * 0.1
        s = 1.0 / np.sqrt(D)
        wq = jax.random.normal(ks[3], (D, D), dtype=jnp.float32) * s
        bq = jax.random.normal(ks[4], (D,), dtype=jnp.float32) * 0.02
        wk = jax.random.normal(ks[5], (D, D), dtype=jnp.float32) * s
        bk = jax.random.normal(ks[6], (D,), dtype=jnp.float32) * 0.02
        wv = jax.random.normal(ks[7], (D, D), dtype=jnp.float32) * s
        bv = jax.random.normal(ks[8], (D,), dtype=jnp.float32) * 0.02
        wo = jax.random.normal(ks[9], (D, D), dtype=jnp.float32) * s
        bo = jax.random.normal(ks[10], (D,), dtype=jnp.float32) * 0.02
        return {'x': x, 'conv_w': conv_w, 'conv_b': conv_b, 'wq': wq, 'bq': bq, 'wk': wk, 'bk': bk, 'wv': wv, 'bv': bv, 'wo': wo, 'bo': bo}
    _L0_tok_all = _L0_tok_setup()
    _L0_tok_in = {k: v for k, v in _L0_tok_all.items() if k in ('conv_w', 'conv_b', 'wq', 'bq', 'wk', 'bk', 'wv', 'bv', 'wo', 'bo')}
    del _L0_tok_all

    def _L0_attn_setup():
        import jax, jax.numpy as jnp
        import numpy as np
        import math
        D = 64
        K = 32
        B = 2
        L = 512
        MAX_SEQ = 2048
        PI = math.pi

        def _content_stream(x, Wk1, bk1, Wk2, bk2, Wq1, bq1, Wq2, bq2, Wvc, bvc):
            Bc, Lc, Dc = x.shape
            key_phase = jnp.tanh(jnp.tanh(x @ Wk1 + bk1) @ Wk2 + bk2) * PI
            query_phase = jnp.tanh(jnp.tanh(x @ Wq1 + bq1) @ Wq2 + bq2) * PI
            value = x @ Wvc + bvc
            cos_k = jnp.cos(key_phase)[..., None]
            sin_k = jnp.sin(key_phase)[..., None]
            v_e = value[:, :, None, :]
            mem_real = jnp.cumsum(cos_k * v_e, axis=1)
            mem_imag = jnp.cumsum(sin_k * v_e, axis=1)
            cos_q = jnp.cos(query_phase)[..., None]
            sin_q = jnp.sin(query_phase)[..., None]
            retrieved = (mem_real * cos_q + mem_imag * sin_q).sum(axis=2)
            positions = jnp.arange(1, Lc + 1, dtype=jnp.float32)
            norm = jnp.sqrt(positions * K)[None, :, None]
            return retrieved / norm

        def _pos_stream(x, base_phases, Wvp, bvp):
            Bc, Lc, Dc = x.shape
            phases = base_phases[:Lc][None]
            value = x @ Wvp + bvp
            cos_p = jnp.cos(phases)
            sin_p = jnp.sin(phases)
            mem_real = jnp.cumsum(value * cos_p, axis=1)
            mem_imag = jnp.cumsum(value * sin_p, axis=1)
            retrieved = mem_real * cos_p + mem_imag * sin_p
            positions = jnp.arange(1, Lc + 1, dtype=jnp.float32)
            return retrieved / jnp.sqrt(positions)[None, :, None]
        key = jax.random.key(seed)
        ks = jax.random.split(key, 24)
        s = 0.02
        inp = {}
        inp['x'] = jax.random.normal(ks[0], (B, L, D), dtype=jnp.float32)
        inp['base_phases'] = jax.random.normal(ks[1], (MAX_SEQ, D), dtype=jnp.float32) * PI
        inp['Wk1'] = jax.random.normal(ks[2], (D, D), dtype=jnp.float32) * s
        inp['bk1'] = jnp.zeros((D,), jnp.float32)
        inp['Wk2'] = jax.random.normal(ks[3], (D, K), dtype=jnp.float32) * s
        inp['bk2'] = jnp.zeros((K,), jnp.float32)
        inp['Wq1'] = jax.random.normal(ks[4], (D, D), dtype=jnp.float32) * s
        inp['bq1'] = jnp.zeros((D,), jnp.float32)
        inp['Wq2'] = jax.random.normal(ks[5], (D, K), dtype=jnp.float32) * s
        inp['bq2'] = jnp.zeros((K,), jnp.float32)
        inp['Wvc'] = jax.random.normal(ks[6], (D, D), dtype=jnp.float32) * s
        inp['bvc'] = jnp.zeros((D,), jnp.float32)
        inp['Wvp'] = jax.random.normal(ks[7], (D, D), dtype=jnp.float32) * s
        inp['bvp'] = jnp.zeros((D,), jnp.float32)
        inp['Wg1'] = jax.random.normal(ks[8], (D, D // 4), dtype=jnp.float32) * s
        inp['bg1'] = jnp.zeros((D // 4,), jnp.float32)
        inp['Wg2'] = jax.random.normal(ks[9], (D // 4, 2), dtype=jnp.float32) * s
        inp['bg2'] = jnp.zeros((2,), jnp.float32)
        inp['ln_g'] = jnp.ones((D,), jnp.float32)
        inp['ln_b'] = jnp.zeros((D,), jnp.float32)
        inp['Wo'] = jax.random.normal(ks[10], (D, D), dtype=jnp.float32) * s
        inp['bo'] = jnp.zeros((D,), jnp.float32)
        return inp
    _L0_attn_all = _L0_attn_setup()
    _L0_attn_in = {k: v for k, v in _L0_attn_all.items() if k in ('base_phases', 'Wk1', 'bk1', 'Wk2', 'bk2', 'Wq1', 'bq1', 'Wq2', 'bq2', 'Wvc', 'bvc', 'Wvp', 'bvp', 'Wg1', 'bg1', 'Wg2', 'bg2', 'ln_g', 'ln_b', 'Wo', 'bo')}
    del _L0_attn_all

    def _L0_ffn_setup():
        import jax, jax.numpy as jnp
        import numpy as np
        TOP_K = 2
        key = jax.random.key(seed)
        ks = jax.random.split(key, 4)
        B, L, D, H, E = (8, 1024, 64, 256, 8)
        s = 0.02
        return {'x': jax.random.normal(ks[0], (B, L, D), jnp.float32), 'Wg': jax.random.normal(ks[1], (D, E), jnp.float32) * s, 'bg': jnp.zeros((E,), jnp.float32), 'W1': jax.random.normal(ks[2], (E, D, H), jnp.float32) * s, 'b1': jnp.zeros((E, H), jnp.float32), 'W2': jax.random.normal(ks[3], (E, H, D), jnp.float32) * s, 'b2': jnp.zeros((E, D), jnp.float32)}
    _L0_ffn_all = _L0_ffn_setup()
    _L0_ffn_in = {k: v for k, v in _L0_ffn_all.items() if k in ('Wg', 'bg', 'W1', 'b1', 'W2', 'b2')}
    del _L0_ffn_all
    return {'x': x, 'txt': txt, 'L0_tok_conv_w': _L0_tok_in['conv_w'], 'L0_tok_conv_b': _L0_tok_in['conv_b'], 'L0_tok_wq': _L0_tok_in['wq'], 'L0_tok_bq': _L0_tok_in['bq'], 'L0_tok_wk': _L0_tok_in['wk'], 'L0_tok_bk': _L0_tok_in['bk'], 'L0_tok_wv': _L0_tok_in['wv'], 'L0_tok_bv': _L0_tok_in['bv'], 'L0_tok_wo': _L0_tok_in['wo'], 'L0_tok_bo': _L0_tok_in['bo'], 'L0_attn_base_phases': _L0_attn_in['base_phases'], 'L0_attn_Wk1': _L0_attn_in['Wk1'], 'L0_attn_bk1': _L0_attn_in['bk1'], 'L0_attn_Wk2': _L0_attn_in['Wk2'], 'L0_attn_bk2': _L0_attn_in['bk2'], 'L0_attn_Wq1': _L0_attn_in['Wq1'], 'L0_attn_bq1': _L0_attn_in['bq1'], 'L0_attn_Wq2': _L0_attn_in['Wq2'], 'L0_attn_bq2': _L0_attn_in['bq2'], 'L0_attn_Wvc': _L0_attn_in['Wvc'], 'L0_attn_bvc': _L0_attn_in['bvc'], 'L0_attn_Wvp': _L0_attn_in['Wvp'], 'L0_attn_bvp': _L0_attn_in['bvp'], 'L0_attn_Wg1': _L0_attn_in['Wg1'], 'L0_attn_bg1': _L0_attn_in['bg1'], 'L0_attn_Wg2': _L0_attn_in['Wg2'], 'L0_attn_bg2': _L0_attn_in['bg2'], 'L0_attn_ln_g': _L0_attn_in['ln_g'], 'L0_attn_ln_b': _L0_attn_in['ln_b'], 'L0_attn_Wo': _L0_attn_in['Wo'], 'L0_attn_bo': _L0_attn_in['bo'], 'L0_ffn_Wg': _L0_ffn_in['Wg'], 'L0_ffn_bg': _L0_ffn_in['bg'], 'L0_ffn_W1': _L0_ffn_in['W1'], 'L0_ffn_b1': _L0_ffn_in['b1'], 'L0_ffn_W2': _L0_ffn_in['W2'], 'L0_ffn_b2': _L0_ffn_in['b2']}

def reference(x, txt, L0_tok_conv_w, L0_tok_conv_b, L0_tok_wq, L0_tok_bq, L0_tok_wk, L0_tok_bk, L0_tok_wv, L0_tok_bv, L0_tok_wo, L0_tok_bo, L0_attn_base_phases, L0_attn_Wk1, L0_attn_bk1, L0_attn_Wk2, L0_attn_bk2, L0_attn_Wq1, L0_attn_bq1, L0_attn_Wq2, L0_attn_bq2, L0_attn_Wvc, L0_attn_bvc, L0_attn_Wvp, L0_attn_bvp, L0_attn_Wg1, L0_attn_bg1, L0_attn_Wg2, L0_attn_bg2, L0_attn_ln_g, L0_attn_ln_b, L0_attn_Wo, L0_attn_bo, L0_ffn_Wg, L0_ffn_bg, L0_ffn_W1, L0_ffn_b1, L0_ffn_W2, L0_ffn_b2):
    import jax
    import jax.numpy as jnp

    def _L0_tok_ref(x, conv_w, conv_b, wq, bq, wk, bk, wv, bv, wo, bo):
        import jax, jax.numpy as jnp
        import numpy as np
        from jax import lax
        EMBED_DIM = 64
        B = x.shape[0]
        D = EMBED_DIM
        feat = lax.conv_general_dilated(x, conv_w, window_strides=(2, 2), padding='VALID', dimension_numbers=('NCHW', 'OIHW', 'NCHW'))
        feat = feat + conv_b[None, :, None, None]
        qfeat = feat.reshape(B, -1)
        seq_len = qfeat.shape[1] // D
        qfeat = qfeat.reshape(B, seq_len, D)
        Q = jnp.einsum('bsd,ed->bse', qfeat, wq) + bq
        K = jnp.einsum('bsd,ed->bse', qfeat, wk) + bk
        V = jnp.einsum('bsd,ed->bse', qfeat, wv) + bv
        scores = jax.nn.softmax(jnp.einsum('bse,bte->bst', Q, K) / jnp.sqrt(jnp.float32(D)), axis=-1)
        attn_out = jnp.einsum('bst,bte->bse', scores, V)
        out = jnp.einsum('bse,fe->bsf', attn_out, wo) + bo
        return out

    def _L0_attn_ref(x, base_phases, Wk1, bk1, Wk2, bk2, Wq1, bq1, Wq2, bq2, Wvc, bvc, Wvp, bvp, Wg1, bg1, Wg2, bg2, ln_g, ln_b, Wo, bo):
        import jax, jax.numpy as jnp
        import numpy as np
        import math
        D = 64
        K = 32
        B = 2
        L = 512
        MAX_SEQ = 2048
        PI = math.pi

        def _content_stream(x, Wk1, bk1, Wk2, bk2, Wq1, bq1, Wq2, bq2, Wvc, bvc):
            Bc, Lc, Dc = x.shape
            key_phase = jnp.tanh(jnp.tanh(x @ Wk1 + bk1) @ Wk2 + bk2) * PI
            query_phase = jnp.tanh(jnp.tanh(x @ Wq1 + bq1) @ Wq2 + bq2) * PI
            value = x @ Wvc + bvc
            cos_k = jnp.cos(key_phase)[..., None]
            sin_k = jnp.sin(key_phase)[..., None]
            v_e = value[:, :, None, :]
            mem_real = jnp.cumsum(cos_k * v_e, axis=1)
            mem_imag = jnp.cumsum(sin_k * v_e, axis=1)
            cos_q = jnp.cos(query_phase)[..., None]
            sin_q = jnp.sin(query_phase)[..., None]
            retrieved = (mem_real * cos_q + mem_imag * sin_q).sum(axis=2)
            positions = jnp.arange(1, Lc + 1, dtype=jnp.float32)
            norm = jnp.sqrt(positions * K)[None, :, None]
            return retrieved / norm

        def _pos_stream(x, base_phases, Wvp, bvp):
            Bc, Lc, Dc = x.shape
            phases = base_phases[:Lc][None]
            value = x @ Wvp + bvp
            cos_p = jnp.cos(phases)
            sin_p = jnp.sin(phases)
            mem_real = jnp.cumsum(value * cos_p, axis=1)
            mem_imag = jnp.cumsum(value * sin_p, axis=1)
            retrieved = mem_real * cos_p + mem_imag * sin_p
            positions = jnp.arange(1, Lc + 1, dtype=jnp.float32)
            return retrieved / jnp.sqrt(positions)[None, :, None]
        pos_retrieved = _pos_stream(x, base_phases, Wvp, bvp)
        content_retrieved = _content_stream(x, Wk1, bk1, Wk2, bk2, Wq1, bq1, Wq2, bq2, Wvc, bvc)
        gates = jax.nn.softmax(jax.nn.relu(x @ Wg1 + bg1) @ Wg2 + bg2, axis=-1)
        combined = gates[:, :, 0:1] * pos_retrieved + gates[:, :, 1:2] * content_retrieved
        mu = combined.mean(axis=-1, keepdims=True)
        var = ((combined - mu) ** 2).mean(axis=-1, keepdims=True)
        normed = (combined - mu) / jnp.sqrt(var + 1e-05) * ln_g + ln_b
        return x + normed @ Wo + bo

    def _L0_ffn_ref(x, Wg, bg, W1, b1, W2, b2):
        import jax, jax.numpy as jnp
        import numpy as np
        TOP_K = 2
        B, L, D = x.shape
        E = W1.shape[0]
        xf = x.reshape(-1, D)
        gate_logits = xf @ Wg + bg
        top_w, top_i = jax.lax.top_k(gate_logits, TOP_K)
        top_w = jax.nn.softmax(top_w, axis=-1)
        w_dense = jnp.sum(jax.nn.one_hot(top_i, E, dtype=xf.dtype) * top_w[..., None], axis=1)
        out = jnp.zeros_like(xf)
        for e in range(E):
            h = jax.nn.gelu(xf @ W1[e] + b1[e], approximate=False)
            out = out + w_dense[:, e:e + 1] * (h @ W2[e] + b2[e])
        return out.reshape(B, L, D)
    h = _L0_tok_ref(x, L0_tok_conv_w, L0_tok_conv_b, L0_tok_wq, L0_tok_bq, L0_tok_wk, L0_tok_bk, L0_tok_wv, L0_tok_bv, L0_tok_wo, L0_tok_bo)
    h = jnp.concatenate([h, txt], axis=1)
    h = h + _L0_attn_ref(_layernorm(h, axis=-1), L0_attn_base_phases, L0_attn_Wk1, L0_attn_bk1, L0_attn_Wk2, L0_attn_bk2, L0_attn_Wq1, L0_attn_bq1, L0_attn_Wq2, L0_attn_bq2, L0_attn_Wvc, L0_attn_bvc, L0_attn_Wvp, L0_attn_bvp, L0_attn_Wg1, L0_attn_bg1, L0_attn_Wg2, L0_attn_bg2, L0_attn_ln_g, L0_attn_ln_b, L0_attn_Wo, L0_attn_bo)
    h = h + _L0_ffn_ref(_layernorm(h, axis=-1), L0_ffn_Wg, L0_ffn_bg, L0_ffn_W1, L0_ffn_b1, L0_ffn_W2, L0_ffn_b2)
    return h

_drawn_inputs = setup_inputs


def setup_inputs(seed=0):
    import zlib

    import numpy as np

    out = dict(_drawn_inputs(seed))
    spreads = {'L0_attn_bk1': (0.0, 0.8),
     'L0_attn_bk2': (0.0, 0.8),
     'L0_attn_bq1': (0.0, 0.8),
     'L0_attn_bq2': (0.0, 0.8),
     'L0_attn_bvc': (0.0, 0.1),
     'L0_attn_bvp': (0.0, 0.8),
     'L0_attn_bg1': (0.0, 0.8),
     'L0_attn_bg2': (0.0, 0.8),
     'L0_attn_ln_g': (1.0, 0.6),
     'L0_attn_ln_b': (0.0, 0.605),
     'L0_attn_bo': (0.0, 0.1),
     'L0_ffn_bg': (0.0, 0.1),
     'L0_ffn_b1': (0.0, 0.8),
     'L0_ffn_b2': (0.0, 0.1)}
    factors = {'L0_tok_bq': 4.559,
     'L0_tok_bk': 8.0,
     'L0_attn_base_phases': 8.0,
     'L0_attn_Wk1': 8.0,
     'L0_attn_Wk2': 8.0,
     'L0_attn_Wq1': 8.0,
     'L0_attn_Wq2': 8.0,
     'L0_attn_Wvp': 8.0,
     'L0_attn_Wg1': 8.0,
     'L0_attn_Wg2': 8.0,
     'L0_ffn_W1': 4.505,
     'L0_ffn_W2': 3.767}
    for name, (base, spread) in spreads.items():
        noise = np.random.default_rng([zlib.crc32(name.encode()), seed]).standard_normal(out[name].shape)
        drawn = base * np.exp(spread * noise) if base else spread * noise
        out[name] = jnp.asarray(drawn.astype(out[name].dtype))
    for name, factor in factors.items():
        out[name] = (out[name] * factor).astype(out[name].dtype)
    return out
```

```python
from contextlib import ExitStack

import numpy as np
import concourse.bass as bass
from concourse import mybir

F32 = mybir.dt.float32
F32R = mybir.dt.float32r
ACT = mybir.ActivationFunctionType
ALU = mybir.AluOpType
AX = mybir.AxisListType

B, IMG, D, TXT = 16, 96, 64, 128
CH = 4
PATCH = (IMG // 2) ** 2 // D
SI = CH * PATCH
SC = SI // 2
L = SI + TXT
NP = B // 2
COLS = NP * L
NWIN = COLS // 128
GW = [min(4, NWIN - g) for g in range(0, NWIN, 4)]
NG = len(GW)
E, HID = 8, 256
MCH = [(m, min(128, L - m)) for m in range(0, L, 128)]
MOFF = [0, L, 2 * L - 128]
MEND = MOFF[2] + L - 256
EPS = 1e-5
LAST_PAIR = [min(512 * g + 128 * GW[g] - 1, COLS - 1) // L for g in range(NG)]
LAST_GROUP = [(L * b + L - 1) // 512 for b in range(NP)]

TWO_PI_1 = 6.28125
TWO_PI_2 = float(np.float32(np.round((2 * np.pi - TWO_PI_1) * 2 ** 22) / 2 ** 22))
TWO_PI_3 = float(np.float32(2 * np.pi - TWO_PI_1 - TWO_PI_2))
ROUND = 1.5 * 2.0 ** 23
PI32 = 3.1415925

COL = {}
for _name, _n in [("conv_w", 16), ("conv_b", 4), ("bq", 1), ("bk", 1), ("bv", 1), ("bo", 1),
                  ("kq1", 1), ("k2", 1), ("q2", 1), ("vp", 1), ("ln_g", 1), ("ln_b", 1), ("b1", 16),
                  ("sign", 1), ("sin_scale", 1), ("sin_bias", 1), ("half_pi", 1)]:
    COL[_name] = (sum(n for _, n in COL.values()), _n)
NCOL = sum(n for _, n in COL.values())
ROW = {}
for _name, _n in [("bvc", 64), ("bo", 64), ("bg1", 16), ("wg2", 32), ("bg2", 2), ("bg", 8), ("rank", 8)]:
    ROW[_name] = (sum(n for _, n in ROW.values()), _n)
NROW = sum(n for _, n in ROW.values())
SPL = {}
for _name, _n in [("kq1", 128), ("vc", 64), ("vp", 256), ("g1", 16), ("gate", 8)]:
    SPL[_name] = (sum(n for _, n in SPL.values()), _n)
NSPL = sum(n for _, n in SPL.values())


def make_plan():
    slots = {}

    def put(slot, order, stage, i):
        slots.setdefault(slot, []).append((order, stage, i))

    for b in range(NP):
        put(b, 0, "qkv", b)
        put(b + 1, 1, "scores", b)
        put(b + 2, 4.5, "probs_t", b)
        put(b + 3, 3, "mix", b)
        put(b + 4, 4, "tok_out", b)
    for g in range(NG):
        s = LAST_PAIR[g] + 5
        put(s, 5, "h0_t", g)
        put(s, 6, "ln1_stats", g)
        put(s + 1, 5.5, "ln1_norm", g)
        put(s + 2, 6, "xn_t", g)
        put(s + 3, 7, "mix_gate", g)
    s3 = NP + 4
    for b in range(NP):
        put(s3 + b, 8, "hidden", b)
        put(s3 + b, 9, "values", b)
        put(s3 + b + 1, 7.5, "phases", b)
    s4 = s3 + NP + 1
    for b in range(NP):
        put(s4 - 1, 20 + b, "trig", b)
        put(s4 + b, 8, "memory", b)
        put(s4 + b + 1, 9, "recall", b)
    s5 = s4 + NP + 2
    for g in range(NG):
        for e in range(E):
            put(s5 + E * g + e, 10, "expert", E * g + e)
            put(s5 + E * g + e + 1, 10.5, "expert_out", E * g + e)
        put(s5 + E * g + E + 1, 10.7, "finish", g)
    for g in range(NG):
        s = [s4 + 3, s4 + 6, s5 + 4, s5 + 12, s5 + 20][g]
        d = 1 if g < 2 else 1
        put(s, 11, "combine", g)
        put(s, 12, "ln2_stats", g)
        put(s + d, 11.1, "ln2_norm", g)
        put(s + d * 2, 11.2, "norm_s", g)
        put(s + d * 3, 11.3, "attn_out", g)
        put(s + d * 3, 12.3, "ln3_stats", g)
        put(s + d * 4, 11.4, "ln3_norm", g)
        put(s + d * 5, 11.5, "xn2_t", g)
        put(s + d * 5, 12.5, "route", g)
        put(s + d * 6, 11.6, "route_bias", g)
    return [(stage, i) for s in sorted(slots) for _, stage, i in sorted(slots[s])]


PLAN = make_plan()


def fusion_block(nc, x_a, x_b, cols_d, tokw_d, phase_d, rows_d, attw_d, spl_d, txt_d, const_d, w1_d,
                 w2_d, b2_d, sel_d, out):
    with ExitStack() as ctx:
        def sb(name, shape, dt=F32):
            return ctx.enter_context(nc.sbuf_tensor(name, shape, dt))

        def sem(name):
            return ctx.enter_context(nc.semaphore(name))

        cols = sb("cols", [128, NCOL])
        rows = sb("rows", [128, NROW])
        tokw = sb("tokw", [128, 512])
        attw = sb("attw", [128, 192])
        ident = sb("ident", [128, 128])
        mask = sb("mask", [128, MEND])
        spl_raw = sb("spl_raw", [128, NSPL])
        spl_h = sb("spl_h", [128, NSPL], F32R)
        spl_l = sb("spl_l", [128, NSPL], F32R)
        w1_h = sb("w1_h", [128, E * HID], F32R)
        w1_l = sb("w1_l", [128, E * HID], F32R)
        w2 = sb("w2", [128, 16, 64])
        b2_raw = sb("b2_raw", [32, 128])
        b2_h = sb("b2_h", [32, 128], F32R)
        b2_l = sb("b2_l", [32, 128], F32R)
        sel = sb("sel", [32, E, 128], F32R)
        gate_hl = sb("gate_hl", [128, 2, 24], F32R)
        minus_half = sb("minus_half", [128, 8])
        phase = sb("phase", [128, 2, L])
        turns = sb("turns", [128, L])
        turn_part = sb("turn_part", [128, L])
        cos_p = sb("cos_p", [128, L])
        sin_p = sb("sin_p", [128, L])
        cos_n = sb("cos_n", [128, L])
        sin_n = sb("sin_n", [128, L])
        arena = sb("arena", [128, 4, 1024])
        flat = arena[:, :, :].rearrange("p a b -> p (a b)")
        hidden_e = arena
        pix = flat[:, 0:1152].rearrange("p (v t b s) -> p v t (b s)", v=2, t=4, b=4)
        feat = flat[:, 1152:2304].rearrange("p (b c s) -> p b c s", b=NP, c=CH)
        featf = flat[:, 1152:2304].rearrange("p (b s) -> p b s", b=NP)
        w1_raw = sb("w1_raw", [128, E * HID])
        early = sb("early", [128, 2 * NP * SI])
        qs = early[:, 0:NP * SI].rearrange("p (b s) -> p b s", b=NP)
        ks = early[:, NP * SI:].rearrange("p (b s) -> p b s", b=NP)
        y = early[:, 0:4 * L].rearrange("p (n k t) -> p n k t", n=2, k=2)
        cum = early[:, 4 * L:8 * L].rearrange("p (n k t) -> p n k t", n=2, k=2)
        vs = sb("vs", [128, 4, 256])
        early_p = sb("early_p", [128, 16 * SI])
        probs = early_p[:, 0:8 * SI].rearrange("p (n k s) -> p n k s", n=2, k=4)
        probs_t = early_p[:, 8 * SI:].rearrange("p (n h s) -> p n h s", n=2, h=2)
        mem = early_p[:, 0:4 * MEND].rearrange("p (n h s) -> p n h s", n=2, h=2)
        negmax = sb("negmax", [128, 2, 4])
        rsum = sb("rsum", [128, 2, 4])
        rinv = sb("rinv", [128, 2, 4])
        mixed = sb("mixed", [128, 2, SI])
        h0s = sb("h0s", [128, NP, L])
        h0f = h0s[:, :, :].rearrange("p b l -> p (b l)")
        res = sb("res", [128, NWIN * 128])
        xn = sb("xn", [128, 2, 512])
        hl = sb("hl", [128, 2, 8, 2, 64])
        xhl = sb("xhl", [128, 2, COLS], F32R)
        stat = sb("stat", [128, 2, 8, 6])
        mean = sb("mean", [128, 2, 8])
        msum = sb("msum", [128, 8])
        mdif = sb("mdif", [128, 8])
        msq = sb("msq", [128, 8])
        mvar = sb("mvar", [128, 8])
        vare = sb("vare", [128, 2, 8])
        rstd = sb("rstd", [128, 2, 8])
        hid = sb("hid", [128, 2, 2, L])
        trig = sb("trig", [128, 2, COLS])
        vc = sb("vc", [128, NP, 384])
        ones = sb("ones", [128, L])
        cons = sb("cons", [128, COLS])
        gu = sb("gu", [128, 8, 16])
        gd = sb("gd", [128, 16])
        gb = sb("gb", [128, 1])
        zg = sb("zg", [128, NG, 8])
        tg = sb("tg", [128, NG, 8])
        p0 = sb("p0", [128, NG, 8])
        p1 = sb("p1", [128, NG, 8])
        c1 = sb("c1", [128, 512])
        c2 = sb("c2", [128, 512])
        comb = sb("comb", [128, 2, 512])
        ns = sb("ns", [128, 2, 512])
        lg = sb("lg", [128, 8, 8])
        eq = sb("eq", [128, 8, 8])
        k1 = sb("k1", [128, 8, 8])
        k2 = sb("k2", [128, 8, 8])
        top = sb("top", [128, 4, 8])
        dl = sb("dl", [128, NG, 8])
        tl = sb("tl", [128, NG, 8])
        wsp = sb("wsp", [128, 4, 2, 16])
        wt = sb("wt", [32, 2, 512], F32R)
        scaled = sb("scaled", [128, 2, 512])
        acc = w1_raw[:, 0:1024].rearrange("p (n c) -> p n c", n=2)
        wide = w1_raw[:, 1024:2048].rearrange("p (n c) -> p n c", n=2)
        sel_raw = comb[0:32, :, :].rearrange("p n c -> p (n c)").rearrange("p (e c) -> p e c", e=E)

        ps = ctx.enter_context(nc.psum_tensor("ps", [128, 8, 512], F32))

        ld = {n: sem("ld_" + n) for n in ("pixa", "pixb", "cols", "tokw", "phase", "rows", "attw", "spl",
                                          "txt", "ident", "mask", "w1", "w2", "b2", "sel")}
        S = {n: sem(n) for n in (
            "conv", "qk_mm", "v_mm", "qk_sb", "v_sb", "score_mm", "rowmax", "exps", "rowinv", "pnorm",
            "pt_mm", "pt_v", "pt_a", "mix_mm", "mix_sb", "tok_mm", "h0_sb",
            "ht_mm", "h0t", "xt_mm", "xhl_sb", "mg_mm", "mg_z", "mg_t", "mg_p", "res_bo", "res_1",
            "split", "w1split", "hid_mm", "hid_sb", "vp_mm", "vp_used", "vc_mm", "vc_sb", "ph_mm", "ph_sb",
            "ph_abs", "trig_sb", "cum_sb", "pos_sb", "reduced", "base_abs", "base_trig", "base_n", "consts",
            "mem_mm", "mem_sb", "rec_mm", "rec_sb", "comb_mm", "comb_sb", "ns_mm", "ns_sb",
            "ao_mm", "h1_sb", "lg_mm", "route_d", "route_t", "route_w", "wt_mm", "wt_sb", "rb_mm", "rb_sb",
            "e1_mm", "gelu", "e2_mm", "scaled_sb", "acc_sb", "stored", "small", "wide_mm", "wide_sb",
            "fin_mm", "out_sb", "vchain", "pchain", "lg_sb")}
        var_ok = [sem(f"var{k}") for k in range(3)]
        rstd_ok = [sem(f"rstd{k}") for k in range(3)]
        hl_ok = [sem(f"hl{k}") for k in range(3)]

        def col(name, i=0, lo=0, hi=128):
            c = COL[name][0] + i
            return cols[lo:hi, c:c + 1]

        def row(name):
            a, n = ROW[name]
            return rows[:, a:a + n]

        def split(part, name):
            a, n = SPL[name]
            return part[:, a:a + n]

        def blocks(ap, width=64):
            return ap.rearrange("p (k d) -> p k d", d=width)

        def spread(ap, n, width=64):
            return ap.unsqueeze(2).to_broadcast([128, n, width])

        def over(ap, n):
            return ap.unsqueeze(1).to_broadcast([128, n, ap.shape[-1]])

        def nb(g):
            return 2 * GW[g]

        def cut(g):
            return slice(512 * g, 512 * g + 128 * GW[g])

        def xt_steps(g):
            return [range(w, min(w + 2, GW[g])) for w in range(0, GW[g], 2)]

        XT_DONE = [sum(len(xt_steps(k)) for k in range(g + 1)) for g in range(NG)]
        NXT = XT_DONE[-1]
        BLK_BEFORE = [sum(nb(k) for k in range(g)) for g in range(NG)]

        block = ctx.enter_context(nc.Block())

        @block.sync
        def _(sp):
            sp.dma_start(pix[:, 0, :, :], x_a).then_inc(ld["pixa"], 16)
            sp.dma_start(tokw[:, :], tokw_d).then_inc(ld["tokw"], 16)
            sp.dma_start(pix[:, 1, :, :], x_b).then_inc(ld["pixb"], 16)
            sp.dma_start(h0s[:, :, SI:L], txt_d).then_inc(ld["txt"], 16)
            sp.dma_start(spl_raw[:, :], spl_d).then_inc(ld["spl"], 16)
            sp.dma_start(attw[:, :], attw_d).then_inc(ld["attw"], 16)
            sp.dma_start(mask[:, :], const_d[:, 128:]).then_inc(ld["mask"], 16)
            sp.dma_start(w1_raw[:, :], w1_d).then_inc(ld["w1"], 16)
            sp.dma_start(w2[:, :, :], w2_d).then_inc(ld["w2"], 16)
            sp.dma_start(b2_raw[:, :], b2_d).then_inc(ld["b2"], 16)
            sp.dma_start(sel_raw, sel_d).then_inc(ld["sel"], 16)
            for g in range(NG):
                sp.wait_ge(S["out_sb"], g + 1)
                for h in range(2):
                    dst = out[COLS * h + 512 * g:COLS * h + 512 * g + 128 * GW[g], :]
                    src = res[:, cut(g)].rearrange("p (w h d) -> p w h d", h=2, d=64)[:, :, h, :]
                    sp.dma_start(dst.rearrange("(w p) d -> p w d", p=128), src).then_inc(S["stored"], 16)
            sp.wait_ge(S["stored"], 16 * 2 * NG)

        @block.gpsimd
        def _(pool):
            steps = [0]

            def link(ins):
                steps[0] += 1
                ins.then_inc(S["pchain"], 1)
                pool.wait_ge(S["pchain"], steps[0])

            pool.memset(minus_half[:, :], -0.5)
            pool.memset(ones[:, :], 1.0).then_inc(S["consts"], 1)
            pool.wait_ge(ld["phase"], 16)
            raw = phase[:, 0, :]
            link(pool.tensor_scalar(turns[:, :], raw, float(1 / (2 * np.pi)), ROUND, ALU.mult, ALU.add))
            link(pool.tensor_scalar(turns[:, :], turns[:, :], ROUND, None, ALU.subtract))
            for part in (TWO_PI_1, TWO_PI_2, TWO_PI_3):
                link(pool.tensor_scalar(turn_part[:, :], turns[:, :], part, None, ALU.mult))
                link(pool.tensor_tensor(raw, raw, turn_part[:, :], ALU.subtract))
            pool.tensor_scalar(raw, raw, PI32, -PI32, ALU.min, ALU.max).then_inc(S["reduced"], 1)
            pool.wait_ge(S["base_trig"], 1)
            pool.tensor_tensor(cos_n[:, :], cos_p[:, :], phase[:, 1, :], ALU.mult)
            pool.tensor_tensor(sin_n[:, :], sin_p[:, :], phase[:, 1, :], ALU.mult).then_inc(S["base_n"], 1)
            pool.wait_ge(S["base_n"], 1)
            pool.wait_ge(ld["w1"], 16)
            link(pool.tensor_scalar(w1_h[:, :], w1_raw[:, :], 1.0, None, ALU.mult))
            pool.tensor_tensor(w1_l[:, :], w1_raw[:, :], w1_h[:, :].bitcast(F32), ALU.subtract)\
                .then_inc(S["w1split"], 1)

            def root(kind, g):
                pool.wait_ge(var_ok[kind], g + 1)
                pool.tensor_tensor(rstd[:, g % 2, 0:nb(g)], vare[:, g % 2, 0:nb(g)],
                                   minus_half[:, 0:nb(g)], ALU.pow).then_inc(rstd_ok[kind], 1)

            for stage, i in PLAN:
                if stage == "ln1_stats":
                    root(0, i)
                elif stage == "ln1_norm":
                    pool.wait_ge(hl_ok[0], i + 1)
                    pool.wait_ge(ld["rows"], 16)
                    pool.tensor_tensor(blocks(res[:, cut(i)]), blocks(res[:, cut(i)]),
                                       over(row("bo"), nb(i)), ALU.add).then_inc(S["res_bo"], 1)
                    pool.wait_ge(S["res_bo"], i + 1)
                    pool.tensor_tensor(res[:, cut(i)], res[:, cut(i)], xn[:, i % 2, 0:128 * GW[i]],
                                       ALU.add).then_inc(S["res_1"], 1)
                elif stage == "values":
                    pool.wait_ge(S["cum_sb"], i + 1)
                    link(pool.tensor_tensor(cum[:, i % 2, 0, :], cum[:, i % 2, 0, :], cos_n[:, :], ALU.mult))
                    link(pool.tensor_tensor(cum[:, i % 2, 1, :], cum[:, i % 2, 1, :], sin_n[:, :], ALU.mult))
                    pool.tensor_tensor(h0s[:, i, :], cum[:, i % 2, 0, :], cum[:, i % 2, 1, :],
                                       ALU.add).then_inc(S["pos_sb"], 1)
                elif stage == "ln2_stats":
                    root(1, i)
                elif stage == "ln3_stats":
                    root(2, i)
                elif stage == "expert_out":
                    g = i // E
                    pool.wait_ge(S["scaled_sb"], i + 1)
                    pool.wait_ge(S["rb_sb"], g + 1)
                    if i > 0:
                        pool.wait_ge(S["acc_sb"], i)
                    pool.tensor_tensor(acc[:, g % 2, 0:128 * GW[g]], acc[:, g % 2, 0:128 * GW[g]],
                                       scaled[:, i % 2, 0:128 * GW[g]], ALU.add).then_inc(S["acc_sb"], 1)

        @block.scalar
        def _(act):
            act.dma_start(phase[:, :, :], phase_d).then_inc(ld["phase"], 16)
            act.dma_start(cols[:, :], cols_d).then_inc(ld["cols"], 16)
            act.dma_start(ident[:, :], const_d[:, 0:128]).then_inc(ld["ident"], 16)
            act.dma_start(rows[:, :], rows_d).then_inc(ld["rows"], 16)
            act.wait_ge(ld["cols"], 16)
            act.wait_ge(S["reduced"], 1)
            act.activation(sin_p[:, :], phase[:, 0, :], ACT.Sin)
            act.activation(turns[:, :], phase[:, 0, :], ACT.Abs).then_inc(S["base_abs"], 1)
            act.wait_ge(S["base_abs"], 1)
            act.activation(cos_p[:, :], turns[:, :], ACT.Sin, scale=-1.0, bias=col("half_pi"))\
                .then_inc(S["base_trig"], 1)

            for stage, i in PLAN:
                if stage == "qkv":
                    act.wait_ge(S["v_mm"], i + 1)
                    if i >= 4:
                        act.wait_ge(S["mix_mm"], i - 3)
                    act.activation(vs[0:SC, i % 4, :], ps[0:SC, 1, 0:256], ACT.Copy).then_inc(S["v_sb"], 1)
                elif stage == "scores":
                    act.wait_ge(S["rowmax"], i + 1)
                    for k in range(4):
                        ins = act.activation(probs[0:SC, i % 2, k, :],
                                             ps[0:SC, 2 + 2 * (i % 2) + k // 2, SI * (k % 2):SI * (k % 2) + SI],
                                             ACT.Exp, bias=negmax[0:SC, i % 2, k:k + 1],
                                             accum_out=rsum[0:SC, i % 2, k:k + 1])
                    ins.then_inc(S["exps"], 1)
                elif stage == "probs_t":
                    act.wait_ge(S["pt_mm"], i + 1)
                    act.activation(probs_t[0:SC, i % 2, 1, :], ps[0:SC, 3 + 2 * (i % 2), 0:2 * SI], ACT.Copy)\
                        .then_inc(S["pt_a"], 1)
                elif stage == "mix":
                    act.wait_ge(S["mix_mm"], i + 1)
                    act.activation(mixed[:, i % 2, :], ps[:, 1, 0:SI], ACT.Identity, bias=col("bv"))\
                        .then_inc(S["mix_sb"], 1)
                elif stage == "tok_out":
                    act.wait_ge(S["tok_mm"], i + 1)
                    act.activation(h0s[:, i, 0:SI], ps[:, 0, 0:SI], ACT.Identity, bias=col("bo"))\
                        .then_inc(S["h0_sb"], 1)
                elif stage == "h0_t":
                    act.wait_ge(S["ht_mm"], i + 1)
                    act.activation(res[:, cut(i)], ps[:, 6, 0:128 * GW[i]], ACT.Copy).then_inc(S["h0t"], 1)
                elif stage in ("xn_t", "xn2_t"):
                    base = 0 if stage == "xn_t" else NXT
                    for s, ws in enumerate(xt_steps(i)):
                        n = base + XT_DONE[i] - len(xt_steps(i)) + s
                        act.wait_ge(S["xt_mm"], n + 1)
                        c = 512 * i + 128 * ws[0]
                        act.activation(xhl[:, :, c:c + 128 * len(ws)].rearrange("p h (w t) -> p w h t", t=128),
                                       ps[:, 7, 0:256 * len(ws)].rearrange("p (w h t) -> p w h t", h=2, t=128),
                                       ACT.Copy).then_inc(S["xhl_sb"], 1)
                elif stage == "mix_gate":
                    act.wait_ge(S["mg_z"], i + 1)
                    act.activation(tg[:, i, 0:nb(i)], zg[:, i, 0:nb(i)], ACT.Tanh, scale=0.5)\
                        .then_inc(S["mg_t"], 1)
                elif stage == "hidden":
                    act.wait_ge(S["hid_mm"], i + 1)
                    if i >= 2:
                        act.wait_ge(S["ph_mm"], i - 1)
                    act.activation(hid[:, i % 2, :, :], ps[:, 0:2, 0:L], ACT.Tanh, bias=col("kq1"))\
                        .then_inc(S["hid_sb"], 1)
                elif stage == "phases":
                    act.wait_ge(S["ph_mm"], i + 1)
                    act.activation(trig[:, 0, L * i:L * i + L], ps[:, 2, 0:L], ACT.Tanh, bias=col("k2"))
                    act.activation(trig[:, 1, L * i:L * i + L], ps[:, 3, 0:L], ACT.Tanh, bias=col("q2"))\
                        .then_inc(S["ph_sb"], 1)
                elif stage == "trig":
                    act.wait_ge(S["ph_abs"], i + 1)
                    act.activation(trig[:, :, L * i:L * i + L], trig[:, :, L * i:L * i + L], ACT.Sin,
                                   scale=col("sin_scale"), bias=col("sin_bias")).then_inc(S["trig_sb"], 1)
                elif stage == "recall":
                    act.wait_ge(S["rec_mm"], i + 1)
                    act.activation(cons[:, L * i:L * i + L], ps[:, 4 + i % 2, 0:L], ACT.Copy)\
                        .then_inc(S["rec_sb"], 1)
                elif stage == "norm_s":
                    act.wait_ge(S["ns_mm"], i + 1)
                    if i >= 2:
                        act.wait_ge(S["ao_mm"], i - 1)
                    act.activation(ns[:, i % 2, 0:128 * GW[i]], ps[:, 6, 0:128 * GW[i]], ACT.Identity,
                                   scale=col("ln_g"), bias=col("ln_b")).then_inc(S["ns_sb"], 1)
                elif stage == "route":
                    act.wait_ge(S["route_d"], i + 1)
                    act.activation(tl[:, i, 0:nb(i)], dl[:, i, 0:nb(i)], ACT.Tanh, scale=0.5)\
                        .then_inc(S["route_t"], 1)
                elif stage == "route_bias":
                    act.wait_ge(S["wt_mm"], i + 1)
                    if i >= 2:
                        act.wait_ge(S["wide_mm"], E * (i - 1))
                    act.activation(wt[:, i % 2, 0:128 * GW[i]], ps[0:32, 6, 0:128 * GW[i]], ACT.Copy)\
                        .then_inc(S["wt_sb"], 1)
                elif stage == "expert":
                    g = i // E
                    n = 128 * GW[g]
                    for j in range(2):
                        k = 2 * i + j
                        act.wait_ge(S["e1_mm"], k + 1)
                        if i >= 2:
                            act.wait_ge(S["e2_mm"], i - 1)
                        act.activation(hidden_e[:, k % 4, 0:2 * n].rearrange("p (h t) -> p h t", h=2),
                                       ps[:, 2 * j:2 * j + 2, 0:n], ACT.Gelu, bias=col("b1", 2 * (i % E) + j))\
                            .then_inc(S["gelu"], 1)
                    act.wait_ge(S["wide_mm"], i + 1)
                    if i >= 2:
                        act.wait_ge(S["scaled_sb"], i - 1)
                    act.activation(wide[:, i % 2, 0:n], ps[:, 4 + i % 2, 0:n], ACT.Copy).then_inc(S["wide_sb"], 1)

        @block.vector
        def _(dve):
            steps = [0]

            def link(ins):
                steps[0] += 1
                ins.then_inc(S["vchain"], 1)
                dve.wait_ge(S["vchain"], steps[0])

            dve.wait_ge(ld["cols"], 16)
            for v in range(2):
                dve.wait_ge(ld["pixa" if v == 0 else "pixb"], 16)
                for tap in range(4):
                    for c in range(CH):
                        o = feat[:, 4 * v:4 * v + 4, c, :]
                        p = pix[:, v, tap, :].rearrange("p (b s) -> p b s", b=4)
                        n = 16 * v + 4 * tap + c
                        if tap == 0:
                            ins = dve.tensor_scalar(o, p, col("conv_w", 4 * c), col("conv_b", c),
                                                    ALU.mult, ALU.add)
                        else:
                            dve.wait_ge(S["conv"], n - 3)
                            ins = dve.scalar_tensor_tensor(out=o, in0=p, scalar=col("conv_w", 4 * c + tap),
                                                           in1=o, op0=ALU.mult, op1=ALU.add)
                        ins.then_inc(S["conv"], 1)
                if v == 0:
                    dve.wait_ge(ld["spl"], 16)
                    link(dve.tensor_copy(spl_h[:, :], spl_raw[:, :]))
                    dve.tensor_tensor(spl_l[:, :], spl_raw[:, :], spl_h[:, :].bitcast(F32), ALU.subtract)\
                        .then_inc(S["split"], 1)
            dve.wait_ge(ld["rows"], 16)
            dve.wait_ge(S["split"], 1)
            dve.tensor_copy(gate_hl[:, 0, :], spl_h[:, NSPL - 24:NSPL].bitcast(F32))
            dve.tensor_copy(gate_hl[:, 1, :], spl_l[:, NSPL - 24:NSPL].bitcast(F32)).then_inc(S["split"], 1)
            wg2 = row("wg2").rearrange("p (a k) -> p a k", a=2)
            dve.tensor_tensor(gd[:, :], wg2[:, 0, :], wg2[:, 1, :], ALU.subtract)
            link(dve.tensor_tensor(gb[:, :], row("bg2")[:, 0:1], row("bg2")[:, 1:2], ALU.subtract))

            def small_weights():
                dve.wait_ge(ld["b2"], 16)
                dve.wait_ge(ld["sel"], 16)
                link(dve.tensor_copy(b2_h[:, :], b2_raw[:, :]))
                dve.tensor_tensor(b2_l[:, :], b2_raw[:, :], b2_h[:, :].bitcast(F32), ALU.subtract)
                dve.tensor_copy(sel[:, :, :], sel_raw).then_inc(S["small"], 1)

            def moments(kind, g, src):
                n = nb(g)
                st = stat[:, g % 2, 0:n, :]
                for k in range(n):
                    ins = dve.bn_stats(stat[:, g % 2, k, :], src[:, 64 * k:64 * k + 64])
                link(ins)
                dve.tensor_tensor(msum[:, 0:n], st[:, :, 1], st[:, :, 4], ALU.add)
                dve.tensor_tensor(mvar[:, 0:n], st[:, :, 2], st[:, :, 5], ALU.add)
                link(dve.tensor_tensor(mdif[:, 0:n], st[:, :, 1], st[:, :, 4], ALU.subtract))
                dve.tensor_scalar(mean[:, g % 2, 0:n], msum[:, 0:n], 0.5, None, ALU.mult)
                link(dve.tensor_tensor(msq[:, 0:n], mdif[:, 0:n], mdif[:, 0:n], ALU.mult))
                link(dve.scalar_tensor_tensor(out=mvar[:, 0:n], in0=msq[:, 0:n], scalar=16.0,
                                              in1=mvar[:, 0:n], op0=ALU.mult, op1=ALU.add))
                dve.tensor_scalar(vare[:, g % 2, 0:n], mvar[:, 0:n], 1.0 / 64, EPS, ALU.mult, ALU.add)\
                    .then_inc(var_ok[kind], 1)

            def normalise(kind, g, src, dst):
                dve.wait_ge(rstd_ok[kind], g + 1)
                for k in range(nb(g)):
                    ins = dve.tensor_scalar(dst[:, 64 * k:64 * k + 64], src[:, 64 * k:64 * k + 64],
                                            mean[:, g % 2, k:k + 1], rstd[:, g % 2, k:k + 1],
                                            ALU.subtract, ALU.mult)
                return ins

            def split_tokens(kind, g):
                n = nb(g)
                x = blocks(xn[:, g % 2, 0:64 * n])
                link(dve.tensor_copy(hl[:, g % 2, 0:n, 0, :].bitcast(F32R), x))
                dve.tensor_tensor(hl[:, g % 2, 0:n, 1, :], x, hl[:, g % 2, 0:n, 0, :], ALU.subtract)\
                    .then_inc(hl_ok[kind], 1)

            def pick(n, values, one_hot, best):
                link(dve.tensor_reduce(best, values, AX.X, ALU.max))
                link(dve.tensor_tensor(eq[:, 0:n, :], values, spread(best, n, 8), ALU.is_equal))
                link(dve.tensor_tensor(eq[:, 0:n, :], eq[:, 0:n, :], over(row("rank"), n), ALU.mult))
                link(dve.tensor_reduce(top[:, 3, 0:n], eq[:, 0:n, :], AX.X, ALU.max))
                link(dve.tensor_tensor(one_hot, eq[:, 0:n, :], spread(top[:, 3, 0:n], n, 8), ALU.is_equal))

            for stage, i in PLAN:
                if stage == "qkv":
                    dve.wait_ge(S["qk_mm"], i + 1)
                    dve.tensor_scalar(qs[:, i, :], ps[:, 0, 0:SI], col("bq"), float(D) ** -0.5, ALU.add, ALU.mult)
                    dve.tensor_scalar(ks[:, i, :], ps[:, 0, SI:2 * SI], col("bk"), None, ALU.add)\
                        .then_inc(S["qk_sb"], 1)
                elif stage == "scores":
                    dve.wait_ge(S["score_mm"], i + 1)
                    b0 = 2 + 2 * (i % 2)
                    dve.tensor_reduce(negmax[0:SC, i % 2, :].rearrange("p (h c) -> p h c", h=2),
                                      ps[0:SC, b0:b0 + 2, 0:2 * SI].rearrange("p h (c t) -> p h c t", c=2),
                                      AX.X, ALU.max, negate=True).then_inc(S["rowmax"], 1)
                elif stage == "probs_t":
                    dve.wait_ge(S["exps"], i + 1)
                    dve.reciprocal(rinv[0:SC, i % 2, :], rsum[0:SC, i % 2, :]).then_inc(S["rowinv"], 1)
                    dve.wait_ge(S["rowinv"], i + 1)
                    dve.tensor_tensor(probs[0:SC, i % 2, :, :], probs[0:SC, i % 2, :, :],
                                      rinv[0:SC, i % 2, :].unsqueeze(2).to_broadcast([SC, 4, SI]), ALU.mult)\
                        .then_inc(S["pnorm"], 1)
                    dve.wait_ge(S["pt_mm"], i + 1)
                    dve.tensor_copy(probs_t[0:SC, i % 2, 0, :], ps[0:SC, 2 + 2 * (i % 2), 0:2 * SI])\
                        .then_inc(S["pt_v"], 1)
                elif stage == "ln1_stats":
                    dve.wait_ge(S["h0t"], i + 1)
                    moments(0, i, res[:, cut(i)])
                elif stage == "ln1_norm":
                    if i >= 2:
                        dve.wait_ge(S["res_1"], i - 1)
                        dve.wait_ge(S["xt_mm"], XT_DONE[i - 2])
                    link(normalise(0, i, res[:, cut(i)], xn[:, i % 2, :]))
                    split_tokens(0, i)
                elif stage == "mix_gate":
                    n = nb(i)
                    dve.wait_ge(S["mg_mm"], i + 1)
                    link(dve.tensor_reduce(gu[:, 0:n, :],
                                           ps[:, 6, 0:32 * n].rearrange("p (k a j) -> p k j a", a=2, j=16),
                                           AX.X, ALU.add))
                    link(dve.tensor_tensor(gu[:, 0:n, :], gu[:, 0:n, :], over(row("bg1"), n), ALU.add))
                    link(dve.scalar_tensor_tensor(out=gu[:, 0:n, :], in0=gu[:, 0:n, :], scalar=0.0,
                                                  in1=over(gd[:, :], n), op0=ALU.max, op1=ALU.mult))
                    link(dve.tensor_reduce(zg[:, i, 0:n], gu[:, 0:n, :], AX.X, ALU.add))
                    dve.tensor_scalar(zg[:, i, 0:n], zg[:, i, 0:n], gb[:, 0:1], None, ALU.add)\
                        .then_inc(S["mg_z"], 1)
                    dve.wait_ge(S["mg_t"], i + 1)
                    dve.tensor_scalar(p0[:, i, 0:n], tg[:, i, 0:n], 0.5, 0.5, ALU.mult, ALU.add)
                    dve.tensor_scalar(p1[:, i, 0:n], tg[:, i, 0:n], -0.5, 0.5, ALU.mult, ALU.add)\
                        .then_inc(S["mg_p"], 1)
                elif stage == "values":
                    dve.wait_ge(S["vp_mm"], i + 1)
                    if i == 0:
                        dve.wait_ge(S["base_trig"], 1)
                        dve.wait_ge(S["consts"], 1)
                    if i >= 2:
                        dve.wait_ge(S["pos_sb"], i - 1)
                    for k, t in enumerate((cos_p, sin_p)):
                        ins = dve.scalar_tensor_tensor(out=y[:, i % 2, k, :], in0=ps[:, 4, 0:L], scalar=col("vp"),
                                                       in1=t[:, :], op0=ALU.add, op1=ALU.mult)
                    ins.then_inc(S["vp_used"], 1)
                    dve.wait_ge(S["vc_mm"], i + 1)
                    dve.tensor_tensor(blocks(vc[:, i, 0:256]), blocks(ps[:, 5, 0:256]), over(row("bvc"), 4), ALU.add)
                    tail = MCH[2][1]
                    dve.tensor_tensor(blocks(vc[0:tail, i, 256:384]), blocks(ps[0:tail, 5, 256:384]),
                                      row("bvc")[0:tail, :].unsqueeze(1).to_broadcast([tail, 2, 64]), ALU.add)\
                        .then_inc(S["vc_sb"], 1)
                    dve.wait_ge(S["vp_used"], i + 1)
                    for k in range(2):
                        ins = dve.tensor_tensor_scan(cum[:, i % 2, k, :], ones[:, :], y[:, i % 2, k, :], 0.0,
                                                     ALU.mult, ALU.add)
                    ins.then_inc(S["cum_sb"], 1)
                elif stage == "phases":
                    if i == 1:
                        small_weights()
                    dve.wait_ge(S["ph_sb"], i + 1)
                    t = trig[:, :, L * i:L * i + L]
                    dve.scalar_tensor_tensor(out=t, in0=t, scalar=col("sign"), in1=t, op0=ALU.mult, op1=ALU.max)\
                        .then_inc(S["ph_abs"], 1)
                elif stage == "memory":
                    dve.wait_ge(S["mem_mm"], i + 1)
                    if i == 0:
                        dve.wait_ge(ld["mask"], 16)
                    if i >= 2:
                        dve.wait_ge(S["rec_mm"], i - 1)
                    b0, full, tail = 2 * (i % 2), MOFF[2], MCH[2][1]
                    dve.tensor_tensor(mem[:, i % 2, :, 0:full], ps[:, b0:b0 + 2, 0:full],
                                      over(mask[:, 0:full], 2), ALU.mult)
                    dve.tensor_tensor(mem[0:tail, i % 2, :, full:MEND], ps[0:tail, b0:b0 + 2, full:MEND],
                                      mask[0:tail, full:MEND].unsqueeze(1).to_broadcast([tail, 2, tail]), ALU.mult)\
                        .then_inc(S["mem_sb"], 1)
                elif stage == "combine":
                    n = nb(i)
                    if i >= 2:
                        dve.wait_ge(S["ns_mm"], i - 1)
                    dve.wait_ge(S["comb_mm"], i + 1)
                    dve.wait_ge(S["mg_p"], i + 1)
                    dve.tensor_tensor(blocks(c1[:, 0:64 * n]), blocks(ps[:, 6, 0:64 * n]),
                                      spread(p0[:, i, 0:n], n), ALU.mult)
                    link(dve.tensor_tensor(blocks(c2[:, 0:64 * n]), blocks(ps[:, 7, 0:64 * n]),
                                           spread(p1[:, i, 0:n], n), ALU.mult))
                    dve.tensor_tensor(comb[:, i % 2, 0:64 * n], c1[:, 0:64 * n], c2[:, 0:64 * n], ALU.add)\
                        .then_inc(S["comb_sb"], 1)
                elif stage == "ln2_stats":
                    dve.wait_ge(S["comb_sb"], i + 1)
                    moments(1, i, comb[:, i % 2, :])
                elif stage == "ln2_norm":
                    normalise(1, i, comb[:, i % 2, :], comb[:, i % 2, :]).then_inc(hl_ok[1], 1)
                elif stage == "attn_out":
                    n = 64 * nb(i)
                    dve.wait_ge(S["ao_mm"], i + 1)
                    dve.wait_ge(S["res_1"], i + 1)
                    dve.tensor_tensor(res[:, cut(i)], ps[:, 7, 0:n], res[:, cut(i)], ALU.add).then_inc(S["h1_sb"], 1)
                elif stage == "ln3_stats":
                    dve.wait_ge(S["h1_sb"], i + 1)
                    moments(2, i, res[:, cut(i)])
                elif stage == "ln3_norm":
                    if i == 0:
                        dve.wait_ge(S["res_1"], NG)
                        dve.wait_ge(S["xt_mm"], NXT)
                    if i >= 2:
                        dve.wait_ge(S["xt_mm"], NXT + XT_DONE[i - 2])
                    link(normalise(2, i, res[:, cut(i)], xn[:, i % 2, :]))
                    split_tokens(2, i)
                elif stage == "route":
                    n = nb(i)
                    dve.wait_ge(S["lg_mm"], i + 1)
                    dve.tensor_reduce(lg[:, 0:n, :], ps[:, 6, 0:16 * n].rearrange("p (k a j) -> p k j a", a=2, j=8),
                                      AX.X, ALU.add).then_inc(S["lg_sb"], 1)
                    dve.wait_ge(S["lg_sb"], i + 1)
                    link(dve.tensor_tensor(lg[:, 0:n, :], lg[:, 0:n, :], over(row("bg"), n), ALU.add))
                    pick(n, lg[:, 0:n, :], k1[:, 0:n, :], top[:, 0, 0:n])
                    link(dve.scalar_tensor_tensor(out=lg[:, 0:n, :], in0=k1[:, 0:n, :], scalar=-3.0e38,
                                                  in1=lg[:, 0:n, :], op0=ALU.mult, op1=ALU.add))
                    pick(n, lg[:, 0:n, :], k2[:, 0:n, :], top[:, 1, 0:n])
                    dve.tensor_tensor(dl[:, i, 0:n], top[:, 0, 0:n], top[:, 1, 0:n], ALU.subtract)\
                        .then_inc(S["route_d"], 1)
                    dve.wait_ge(S["route_t"], i + 1)
                    dve.tensor_scalar(top[:, 0, 0:n], tl[:, i, 0:n], 0.5, 0.5, ALU.mult, ALU.add)
                    link(dve.tensor_scalar(top[:, 1, 0:n], tl[:, i, 0:n], -0.5, 0.5, ALU.mult, ALU.add))
                    dve.tensor_tensor(k1[:, 0:n, :], k1[:, 0:n, :], spread(top[:, 0, 0:n], n, 8), ALU.mult)
                    link(dve.tensor_tensor(k2[:, 0:n, :], k2[:, 0:n, :], spread(top[:, 1, 0:n], n, 8), ALU.mult))
                    link(dve.tensor_tensor(k1[:, 0:n, :], k1[:, 0:n, :], k2[:, 0:n, :], ALU.add))
                    if i >= 1:
                        dve.wait_ge(S["wt_mm"], i)
                    wv = k1[:, 0:n, :].rearrange("p (w h) e -> p w (h e)", h=2)
                    link(dve.tensor_copy(wsp[:, 0:GW[i], 0, :].bitcast(F32R), wv))
                    dve.tensor_tensor(wsp[:, 0:GW[i], 1, :], wv, wsp[:, 0:GW[i], 0, :], ALU.subtract)\
                        .then_inc(S["route_w"], 1)
                elif stage == "route_bias":
                    n = 64 * nb(i)
                    dve.wait_ge(S["rb_mm"], i + 1)
                    if i == 0:
                        dve.wait_ge(S["w1split"], 1)
                    if i >= 2:
                        dve.wait_ge(S["fin_mm"], i - 1)
                    dve.tensor_copy(acc[:, i % 2, 0:n], ps[:, 7, 0:n]).then_inc(S["rb_sb"], 1)
                elif stage == "expert_out":
                    g = i // E
                    n = nb(g)
                    dve.wait_ge(S["e2_mm"], i + 1)
                    dve.wait_ge(S["wide_sb"], i + 1)
                    if i >= 2:
                        dve.wait_ge(S["acc_sb"], i - 1)
                    dve.tensor_tensor(scaled[:, i % 2, 0:64 * n], ps[:, 4 + i % 2, 0:64 * n],
                                      wide[:, i % 2, 0:64 * n], ALU.mult).then_inc(S["scaled_sb"], 1)
                elif stage == "finish":
                    n = 64 * nb(i)
                    dve.wait_ge(S["fin_mm"], i + 1)
                    dve.tensor_tensor(res[:, cut(i)], ps[:, 7, 0:n], res[:, cut(i)], ALU.add).then_inc(S["out_sb"], 1)

        @block.tensor
        def _(pe):
            def exact(outp, lhs_parts, rhs_parts, start=True, stop=True):
                pe.matmul(outp, lhs_parts[0], rhs_parts[0], start=start, stop=False)
                return pe.matmul(outp, lhs_parts[1], rhs_parts[1], start=False, stop=stop)

            reader = {}

            def take(bank, read_out, count):
                if bank in reader:
                    pe.wait_ge(*reader[bank])
                reader[bank] = (S[read_out], count)

            wq, wk, wo, wv = (tokw[:, 128 * k:128 * k + 128] for k in range(4))
            for stage, i in PLAN:
                if stage == "qkv":
                    if i == 0:
                        pe.wait_ge(ld["tokw"], 16)
                    pe.wait_ge(S["conv"], 16 if i < 4 else 32)
                    if i >= 1:
                        pe.wait_ge(S["qk_sb"], i)
                    if i >= 5:
                        pe.wait_ge(S["h0_sb"], i - 4)
                    pe.matmul(ps[:, 0, 0:SI], wq, featf[:, i, :], start=True, stop=True)
                    pe.matmul(ps[:, 0, SI:2 * SI], wk, featf[:, i, :], start=True, stop=True).then_inc(S["qk_mm"], 1)
                    if i >= 1:
                        pe.wait_ge(S["v_sb"], i)
                    if i >= 4:
                        pe.wait_ge(S["mix_sb"], i - 3)
                    for c in range(2):
                        ins = pe.matmul(ps[0:SC, 1, 128 * c:128 * c + 128], featf[:, i, SC * c:SC * c + SC], wv,
                                        start=True, stop=True)
                    ins.then_inc(S["v_mm"], 1)
                elif stage == "scores":
                    pe.wait_ge(S["qk_sb"], i + 1)
                    if i >= 2:
                        pe.wait_ge(S["pt_v"], i - 1)
                        pe.wait_ge(S["pt_a"], i - 1)
                    for h in range(2):
                        for c in range(2):
                            ins = pe.matmul(ps[0:SC, 2 + 2 * (i % 2) + h, SI * c:SI * c + SI],
                                            qs[64 * h:64 * h + 64, i, SC * c:SC * c + SC],
                                            ks[64 * h:64 * h + 64, i, :], start=True, stop=True)
                    ins.then_inc(S["score_mm"], 1)
                elif stage == "probs_t":
                    pe.wait_ge(S["pnorm"], i + 1)
                    if i == 0:
                        pe.wait_ge(ld["ident"], 16)
                    for h in range(2):
                        for c in range(2):
                            for t in range(2):
                                ins = pe.transpose(ps[0:SC, 2 + 2 * (i % 2) + h, SI * t + SC * c:SI * t + SC * c + SC],
                                                   probs[0:SC, i % 2, 2 * h + c, SC * t:SC * t + SC],
                                                   ident[0:SC, 0:SC])
                    ins.then_inc(S["pt_mm"], 1)
                elif stage == "mix":
                    pe.wait_ge(S["pt_v"], i + 1)
                    pe.wait_ge(S["pt_a"], i + 1)
                    pe.wait_ge(S["v_sb"], min(i + 4, NP))
                    if i >= 1:
                        pe.wait_ge(S["mix_sb"], i)
                    for h in range(2):
                        for t in range(2):
                            k = 2 * t + h
                            ins = pe.matmul(ps[64 * h:64 * h + 64, 1, 0:SI], vs[0:SC, i % 4, 64 * k:64 * k + 64],
                                            probs_t[0:SC, i % 2, h, SI * t:SI * t + SI], start=(t == 0), stop=(t == 1))
                    ins.then_inc(S["mix_mm"], 1)
                elif stage == "tok_out":
                    pe.wait_ge(S["mix_sb"], i + 1)
                    pe.wait_ge(S["qk_sb"], min(i + 5, NP))
                    if i >= 1:
                        pe.wait_ge(S["h0_sb"], i)
                    pe.matmul(ps[:, 0, 0:SI], wo, mixed[:, i % 2, :], start=True, stop=True).then_inc(S["tok_mm"], 1)
                elif stage == "h0_t":
                    pe.wait_ge(S["h0_sb"], LAST_PAIR[i] + 1)
                    if i == 0:
                        pe.wait_ge(ld["txt"], 16)
                    take(6, "h0t", i + 1)
                    for w in range(GW[i]):
                        c = 512 * i + 128 * w
                        ins = pe.transpose(ps[:, 6, 128 * w:128 * w + 128], h0f[:, c:c + 128], ident[:, :])
                    ins.then_inc(S["ht_mm"], 1)
                elif stage in ("xn_t", "xn2_t"):
                    second = stage == "xn2_t"
                    pe.wait_ge(hl_ok[2 if second else 0], i + 1)
                    for s, ws in enumerate(xt_steps(i)):
                        n = (NXT if second else 0) + XT_DONE[i] - len(xt_steps(i)) + s
                        take(7, "xhl_sb", n + 1)
                        for w in ws:
                            for h in range(2):
                                k = 2 * w + h
                                q = 2 * (w - ws[0]) + h
                                ins = pe.transpose(ps[:, 7, 128 * q:128 * q + 128],
                                                   hl[:, i % 2, k, :, :].rearrange("p a d -> p (a d)"), ident[:, :])
                        ins.then_inc(S["xt_mm"], 1)
                elif stage == "mix_gate":
                    if i == 0:
                        pe.wait_ge(S["split"], 2)
                    pe.wait_ge(S["xhl_sb"], XT_DONE[i])
                    take(6, "mg_z", i + 1)
                    for k in range(nb(i)):
                        c = 512 * i + 128 * (k // 2)
                        ins = pe.matmul(ps[:, 6, 32 * k:32 * k + 32], xhl[:, k % 2, c:c + 128],
                                        gate_hl[:, :, 0:16], start=True, stop=True)
                    ins.then_inc(S["mg_mm"], 1)
                elif stage == "hidden":
                    pe.wait_ge(S["xhl_sb"], XT_DONE[LAST_GROUP[i]])
                    if i == 0:
                        pe.wait_ge(S["split"], 1)
                        pe.wait_ge(S["h0_sb"], NP)
                        pe.wait_ge(S["mix_sb"], NP)
                    else:
                        pe.wait_ge(S["hid_sb"], i)
                    wk1 = (split(spl_h, "kq1"), split(spl_l, "kq1"))
                    for h in range(2):
                        x = xhl[:, h, L * i:L * i + L]
                        ins = exact(ps[:, h, 0:L], wk1, (x, x))
                    ins.then_inc(S["hid_mm"], 1)
                elif stage == "values":
                    if i == 0:
                        pe.wait_ge(S["pt_v"], NP)
                        pe.wait_ge(S["pt_a"], NP)
                    else:
                        pe.wait_ge(S["vp_used"], i)
                        pe.wait_ge(S["vc_sb"], i)
                    for h in range(2):
                        x = xhl[:, h, L * i:L * i + L]
                        wv = tuple(split(p, "vp")[:, 128 * h:128 * h + 128] for p in (spl_h, spl_l))
                        ins = exact(ps[:, 4, 0:L], wv, (x, x), start=(h == 0), stop=(h == 1))
                    ins.then_inc(S["vp_mm"], 1)
                    for k, (m, size) in enumerate(MCH):
                        for h in range(2):
                            x = xhl[:, h, L * i + m:L * i + m + size]
                            o = 128 * k + 64 * h
                            ins = exact(ps[0:size, 5, o:o + 64], (x, x), (split(spl_h, "vc"), split(spl_l, "vc")))
                    ins.then_inc(S["vc_mm"], 1)
                elif stage == "phases":
                    pe.wait_ge(S["hid_sb"], i + 1)
                    if i == 0:
                        pe.wait_ge(ld["attw"], 16)
                    else:
                        pe.wait_ge(S["ph_sb"], i)
                    for r in range(2):
                        for h in range(2):
                            ins = pe.matmul(ps[64 * h:64 * h + 64, 2 + r, 0:L], attw[64 * r:64 * r + 64, 0:64],
                                            hid[64 * r:64 * r + 64, i % 2, h, :], start=True, stop=True)
                    ins.then_inc(S["ph_mm"], 1)
                elif stage == "memory":
                    pe.wait_ge(S["trig_sb"], i + 1)
                    if i == 0:
                        pe.wait_ge(S["hid_sb"], NP)
                        pe.wait_ge(S["ph_sb"], NP)
                    if i >= 2:
                        pe.wait_ge(S["mem_sb"], i - 1)
                    for h in range(2):
                        for k, (m, size) in enumerate(MCH):
                            c = L * i + m
                            ins = pe.matmul(ps[0:size, 2 * (i % 2) + h, MOFF[k]:MOFF[k] + L - m],
                                            trig[64 * h:64 * h + 64, 0, c:c + size],
                                            trig[64 * h:64 * h + 64, 1, c:L * i + L], start=True, stop=True)
                    ins.then_inc(S["mem_mm"], 1)
                elif stage == "recall":
                    pe.wait_ge(S["mem_sb"], i + 1)
                    if i == 0:
                        pe.wait_ge(S["vc_sb"], NP)
                        pe.wait_ge(S["vp_used"], NP)
                    if i >= 2:
                        pe.wait_ge(S["rec_sb"], i - 1)
                    for h in range(2):
                        for k, (m, size) in enumerate(MCH):
                            o = 128 * k + 64 * h
                            ins = pe.matmul(ps[64 * h:64 * h + 64, 4 + i % 2, m:L], vc[0:size, i, o:o + 64],
                                            mem[0:size, i % 2, h, MOFF[k]:MOFF[k] + L - m],
                                            start=(k == 0), stop=(k == len(MCH) - 1))
                    ins.then_inc(S["rec_mm"], 1)
                elif stage == "combine":
                    pe.wait_ge(S["rec_sb"], LAST_PAIR[i] + 1)
                    pe.wait_ge(S["pos_sb"], LAST_PAIR[i] + 1)
                    take(6, "comb_sb", i + 1)
                    take(7, "comb_sb", i + 1)
                    for bank, src in ((6, h0f), (7, cons)):
                        for w in range(GW[i]):
                            c = 512 * i + 128 * w
                            ins = pe.transpose(ps[:, bank, 128 * w:128 * w + 128], src[:, c:c + 128], ident[:, :])
                    ins.then_inc(S["comb_mm"], 1)
                elif stage == "norm_s":
                    pe.wait_ge(hl_ok[1], i + 1)
                    take(6, "ns_sb", i + 1)
                    for w in range(GW[i]):
                        ins = pe.transpose(ps[:, 6, 128 * w:128 * w + 128], comb[:, i % 2, 128 * w:128 * w + 128],
                                           ident[:, :])
                    ins.then_inc(S["ns_mm"], 1)
                elif stage == "attn_out":
                    pe.wait_ge(S["ns_sb"], i + 1)
                    take(7, "h1_sb", i + 1)
                    for w in range(GW[i]):
                        ins = pe.matmul(ps[:, 7, 128 * w:128 * w + 128], ns[:, i % 2, 128 * w:128 * w + 128],
                                        attw[:, 64:192], start=True, stop=True)
                    ins.then_inc(S["ao_mm"], 1)
                elif stage == "route":
                    pe.wait_ge(S["xhl_sb"], NXT + XT_DONE[i])
                    take(6, "lg_sb", i + 1)
                    for k in range(nb(i)):
                        c = 512 * i + 128 * (k // 2)
                        ins = pe.matmul(ps[:, 6, 16 * k:16 * k + 16], xhl[:, k % 2, c:c + 128],
                                        gate_hl[:, :, 16:24], start=True, stop=True)
                    ins.then_inc(S["lg_mm"], 1)
                elif stage == "route_bias":
                    pe.wait_ge(S["route_w"], i + 1)
                    take(6, "wt_sb", i + 1)
                    take(7, "rb_sb", i + 1)
                    for w in range(GW[i]):
                        ins = pe.transpose(ps[0:32, 6, 128 * w:128 * w + 128],
                                           wsp[:, w, :, :].rearrange("p a k -> p (a k)"), ident[:, :])
                    ins.then_inc(S["wt_mm"], 1)
                    pe.wait_ge(S["wt_sb"], i + 1)
                    if i == 0:
                        pe.wait_ge(S["small"], 1)
                    x = wt[:, i % 2, 0:128 * GW[i]]
                    exact(ps[:, 7, 0:128 * GW[i]], (b2_h[:, :], b2_l[:, :]), (x, x)).then_inc(S["rb_mm"], 1)
                elif stage == "finish":
                    pe.wait_ge(S["acc_sb"], E * (i + 1))
                    take(7, "out_sb", i + 1)
                    for w in range(GW[i]):
                        ins = pe.transpose(ps[:, 7, 128 * w:128 * w + 128], acc[:, i % 2, 128 * w:128 * w + 128],
                                           ident[:, :])
                    ins.then_inc(S["fin_mm"], 1)
                elif stage == "expert":
                    g = i // E
                    n = 128 * GW[g]
                    if i == 0:
                        pe.wait_ge(S["w1split"], 1)
                        pe.wait_ge(S["mem_sb"], NP)
                    pe.wait_ge(S["xhl_sb"], NXT + XT_DONE[g])
                    for j in range(2):
                        k = 2 * i + j
                        if k >= 2:
                            pe.wait_ge(S["gelu"], k - 1)
                        c = 128 * (2 * (i % E) + j)
                        wts = (w1_h[:, c:c + 128], w1_l[:, c:c + 128])
                        for h in range(2):
                            x = xhl[:, h, 512 * g:512 * g + n]
                            ins = exact(ps[:, 2 * j + h, 0:n], wts, (x, x))
                        ins.then_inc(S["e1_mm"], 1)
                    pe.wait_ge(S["wt_sb"], g + 1)
                    if i >= 2:
                        pe.wait_ge(S["scaled_sb"], i - 1)
                    elif i == 0:
                        pe.wait_ge(S["rec_sb"], NP)
                    pe.matmul(ps[:, 4 + i % 2, 0:n], sel[:, i % E, :], wt[:, g % 2, 0:n], start=True, stop=True)\
                        .then_inc(S["wide_mm"], 1)
                elif stage == "expert_out":
                    g = i // E
                    n = 128 * GW[g]
                    pe.wait_ge(S["gelu"], 2 * i + 2)
                    pe.wait_ge(S["wide_sb"], i + 1)
                    if i == 0:
                        pe.wait_ge(ld["w2"], 16)
                    for j in range(2):
                        for h in range(2):
                            ins = pe.matmul(ps[64 * h:64 * h + 64, 4 + i % 2, 0:n], w2[:, 2 * (i % E) + j, :],
                                            hidden_e[:, (2 * i + j) % 4, n * h:n * h + n],
                                            start=(j == 0), stop=(j == 1))
                    ins.then_inc(S["e2_mm"], 1)


def _stack(a):
    return np.concatenate([a, a], axis=0)


def _diagonal(a):
    out = np.zeros((128, 128), np.float32)
    out[0:64, 0:64] = a
    out[64:128, 64:128] = a
    return out


def kernel(**inputs):
    import concourse.bacc as _bacc
    from concourse.bass_utils import run_bass_kernel_spmd as _run

    a = {k: np.ascontiguousarray(v) for k, v in inputs.items()}
    tok = {k[7:]: v for k, v in a.items() if k.startswith("L0_tok_")}
    att = {k[8:]: v for k, v in a.items() if k.startswith("L0_attn_")}
    ffn = {k[7:]: v for k, v in a.items() if k.startswith("L0_ffn_")}

    px = a["x"].reshape(2, 2, 4, IMG // 2, 2, IMG // 2, 2).transpose(0, 1, 4, 6, 2, 3, 5)
    px = px.reshape(2, 2, 4, 4, PATCH, D).transpose(0, 5, 1, 2, 3, 4).reshape(128, 2, 4, 4 * PATCH)
    txt = a["txt"].reshape(2, NP, TXT, D).transpose(0, 3, 1, 2).reshape(128, NP, TXT)

    half = np.arange(128) % 64 < 32
    col = {
        "conv_w": np.broadcast_to(tok["conv_w"].reshape(1, 16), (128, 16)),
        "conv_b": np.broadcast_to(tok["conv_b"].reshape(1, 4), (128, 4)),
        "bq": _stack(tok["bq"]), "bk": _stack(tok["bk"]), "bv": _stack(tok["bv"]), "bo": _stack(tok["bo"]),
        "kq1": np.concatenate([att["bk1"], att["bq1"]]),
        "k2": np.concatenate([att["bk2"]] * 4), "q2": np.concatenate([att["bq2"]] * 4),
        "vp": _stack(att["bvp"]), "ln_g": _stack(att["ln_g"]), "ln_b": _stack(att["ln_b"]),
        "b1": ffn["b1"].reshape(16, 128).T,
        "sign": np.where(half, -1, 1), "sin_scale": np.where(half, -np.pi, np.pi),
        "sin_bias": np.where(half, np.pi / 2, 0), "half_pi": np.full(128, np.pi / 2),
    }
    row = {"bvc": att["bvc"], "bo": att["bo"], "bg1": att["bg1"], "wg2": att["Wg2"].T.reshape(-1),
           "bg2": att["bg2"], "bg": ffn["bg"], "rank": np.arange(8, 0, -1)}
    zero = np.zeros((64, 64), np.float32)
    spl = {"kq1": np.concatenate([att["Wk1"], att["Wq1"]], 1), "vc": att["Wvc"],
           "vp": np.concatenate([att["Wvp"], zero, zero, att["Wvp"]], 1), "g1": att["Wg1"], "gate": ffn["Wg"]}
    pos = np.arange(1, L + 1, dtype=np.float64)
    mask = np.zeros((128, MEND), np.float32)
    for o, (m, size) in zip(MOFF, MCH):
        q = np.arange(m, L)
        k = np.arange(m, m + size)
        mask[0:size, o:o + L - m] = (q[None] >= k[:, None]) / np.sqrt(32 * pos[q])[None]
    b2 = np.zeros((2, 2, E, 2, D), np.float32)
    sel = np.zeros((2, 2, E, E, 2, D), np.float32)
    for h in range(2):
        b2[:, h, :, h, :] = ffn["b2"]
        for e in range(E):
            sel[:, h, e, e, h, :] = 1
    phases = _stack(att["base_phases"][0:L].T)
    arrays = {
        "x_a": px[:, 0], "x_b": px[:, 1],
        "cols": np.concatenate([np.asarray(col[k], np.float32).reshape(128, n) for k, (_, n) in COL.items()], 1),
        "tokw": np.concatenate([_diagonal(tok[k].T) for k in ("wq", "wk", "wo", "wv")], 1),
        "phase": np.stack([phases, np.broadcast_to((1 / np.sqrt(pos)).astype(np.float32), (128, L))], 1),
        "rows": np.broadcast_to(np.concatenate([np.asarray(row[k], np.float32).reshape(-1) for k in ROW]),
                                (128, NROW)),
        "attw": np.concatenate([np.concatenate([np.concatenate([att[k]] * 2, 1) for k in ("Wk2", "Wq2")], 0),
                                _diagonal(att["Wo"])], 1),
        "spl": np.concatenate([_stack(spl[k]) for k in SPL], 1),
        "txt": txt,
        "const": np.concatenate([np.eye(128, dtype=np.float32), mask], 1),
        "w1": _stack(ffn["W1"].transpose(1, 0, 2).reshape(64, E * HID)),
        "w2": ffn["W2"].reshape(16, 128, 64).transpose(1, 0, 2),
        "b2": b2.reshape(32, 128), "sel": sel.reshape(32, E, 128),
    }
    arrays = {f"in_{k}": np.ascontiguousarray(v, dtype=np.float32) for k, v in arrays.items()}

    nc = _bacc.Bacc("TRN2", target_bir_lowering=False, num_devices=1)
    args = [nc.dram_tensor(k, v.shape, F32, kind="ExternalInput").ap() for k, v in arrays.items()]
    out = nc.dram_tensor("out_0", (B * L, D), F32, kind="ExternalOutput").ap()
    fusion_block(nc, *args, out)
    r = _run(nc, [arrays], core_ids=[0])
    return r.results[0]["out_0"].reshape(B, L, D)
```

```python
from contextlib import ExitStack

import numpy as np
import concourse.bass as bass
from concourse import mybir

F32 = mybir.dt.float32
F32R = mybir.dt.float32r
ACT = mybir.ActivationFunctionType
ALU = mybir.AluOpType
AX = mybir.AxisListType

B, IMG, D, TXT = 16, 96, 64, 128
CH = 4
PATCH = (IMG // 2) ** 2 // D
SI = CH * PATCH
SC = SI // 2
L = SI + TXT
NP = B // 2
COLS = NP * L
NWIN = COLS // 128
GW = [min(4, NWIN - g) for g in range(0, NWIN, 4)]
NG = len(GW)
E, HID = 8, 256
MCH = [(m, min(128, L - m)) for m in range(0, L, 128)]
MOFF = [0, L, 2 * L - 128]
MEND = MOFF[2] + L - 256
EPS = 1e-5
WARM_UP = 10
LAST_PAIR = [min(512 * g + 128 * GW[g] - 1, COLS - 1) // L for g in range(NG)]
LAST_GROUP = [(L * b + L - 1) // 512 for b in range(NP)]

TWO_PI_1 = 6.28125
TWO_PI_2 = float(np.float32(np.round((2 * np.pi - TWO_PI_1) * 2 ** 22) / 2 ** 22))
TWO_PI_3 = float(np.float32(2 * np.pi - TWO_PI_1 - TWO_PI_2))
ROUND = 1.5 * 2.0 ** 23
PI32 = 3.1415925

COL = {}
for _name, _n in [("conv_w", 16), ("conv_b", 4), ("bq", 1), ("bk", 1), ("bv", 1), ("bo", 1),
                  ("kq1", 1), ("k2", 1), ("q2", 1), ("vp", 1), ("ln_g", 1), ("ln_b", 1), ("b1", 16),
                  ("sign", 1), ("sin_scale", 1), ("sin_bias", 1), ("half_pi", 1)]:
    COL[_name] = (sum(n for _, n in COL.values()), _n)
NCOL = sum(n for _, n in COL.values())
ROW = {}
for _name, _n in [("bvc", 64), ("bo", 64), ("bg1", 16), ("wg2", 32), ("bg2", 2), ("bg", 8), ("rank", 8)]:
    ROW[_name] = (sum(n for _, n in ROW.values()), _n)
NROW = sum(n for _, n in ROW.values())
SPL = {}
for _name, _n in [("kq1", 128), ("vc", 64), ("vp", 256), ("g1", 16), ("gate", 8)]:
    SPL[_name] = (sum(n for _, n in SPL.values()), _n)
NSPL = sum(n for _, n in SPL.values())


def make_plan():
    slots = {}

    def put(slot, order, stage, i):
        slots.setdefault(slot, []).append((order, stage, i))

    for b in range(NP):
        put(b, 0, "qkv", b)
        put(b + 1, 1, "scores", b)
        put(b + 1, 4.4, "exps", b)
        put(b + 2, 1.5, "probs_n", b)
        put(b + 2, 4.5, "probs_t", b)
        put(b + 3, 3, "mix", b)
        put(b + 4, 4, "tok_out", b)
    for g in range(NG):
        s = LAST_PAIR[g] + 5
        put(s, 5, "h0_t", g)
        put(s + 1, 0.2, "ln1_stats", g)
        put(s + 1, 7.2, "ln1_norm", g)
        put(s + 2, 6, "xn_t", g)
        put(s + 3, 7, "mix_gate", g)
        put(s + 4, 0.2, "gate_z", g)
        put(s + 4, 7.6, "gate_t", g)
        put(s + 5, 7.6, "gate_p", g)
    s3 = NP + 1
    for b in range(NP):
        put(s3 + b, 8, "hidden", b)
        put(s3 + b + 1, 7.5, "phases", b)
        put(s3 + b + 2, 0.4, "phase_abs", b)
        put(s3 + b + 3, 8.5, "values", b)
        put(s3 + b + 4, 0.5, "streams", b)
    s4 = s3 + NP + 1
    for b in range(NP):
        put(s4 if b < 2 else s4 + b - 2, 1 if b < 2 else 20, "trig", b)
        put(s4 + b, 8, "memory", b)
        put(s4 + b + 2, 1 if b == 0 else 7.5, "recall", b)
    s5 = s4 + NP + 3
    for g in range(NG):
        for e in range(E):
            put(s5 + E * g + e, 10, "expert", E * g + e)
            put(s5 + E * g + e + 1, 10.5, "expert_out", E * g + e)
        put(s5 + E * g + E + 1, 10.7, "finish", g)
    for g in range(NG):
        s = [s4 + 4, s4 + 8, s5 + 5, s5 + 13, s5 + 20][g]
        d = [0, 1, 1, 1, 1, 1, 1][g]
        put(s, 11, "combine", g)
        put(s, 12, "ln2_stats", g)
        put(s + 1, 11.1, "ln2_norm", g)
        put(s + 2, 11.2, "norm_s", g)
        put(s + 3, 11.3, "attn_out", g)
        put(s + 3 + d, 12.3 if d == 0 else 0.2, "ln3_stats", g)
        put(s + 4 + d, 11.4, "ln3_norm", g)
        put(s + 5 + d, 11.5, "xn2_t", g)
        put(s + 6 + d, 9.5, "route", g)
        put(s + 7 + d, 0.3, "route_t", g)
        put(s + 7 + 2 * d, 9.9, "weights_t", g)
        put(s + 8 + 2 * d, 0.3, "route_bias", g)
    return [(stage, i) for s in sorted(slots) for _, stage, i in sorted(slots[s])]


PLAN = make_plan()


def fusion_block(nc, x_a, x_b, cols_d, tokw_d, phase_d, rows_d, attw_d, spl_d, txt_d, const_d, w1_d,
                 w2_d, b2_d, sel_d, out):
    with ExitStack() as ctx:
        def sb(name, shape, dt=F32):
            return ctx.enter_context(nc.sbuf_tensor(name, shape, dt))

        def sem(name):
            return ctx.enter_context(nc.semaphore(name))

        cols = sb("cols", [128, NCOL])
        rows = sb("rows", [128, NROW])
        tokw = sb("tokw", [128, 512])
        attw = sb("attw", [128, 256])
        ident = sb("ident", [128, 128])
        mask = sb("mask", [128, MEND])
        spl_raw = sb("spl_raw", [128, NSPL])
        spl_h = sb("spl_h", [128, NSPL], F32R)
        spl_l = sb("spl_l", [128, NSPL], F32R)
        w1_h = sb("w1_h", [128, E * HID], F32R)
        w1_l = sb("w1_l", [128, E * HID], F32R)
        w2 = sb("w2", [128, 16, 64])
        b2_raw = sb("b2_raw", [32, 128])
        b2_h = sb("b2_h", [32, 128], F32R)
        b2_l = sb("b2_l", [32, 128], F32R)
        sel = sb("sel", [32, E, 128], F32R)
        gate_hl = sb("gate_hl", [128, 2, 24], F32R)
        minus_half = sb("minus_half", [128, 8])
        phase = sb("phase", [128, 2, L])
        turns = sb("turns", [128, L])
        cos_p = sb("cos_p", [128, L])
        sin_p = sb("sin_p", [128, L])
        cos_n = sb("cos_n", [128, L])
        sin_n = sb("sin_n", [128, L])
        arena = sb("arena", [128, 4, 1024])
        flat = arena[:, :, :].rearrange("p a b -> p (a b)")
        hidden_e = arena
        pix = flat[:, 0:1152].rearrange("p (v t b s) -> p v t (b s)", v=2, t=4, b=4)
        feat = flat[:, 1152:2304].rearrange("p (b c s) -> p b c s", b=NP, c=CH)
        featf = flat[:, 1152:2304].rearrange("p (b s) -> p b s", b=NP)
        w1_raw = sb("w1_raw", [128, E * HID])
        early = sb("early", [128, 3 * NP * SI])
        qs = early[:, 0:NP * SI].rearrange("p (b s) -> p b s", b=NP)
        ks = early[:, NP * SI:].rearrange("p (h b s) -> p h b s", h=2, b=NP)
        y = early[:, 0:4 * L].rearrange("p (n k t) -> p n k t", n=2, k=2)
        cum = early[:, 4 * L:8 * L].rearrange("p (n k t) -> p n k t", n=2, k=2)
        keyz = early[:, 8 * L:12 * L].rearrange("p (n h t) -> p n h t", n=2, h=2)
        vs = sb("vs", [128, 4, 256])
        early_p = sb("early_p", [128, 16 * SI])
        probs = early_p[:, 0:8 * SI].rearrange("p (n k s) -> p n k s", n=2, k=4)
        probs_t = early_p[:, 8 * SI:].rearrange("p (n h s) -> p n h s", n=2, h=2)
        mem = early_p[:, 0:4 * MEND].rearrange("p (n h s) -> p n h s", n=2, h=2)
        negmax = sb("negmax", [128, 2, 4])
        rsum = sb("rsum", [128, 2, 4])
        rinv = sb("rinv", [128, 2, 4])
        mixed = sb("mixed", [128, 2, SI])
        h0s = sb("h0s", [128, NP, L])
        h0f = h0s[:, :, :].rearrange("p b l -> p (b l)")
        res = sb("res", [128, NWIN * 128])
        xn = sb("xn", [128, 2, 512])
        hl = sb("hl", [128, 2, 8, 2, 64])
        xhl = sb("xhl", [128, 2, COLS], F32R)
        stat = sb("stat", [128, 2, 8, 6])
        mean = sb("mean", [128, 2, 8])
        msum = sb("msum", [128, 8])
        mdif = sb("mdif", [128, 8])
        msq = sb("msq", [128, 8])
        mvar = sb("mvar", [128, 8])
        vare = sb("vare", [128, 2, 8])
        rstd = sb("rstd", [128, 2, 8])
        hid = sb("hid", [128, 2, 2, L])
        trig = sb("trig", [128, 2, COLS])
        vc = sb("vc", [128, NP, 384])
        ones = sb("ones", [128, L])
        cons = sb("cons", [128, COLS])
        gu = sb("gu", [128, 8, 16])
        gd = sb("gd", [128, 16])
        gb = sb("gb", [128, 1])
        zg = sb("zg", [128, NG, 8])
        tg = sb("tg", [128, NG, 8])
        p0 = sb("p0", [128, NG, 8])
        p1 = sb("p1", [128, NG, 8])
        c1 = sb("c1", [128, 512])
        c2 = sb("c2", [128, 512])
        comb = sb("comb", [128, 2, 512])
        ns = sb("ns", [128, 2, 512])
        lg = sb("lg", [128, 8, 8])
        eq = sb("eq", [128, 8, 8])
        k1 = sb("k1", [128, 8, 8])
        k2 = sb("k2", [128, 8, 8])
        top = sb("top", [128, 4, 8])
        dl = sb("dl", [128, NG, 8])
        tl = sb("tl", [128, NG, 8])
        wsp = sb("wsp", [128, 4, 2, 16])
        wt = sb("wt", [32, 2, 512], F32R)
        scaled = vs[:, :, :].rearrange("p (n a) c -> p n (a c)", n=2)
        acc = w1_raw[:, 0:1024].rearrange("p (n c) -> p n c", n=2)
        wide = w1_raw[:, 1024:2048].rearrange("p (n c) -> p n c", n=2)
        sel_raw = comb[0:32, :, :].rearrange("p n c -> p (n c)").rearrange("p (e c) -> p e c", e=E)

        ps = ctx.enter_context(nc.psum_tensor("ps", [128, 8, 512], F32))

        ld = {n: sem("ld_" + n) for n in ("pixa", "pixb", "cols", "tokw", "phase", "rows", "attw", "spl",
                                          "txt", "ident", "mask", "w1", "w2", "b2", "sel")}
        S = {n: sem(n) for n in (
            "conv", "qk_mm", "v_mm", "qk_sb", "v_sb", "score_mm", "rowmax", "exps", "rowinv", "pnorm",
            "pt_mm", "pt_v", "pt_a", "mix_mm", "mix_sb", "tok_mm", "h0_sb",
            "ht_mm", "h0t", "xt_mm", "xhl_sb", "mg_mm", "mg_z", "mg_t", "mg_p", "res_bo", "res_1",
            "split", "w1split", "hid_mm", "hid_sb", "vp_mm", "vp_used", "vc_mm", "vc_sb", "ph_mm", "ph_sb",
            "ph_abs", "trig_sb", "cum_sb", "pos_sb", "reduced", "base_abs", "base_trig", "base_n", "consts",
            "mem_mm", "mem_sb", "rec_mm", "rec_sb", "comb_mm", "comb_sb", "ns_mm", "ns_sb",
            "ao_mm", "h1_sb", "lg_mm", "route_d", "route_t", "route_w", "wt_mm", "wt_sb", "rb_mm", "rb_sb",
            "e1_mm", "gelu", "e2_mm", "scaled_sb", "acc_sb", "stored", "small", "zeros", "key_zeros", "tap0", "wide_mm", "wide_sb",
            "fin_mm", "out_sb", "vchain", "pchain", "lg_sb")}
        var_ok = [sem(f"var{k}") for k in range(3)]
        rstd_ok = [sem(f"rstd{k}") for k in range(3)]
        hl_ok = [sem(f"hl{k}") for k in range(3)]

        def col(name, i=0, lo=0, hi=128):
            c = COL[name][0] + i
            return cols[lo:hi, c:c + 1]

        def row(name):
            a, n = ROW[name]
            return rows[:, a:a + n]

        def split(part, name):
            a, n = SPL[name]
            return part[:, a:a + n]

        def blocks(ap, width=64):
            return ap.rearrange("p (k d) -> p k d", d=width)

        def spread(ap, n, width=64):
            return ap.unsqueeze(2).to_broadcast([128, n, width])

        def over(ap, n):
            return ap.unsqueeze(1).to_broadcast([128, n, ap.shape[-1]])

        def nb(g):
            return 2 * GW[g]

        def cut(g):
            return slice(512 * g, 512 * g + 128 * GW[g])

        def xt_steps(g):
            return [range(w, min(w + 2, GW[g])) for w in range(0, GW[g], 2)]

        XT_DONE = [sum(len(xt_steps(k)) for k in range(g + 1)) for g in range(NG)]
        NXT = XT_DONE[-1]
        BLK_BEFORE = [sum(nb(k) for k in range(g)) for g in range(NG)]

        block = ctx.enter_context(nc.Block())

        @block.sync
        def _(sp):
            sp.dma_start(pix[:, 0, :, :], x_a).then_inc(ld["pixa"], 16)
            sp.dma_start(tokw[:, :], tokw_d).then_inc(ld["tokw"], 16)
            sp.dma_start(pix[:, 1, :, :], x_b).then_inc(ld["pixb"], 16)
            sp.dma_start(h0s[:, :, SI:L], txt_d).then_inc(ld["txt"], 16)
            sp.dma_start(spl_raw[:, :], spl_d).then_inc(ld["spl"], 16)
            sp.dma_start(attw[:, :], attw_d).then_inc(ld["attw"], 16)
            sp.dma_start(mask[:, :], const_d[:, 128:]).then_inc(ld["mask"], 16)
            sp.dma_start(w1_raw[:, :], w1_d).then_inc(ld["w1"], 16)
            sp.dma_start(w2[:, :, :], w2_d).then_inc(ld["w2"], 16)
            sp.dma_start(b2_raw[:, :], b2_d).then_inc(ld["b2"], 16)
            sp.dma_start(sel_raw, sel_d).then_inc(ld["sel"], 16)
            for g in range(NG):
                sp.wait_ge(S["out_sb"], g + 1)
                for h in range(2):
                    dst = out[COLS * h + 512 * g:COLS * h + 512 * g + 128 * GW[g], :]
                    src = res[:, cut(g)].rearrange("p (w h d) -> p w h d", h=2, d=64)[:, :, h, :]
                    sp.dma_start(dst.rearrange("(w p) d -> p w d", p=128), src).then_inc(S["stored"], 16)
            sp.wait_ge(S["stored"], 16 * 2 * NG)

        @block.gpsimd
        def _(pool):
            steps = [0]

            def link(ins):
                steps[0] += 1
                ins.then_inc(S["pchain"], 1)
                pool.wait_ge(S["pchain"], steps[0])

            pool.memset(ones[:, :], 1.0).then_inc(S["consts"], 1)
            link(pool.memset(minus_half[:, :], -0.5))
            link(pool.memset(ks[64:128, 0, :, :], 0.0))
            pool.memset(ks[0:64, 1, :, :], 0.0).then_inc(S["zeros"], 1)
            pool.wait_ge(S["zeros"], 1)
            pool.wait_ge(S["base_trig"], 1)
            pool.tensor_tensor(cos_n[:, :], cos_p[:, :], phase[:, 1, :], ALU.mult)
            pool.tensor_tensor(sin_n[:, :], sin_p[:, :], phase[:, 1, :], ALU.mult).then_inc(S["base_n"], 1)
            pool.wait_ge(S["base_n"], 1)
            pool.wait_ge(ld["w1"], 16)
            link(pool.tensor_scalar(w1_h[:, :], w1_raw[:, :], 1.0, None, ALU.mult))
            pool.tensor_tensor(w1_l[:, :], w1_raw[:, :], w1_h[:, :].bitcast(F32), ALU.subtract)\
                .then_inc(S["w1split"], 1)

            def root(kind, g):
                pool.wait_ge(var_ok[kind], g + 1)
                pool.tensor_tensor(rstd[:, g % 2, 0:nb(g)], vare[:, g % 2, 0:nb(g)],
                                   minus_half[:, 0:nb(g)], ALU.pow).then_inc(rstd_ok[kind], 1)

            for stage, i in PLAN:
                if stage == "ln1_stats":
                    root(0, i)
                elif stage == "ln1_norm":
                    pool.wait_ge(hl_ok[0], i + 1)
                    pool.wait_ge(ld["rows"], 16)
                    pool.tensor_tensor(blocks(res[:, cut(i)]), blocks(res[:, cut(i)]),
                                       over(row("bo"), nb(i)), ALU.add).then_inc(S["res_bo"], 1)
                    pool.wait_ge(S["res_bo"], i + 1)
                    pool.tensor_tensor(res[:, cut(i)], res[:, cut(i)], xn[:, i % 2, 0:128 * GW[i]],
                                       ALU.add).then_inc(S["res_1"], 1)
                elif stage == "streams":
                    if i == 0:
                        pool.wait_ge(S["score_mm"], NP)
                        pool.memset(keyz[:, :, :, :], 0.0).then_inc(S["key_zeros"], 1)
                    pool.wait_ge(S["cum_sb"], i + 1)
                    link(pool.tensor_tensor(cum[:, i % 2, 0, :], cum[:, i % 2, 0, :], cos_n[:, :], ALU.mult))
                    link(pool.tensor_tensor(cum[:, i % 2, 1, :], cum[:, i % 2, 1, :], sin_n[:, :], ALU.mult))
                    pool.tensor_tensor(h0s[:, i, :], cum[:, i % 2, 0, :], cum[:, i % 2, 1, :],
                                       ALU.add).then_inc(S["pos_sb"], 1)
                elif stage == "ln2_stats":
                    root(1, i)
                elif stage == "ln3_stats":
                    root(2, i)
                elif stage == "expert_out":
                    g = i // E
                    pool.wait_ge(S["scaled_sb"], i + 1)
                    pool.wait_ge(S["rb_sb"], g + 1)
                    if i > 0:
                        pool.wait_ge(S["acc_sb"], i)
                    pool.tensor_tensor(acc[:, g % 2, 0:128 * GW[g]], acc[:, g % 2, 0:128 * GW[g]],
                                       scaled[:, i % 2, 0:128 * GW[g]], ALU.add).then_inc(S["acc_sb"], 1)

        @block.scalar
        def _(act):
            act.dma_start(phase[:, :, :], phase_d).then_inc(ld["phase"], 16)
            act.dma_start(cols[:, :], cols_d).then_inc(ld["cols"], 16)
            act.dma_start(ident[:, :], const_d[:, 0:128]).then_inc(ld["ident"], 16)
            act.dma_start(rows[:, :], rows_d).then_inc(ld["rows"], 16)
            act.wait_ge(ld["cols"], 16)
            for v in range(2):
                act.wait_ge(ld["pixa" if v == 0 else "pixb"], 16)
                for c in range(CH):
                    act.activation(feat[:, 4 * v:4 * v + 4, c, :], pix[:, v, 0, :].rearrange("p (b s) -> p b s", b=4),
                                   ACT.Identity, scale=col("conv_w", 4 * c), bias=col("conv_b", c))\
                        .then_inc(S["tap0"], 1)
                if v == 0:
                    act.wait_ge(S["reduced"], 1)
                    act.activation(sin_p[:, :], phase[:, 0, :], ACT.Sin)
                    act.activation(turns[:, :], phase[:, 0, :], ACT.Abs).then_inc(S["base_abs"], 1)
                    act.wait_ge(S["base_abs"], 1)
                    act.activation(cos_p[:, :], turns[:, :], ACT.Sin, scale=-1.0, bias=col("half_pi"))\
                        .then_inc(S["base_trig"], 1)

            for stage, i in PLAN:
                if stage == "qkv":
                    act.wait_ge(S["v_mm"], i + 1)
                    if i >= 4:
                        act.wait_ge(S["mix_mm"], i - 3)
                    act.activation(vs[0:SC, i % 4, :], ps[0:SC, 1, 0:256], ACT.Copy).then_inc(S["v_sb"], 1)
                elif stage == "exps":
                    act.wait_ge(S["rowmax"], i + 1)
                    for k in range(4):
                        ins = act.activation(probs[0:SC, i % 2, k, :],
                                             ps[0:SC, 2 + 2 * (i % 2) + k // 2, SI * (k % 2):SI * (k % 2) + SI],
                                             ACT.Exp, bias=negmax[0:SC, i % 2, k:k + 1],
                                             accum_out=rsum[0:SC, i % 2, k:k + 1])
                    ins.then_inc(S["exps"], 1)
                elif stage == "probs_t":
                    act.wait_ge(S["pt_mm"], i + 1)
                    act.activation(probs_t[0:SC, i % 2, 1, :], ps[0:SC, 3 + 2 * (i % 2), 0:2 * SI], ACT.Copy)\
                        .then_inc(S["pt_a"], 1)
                elif stage == "mix":
                    act.wait_ge(S["mix_mm"], i + 1)
                    act.activation(mixed[:, i % 2, :], ps[:, 1, 0:SI], ACT.Identity, bias=col("bv"))\
                        .then_inc(S["mix_sb"], 1)
                elif stage == "tok_out":
                    act.wait_ge(S["tok_mm"], i + 1)
                    act.activation(h0s[:, i, 0:SI], ps[:, 0, 0:SI], ACT.Identity, bias=col("bo"))\
                        .then_inc(S["h0_sb"], 1)
                elif stage == "h0_t":
                    act.wait_ge(S["ht_mm"], i + 1)
                    act.activation(res[:, cut(i)], ps[:, 6, 0:128 * GW[i]], ACT.Copy).then_inc(S["h0t"], 1)
                elif stage in ("xn_t", "xn2_t"):
                    base = 0 if stage == "xn_t" else NXT
                    for s, ws in enumerate(xt_steps(i)):
                        n = base + XT_DONE[i] - len(xt_steps(i)) + s
                        act.wait_ge(S["xt_mm"], n + 1)
                        c = 512 * i + 128 * ws[0]
                        act.activation(xhl[:, :, c:c + 128 * len(ws)].rearrange("p h (w t) -> p w h t", t=128),
                                       ps[:, 7 - s, 0:256 * len(ws)].rearrange("p (w h t) -> p w h t", h=2, t=128),
                                       ACT.Copy).then_inc(S["xhl_sb"], 1)
                elif stage == "gate_t":
                    act.wait_ge(S["mg_z"], i + 1)
                    act.activation(tg[:, i, 0:nb(i)], zg[:, i, 0:nb(i)], ACT.Tanh, scale=0.5)\
                        .then_inc(S["mg_t"], 1)
                elif stage == "hidden":
                    act.wait_ge(S["hid_mm"], i + 1)
                    if i >= 2:
                        act.wait_ge(S["ph_mm"], i - 1)
                    act.activation(hid[:, i % 2, :, :], ps[:, 2:4, 0:L], ACT.Tanh, bias=col("kq1"))\
                        .then_inc(S["hid_sb"], 1)
                elif stage == "phases":
                    act.wait_ge(S["ph_mm"], i + 1)
                    act.activation(trig[:, 0, L * i:L * i + L], ps[:, 4, 0:L], ACT.Tanh, bias=col("k2"))
                    act.activation(trig[:, 1, L * i:L * i + L], ps[:, 5, 0:L], ACT.Tanh, bias=col("q2"))\
                        .then_inc(S["ph_sb"], 1)
                elif stage == "trig":
                    act.wait_ge(S["ph_abs"], i + 1)
                    if i == 0:
                        act.wait_ge(S["key_zeros"], 1)
                    else:
                        if i >= 2:
                            act.wait_ge(S["mem_mm"], i - 1)
                    act.activation(trig[:, 1, L * i:L * i + L], trig[:, 1, L * i:L * i + L], ACT.Sin,
                                   scale=col("sin_scale"), bias=col("sin_bias"))
                    for h in range(2):
                        r = slice(64 * h, 64 * h + 64)
                        ins = act.activation(keyz[r, i % 2, h, :], trig[r, 0, L * i:L * i + L], ACT.Sin,
                                             scale=col("sin_scale", 0, 64 * h, 64 * h + 64),
                                             bias=col("sin_bias", 0, 64 * h, 64 * h + 64))
                    ins.then_inc(S["trig_sb"], 1)
                elif stage == "recall":
                    act.wait_ge(S["rec_mm"], i + 1)
                    act.activation(cons[:, L * i:L * i + L], ps[:, i % 2, 0:L], ACT.Copy)\
                        .then_inc(S["rec_sb"], 1)
                elif stage == "norm_s":
                    act.wait_ge(S["ns_mm"], i + 1)
                    if i >= 2:
                        act.wait_ge(S["ao_mm"], i - 1)
                    act.activation(ns[:, i % 2, 0:128 * GW[i]], ps[:, 6, 0:128 * GW[i]], ACT.Identity,
                                   scale=col("ln_g"), bias=col("ln_b")).then_inc(S["ns_sb"], 1)
                elif stage == "route_t":
                    act.wait_ge(S["route_d"], i + 1)
                    act.activation(tl[:, i, 0:nb(i)], dl[:, i, 0:nb(i)], ACT.Tanh, scale=0.5)\
                        .then_inc(S["route_t"], 1)
                elif stage == "weights_t":
                    act.wait_ge(S["wt_mm"], i + 1)
                    if i >= 2:
                        act.wait_ge(S["wide_mm"], E * (i - 1))
                    act.activation(wt[:, i % 2, 0:128 * GW[i]], ps[0:32, 6, 0:128 * GW[i]], ACT.Copy)\
                        .then_inc(S["wt_sb"], 1)
                elif stage == "expert":
                    g = i // E
                    n = 128 * GW[g]
                    for j in range(2):
                        k = 2 * i + j
                        act.wait_ge(S["e1_mm"], k + 1)
                        if i >= 2:
                            act.wait_ge(S["e2_mm"], i - 1)
                        act.activation(hidden_e[:, k % 4, 0:2 * n].rearrange("p (h t) -> p h t", h=2),
                                       ps[:, 2 * j:2 * j + 2, 0:n], ACT.Gelu, bias=col("b1", 2 * (i % E) + j))\
                            .then_inc(S["gelu"], 1)
                    act.wait_ge(S["wide_mm"], i + 1)
                    if i >= 2:
                        act.wait_ge(S["scaled_sb"], i - 1)
                    act.activation(wide[:, i % 2, 0:n], ps[:, 4 + i % 2, 0:n], ACT.Copy).then_inc(S["wide_sb"], 1)

        @block.vector
        def _(dve):
            steps = [0]

            def link(ins):
                steps[0] += 1
                ins.then_inc(S["vchain"], 1)
                dve.wait_ge(S["vchain"], steps[0])

            dve.wait_ge(ld["phase"], 16)
            raw = phase[:, 0, :]
            link(dve.tensor_scalar(turns[:, :], raw, float(1 / (2 * np.pi)), ROUND, ALU.mult, ALU.add))
            link(dve.tensor_scalar(turns[:, :], turns[:, :], ROUND, None, ALU.subtract))
            for part in (TWO_PI_1, TWO_PI_2, TWO_PI_3):
                link(dve.scalar_tensor_tensor(out=raw, in0=turns[:, :], scalar=-part, in1=raw,
                                              op0=ALU.mult, op1=ALU.add))
            dve.tensor_scalar(raw, raw, PI32, -PI32, ALU.min, ALU.max).then_inc(S["reduced"], 1)
            dve.wait_ge(ld["cols"], 16)
            dve.wait_ge(ld["pixa"], 16)

            def conv_tap(v, tap):
                for c in range(CH):
                    if tap == 1:
                        dve.wait_ge(S["tap0"], 4 * v + c + 1)
                    else:
                        dve.wait_ge(S["conv"], 12 * v + 4 * (tap - 2) + c + 1)
                    o = feat[:, 4 * v:4 * v + 4, c, :]
                    dve.scalar_tensor_tensor(out=o, in0=pix[:, v, tap, :].rearrange("p (b s) -> p b s", b=4),
                                             scalar=col("conv_w", 4 * c + tap), in1=o, op0=ALU.mult, op1=ALU.add)\
                        .then_inc(S["conv"], 1)

            for tap in range(1, 4):
                conv_tap(0, tap)

            def mixer_weights():
                dve.wait_ge(ld["spl"], 16)
                link(dve.tensor_copy(spl_h[:, :], spl_raw[:, :]))
                dve.tensor_tensor(spl_l[:, :], spl_raw[:, :], spl_h[:, :].bitcast(F32), ALU.subtract)\
                    .then_inc(S["split"], 1)
                dve.wait_ge(ld["rows"], 16)
                dve.wait_ge(S["split"], 1)
                dve.tensor_copy(gate_hl[:, 0, :], spl_h[:, NSPL - 24:NSPL].bitcast(F32))
                dve.tensor_copy(gate_hl[:, 1, :], spl_l[:, NSPL - 24:NSPL].bitcast(F32)).then_inc(S["split"], 1)
                wg2 = row("wg2").rearrange("p (a k) -> p a k", a=2)
                dve.tensor_tensor(gd[:, :], wg2[:, 0, :], wg2[:, 1, :], ALU.subtract)
                link(dve.tensor_tensor(gb[:, :], row("bg2")[:, 0:1], row("bg2")[:, 1:2], ALU.subtract))

            def small_weights():
                dve.wait_ge(ld["b2"], 16)
                dve.wait_ge(ld["sel"], 16)
                link(dve.tensor_copy(b2_h[:, :], b2_raw[:, :]))
                dve.tensor_tensor(b2_l[:, :], b2_raw[:, :], b2_h[:, :].bitcast(F32), ALU.subtract)
                dve.tensor_copy(sel[:, :, :], sel_raw).then_inc(S["small"], 1)

            def moments(kind, g, src):
                n = nb(g)
                st = stat[:, g % 2, 0:n, :]
                for k in range(n):
                    ins = dve.bn_stats(stat[:, g % 2, k, :], src[:, 64 * k:64 * k + 64])
                link(ins)
                dve.tensor_tensor(msum[:, 0:n], st[:, :, 1], st[:, :, 4], ALU.add)
                dve.tensor_tensor(mvar[:, 0:n], st[:, :, 2], st[:, :, 5], ALU.add)
                link(dve.tensor_tensor(mdif[:, 0:n], st[:, :, 1], st[:, :, 4], ALU.subtract))
                dve.tensor_scalar(mean[:, g % 2, 0:n], msum[:, 0:n], 0.5, None, ALU.mult)
                link(dve.tensor_tensor(msq[:, 0:n], mdif[:, 0:n], mdif[:, 0:n], ALU.mult))
                link(dve.scalar_tensor_tensor(out=mvar[:, 0:n], in0=msq[:, 0:n], scalar=16.0,
                                              in1=mvar[:, 0:n], op0=ALU.mult, op1=ALU.add))
                dve.tensor_scalar(vare[:, g % 2, 0:n], mvar[:, 0:n], 1.0 / 64, EPS, ALU.mult, ALU.add)\
                    .then_inc(var_ok[kind], 1)

            def normalise(kind, g, src, dst):
                dve.wait_ge(rstd_ok[kind], g + 1)
                for k in range(nb(g)):
                    ins = dve.tensor_scalar(dst[:, 64 * k:64 * k + 64], src[:, 64 * k:64 * k + 64],
                                            mean[:, g % 2, k:k + 1], rstd[:, g % 2, k:k + 1],
                                            ALU.subtract, ALU.mult)
                return ins

            def split_tokens(kind, g):
                n = nb(g)
                x = blocks(xn[:, g % 2, 0:64 * n])
                link(dve.tensor_copy(hl[:, g % 2, 0:n, 0, :].bitcast(F32R), x))
                dve.tensor_tensor(hl[:, g % 2, 0:n, 1, :], x, hl[:, g % 2, 0:n, 0, :], ALU.subtract)\
                    .then_inc(hl_ok[kind], 1)

            def pick(n, values, one_hot, best):
                link(dve.tensor_reduce(best, values, AX.X, ALU.max))
                link(dve.tensor_tensor(eq[:, 0:n, :], values, spread(best, n, 8), ALU.is_equal))
                link(dve.tensor_tensor(eq[:, 0:n, :], eq[:, 0:n, :], over(row("rank"), n), ALU.mult))
                link(dve.tensor_reduce(top[:, 3, 0:n], eq[:, 0:n, :], AX.X, ALU.max))
                link(dve.tensor_tensor(one_hot, eq[:, 0:n, :], spread(top[:, 3, 0:n], n, 8), ALU.is_equal))

            for stage, i in PLAN:
                if stage == "qkv":
                    dve.wait_ge(S["qk_mm"], i + 1)
                    dve.tensor_scalar(qs[:, i, :], ps[:, 0, 0:SI], col("bq"), float(D) ** -0.5, ALU.add, ALU.mult)
                    for h in range(2):
                        r = slice(64 * h, 64 * h + 64)
                        ins = dve.tensor_scalar(ks[r, h, i, :], ps[r, 0, SI:2 * SI],
                                                col("bk", 0, 64 * h, 64 * h + 64), None, ALU.add)
                    ins.then_inc(S["qk_sb"], 1)
                    if i == 0:
                        mixer_weights()
                        dve.wait_ge(ld["pixb"], 16)
                    if 1 <= i <= 3:
                        conv_tap(1, i)
                elif stage == "scores":
                    dve.wait_ge(S["score_mm"], i + 1)
                    b0 = 2 + 2 * (i % 2)
                    dve.tensor_reduce(negmax[0:SC, i % 2, :].rearrange("p (h c) -> p h c", h=2),
                                      ps[0:SC, b0:b0 + 2, 0:2 * SI].rearrange("p h (c t) -> p h c t", c=2),
                                      AX.X, ALU.max, negate=True).then_inc(S["rowmax"], 1)
                elif stage == "probs_n":
                    dve.wait_ge(S["exps"], i + 1)
                    dve.reciprocal(rinv[0:SC, i % 2, :], rsum[0:SC, i % 2, :]).then_inc(S["rowinv"], 1)
                    dve.wait_ge(S["rowinv"], i + 1)
                    dve.tensor_tensor(probs[0:SC, i % 2, :, :], probs[0:SC, i % 2, :, :],
                                      rinv[0:SC, i % 2, :].unsqueeze(2).to_broadcast([SC, 4, SI]), ALU.mult)\
                        .then_inc(S["pnorm"], 1)
                elif stage == "probs_t":
                    dve.wait_ge(S["pt_mm"], i + 1)
                    dve.tensor_copy(probs_t[0:SC, i % 2, 0, :], ps[0:SC, 2 + 2 * (i % 2), 0:2 * SI])\
                        .then_inc(S["pt_v"], 1)
                elif stage == "ln1_stats":
                    dve.wait_ge(S["h0t"], i + 1)
                    moments(0, i, res[:, cut(i)])
                elif stage == "ln1_norm":
                    if i >= 2:
                        dve.wait_ge(S["res_1"], i - 1)
                        dve.wait_ge(S["xt_mm"], XT_DONE[i - 2])
                    link(normalise(0, i, res[:, cut(i)], xn[:, i % 2, :]))
                    split_tokens(0, i)
                elif stage == "gate_z":
                    n = nb(i)
                    dve.wait_ge(S["mg_mm"], i + 1)
                    link(dve.tensor_reduce(gu[:, 0:n, :],
                                           ps[:, 6, 0:32 * n].rearrange("p (k a j) -> p k j a", a=2, j=16),
                                           AX.X, ALU.add))
                    link(dve.tensor_tensor(gu[:, 0:n, :], gu[:, 0:n, :], over(row("bg1"), n), ALU.add))
                    link(dve.scalar_tensor_tensor(out=gu[:, 0:n, :], in0=gu[:, 0:n, :], scalar=0.0,
                                                  in1=over(gd[:, :], n), op0=ALU.max, op1=ALU.mult))
                    link(dve.tensor_reduce(zg[:, i, 0:n], gu[:, 0:n, :], AX.X, ALU.add))
                    dve.tensor_scalar(zg[:, i, 0:n], zg[:, i, 0:n], gb[:, 0:1], None, ALU.add)\
                        .then_inc(S["mg_z"], 1)
                elif stage == "gate_p":
                    n = nb(i)
                    dve.wait_ge(S["mg_t"], i + 1)
                    dve.tensor_scalar(p0[:, i, 0:n], tg[:, i, 0:n], 0.5, 0.5, ALU.mult, ALU.add)
                    dve.tensor_scalar(p1[:, i, 0:n], tg[:, i, 0:n], -0.5, 0.5, ALU.mult, ALU.add)\
                        .then_inc(S["mg_p"], 1)
                elif stage == "streams":
                    dve.wait_ge(S["vp_mm"], i + 1)
                    if i == 0:
                        dve.wait_ge(S["base_trig"], 1)
                        dve.wait_ge(S["consts"], 1)
                    if i >= 2:
                        dve.wait_ge(S["pos_sb"], i - 1)
                    for k, t in enumerate((cos_p, sin_p)):
                        ins = dve.scalar_tensor_tensor(out=y[:, i % 2, k, :], in0=ps[:, 0, 0:L], scalar=col("vp"),
                                                       in1=t[:, :], op0=ALU.add, op1=ALU.mult)
                    ins.then_inc(S["vp_used"], 1)
                    dve.wait_ge(S["vc_mm"], i + 1)
                    dve.tensor_tensor(blocks(vc[:, i, 0:256]), blocks(ps[:, 1, 0:256]), over(row("bvc"), 4), ALU.add)
                    tail = MCH[2][1]
                    dve.tensor_tensor(blocks(vc[0:tail, i, 256:384]), blocks(ps[0:tail, 1, 256:384]),
                                      row("bvc")[0:tail, :].unsqueeze(1).to_broadcast([tail, 2, 64]), ALU.add)\
                        .then_inc(S["vc_sb"], 1)
                    dve.wait_ge(S["vp_used"], i + 1)
                    for k in range(2):
                        ins = dve.tensor_tensor_scan(cum[:, i % 2, k, :], ones[:, :], y[:, i % 2, k, :], 0.0,
                                                     ALU.mult, ALU.add)
                    ins.then_inc(S["cum_sb"], 1)
                elif stage == "phase_abs":
                    if i == 1:
                        small_weights()
                    dve.wait_ge(S["ph_sb"], i + 1)
                    t = trig[:, :, L * i:L * i + L]
                    dve.scalar_tensor_tensor(out=t, in0=t, scalar=col("sign"), in1=t, op0=ALU.mult, op1=ALU.max)\
                        .then_inc(S["ph_abs"], 1)
                elif stage == "memory":
                    dve.wait_ge(S["mem_mm"], i + 1)
                    if i == 0:
                        dve.wait_ge(ld["mask"], 16)
                    if i >= 2:
                        dve.wait_ge(S["rec_mm"], i - 1)
                    b0, full, tail = 2 + 2 * (i % 2), MOFF[2], MCH[2][1]
                    dve.tensor_tensor(mem[:, i % 2, :, 0:full], ps[:, b0:b0 + 2, 0:full],
                                      over(mask[:, 0:full], 2), ALU.mult)
                    dve.tensor_tensor(mem[0:tail, i % 2, :, full:MEND], ps[0:tail, b0:b0 + 2, full:MEND],
                                      mask[0:tail, full:MEND].unsqueeze(1).to_broadcast([tail, 2, tail]), ALU.mult)\
                        .then_inc(S["mem_sb"], 1)
                elif stage == "combine":
                    n = nb(i)
                    if i >= 2:
                        dve.wait_ge(S["ns_mm"], i - 1)
                    dve.wait_ge(S["comb_mm"], i + 1)
                    dve.wait_ge(S["mg_p"], i + 1)
                    dve.tensor_tensor(blocks(c1[:, 0:64 * n]), blocks(ps[:, 6, 0:64 * n]),
                                      spread(p0[:, i, 0:n], n), ALU.mult)
                    link(dve.tensor_tensor(blocks(c2[:, 0:64 * n]), blocks(ps[:, 7, 0:64 * n]),
                                           spread(p1[:, i, 0:n], n), ALU.mult))
                    dve.tensor_tensor(comb[:, i % 2, 0:64 * n], c1[:, 0:64 * n], c2[:, 0:64 * n], ALU.add)\
                        .then_inc(S["comb_sb"], 1)
                elif stage == "ln2_stats":
                    dve.wait_ge(S["comb_sb"], i + 1)
                    moments(1, i, comb[:, i % 2, :])
                elif stage == "ln2_norm":
                    normalise(1, i, comb[:, i % 2, :], comb[:, i % 2, :]).then_inc(hl_ok[1], 1)
                elif stage == "attn_out":
                    n = 64 * nb(i)
                    dve.wait_ge(S["ao_mm"], i + 1)
                    dve.wait_ge(S["res_1"], i + 1)
                    dve.tensor_tensor(res[:, cut(i)], ps[:, 7, 0:n], res[:, cut(i)], ALU.add).then_inc(S["h1_sb"], 1)
                elif stage == "ln3_stats":
                    dve.wait_ge(S["h1_sb"], i + 1)
                    moments(2, i, res[:, cut(i)])
                elif stage == "ln3_norm":
                    if i == 0:
                        dve.wait_ge(S["res_1"], NG)
                        dve.wait_ge(S["xt_mm"], NXT)
                    if i >= 2:
                        dve.wait_ge(S["xt_mm"], NXT + XT_DONE[i - 2])
                    link(normalise(2, i, res[:, cut(i)], xn[:, i % 2, :]))
                    split_tokens(2, i)
                elif stage == "route":
                    n = nb(i)
                    dve.wait_ge(S["lg_mm"], i + 1)
                    dve.tensor_reduce(lg[:, 0:n, :], ps[:, 6, 0:16 * n].rearrange("p (k a j) -> p k j a", a=2, j=8),
                                      AX.X, ALU.add).then_inc(S["lg_sb"], 1)
                    dve.wait_ge(S["lg_sb"], i + 1)
                    link(dve.tensor_tensor(lg[:, 0:n, :], lg[:, 0:n, :], over(row("bg"), n), ALU.add))
                    pick(n, lg[:, 0:n, :], k1[:, 0:n, :], top[:, 0, 0:n])
                    link(dve.scalar_tensor_tensor(out=lg[:, 0:n, :], in0=k1[:, 0:n, :], scalar=-3.0e38,
                                                  in1=lg[:, 0:n, :], op0=ALU.mult, op1=ALU.add))
                    pick(n, lg[:, 0:n, :], k2[:, 0:n, :], top[:, 1, 0:n])
                    dve.tensor_tensor(dl[:, i, 0:n], top[:, 0, 0:n], top[:, 1, 0:n], ALU.subtract)\
                        .then_inc(S["route_d"], 1)
                elif stage == "route_t":
                    n = nb(i)
                    dve.wait_ge(S["route_t"], i + 1)
                    dve.tensor_scalar(top[:, 0, 0:n], tl[:, i, 0:n], 0.5, 0.5, ALU.mult, ALU.add)
                    link(dve.tensor_scalar(top[:, 1, 0:n], tl[:, i, 0:n], -0.5, 0.5, ALU.mult, ALU.add))
                    dve.tensor_tensor(k1[:, 0:n, :], k1[:, 0:n, :], spread(top[:, 0, 0:n], n, 8), ALU.mult)
                    link(dve.tensor_tensor(k2[:, 0:n, :], k2[:, 0:n, :], spread(top[:, 1, 0:n], n, 8), ALU.mult))
                    link(dve.tensor_tensor(k1[:, 0:n, :], k1[:, 0:n, :], k2[:, 0:n, :], ALU.add))
                    if i >= 1:
                        dve.wait_ge(S["wt_mm"], i)
                    wv = k1[:, 0:n, :].rearrange("p (w h) e -> p w (h e)", h=2)
                    link(dve.tensor_copy(wsp[:, 0:GW[i], 0, :].bitcast(F32R), wv))
                    dve.tensor_tensor(wsp[:, 0:GW[i], 1, :], wv, wsp[:, 0:GW[i], 0, :], ALU.subtract)\
                        .then_inc(S["route_w"], 1)
                elif stage == "route_bias":
                    n = 64 * nb(i)
                    dve.wait_ge(S["rb_mm"], i + 1)
                    if i == 0:
                        dve.wait_ge(S["w1split"], 1)
                    if i >= 2:
                        dve.wait_ge(S["fin_mm"], i - 1)
                    dve.tensor_copy(acc[:, i % 2, 0:n], ps[:, 7, 0:n]).then_inc(S["rb_sb"], 1)
                elif stage == "expert_out":
                    g = i // E
                    n = nb(g)
                    dve.wait_ge(S["e2_mm"], i + 1)
                    dve.wait_ge(S["wide_sb"], i + 1)
                    if i >= 2:
                        dve.wait_ge(S["acc_sb"], i - 1)
                    dve.tensor_tensor(scaled[:, i % 2, 0:64 * n], ps[:, 4 + i % 2, 0:64 * n],
                                      wide[:, i % 2, 0:64 * n], ALU.mult).then_inc(S["scaled_sb"], 1)
                elif stage == "finish":
                    n = 64 * nb(i)
                    dve.wait_ge(S["fin_mm"], i + 1)
                    dve.tensor_tensor(res[:, cut(i)], ps[:, 7, 0:n], res[:, cut(i)], ALU.add).then_inc(S["out_sb"], 1)

        @block.tensor
        def _(pe):
            def exact(outp, lhs_parts, rhs_parts, start=True, stop=True):
                pe.matmul(outp, lhs_parts[0], rhs_parts[0], start=start, stop=False)
                return pe.matmul(outp, lhs_parts[1], rhs_parts[1], start=False, stop=stop)

            reader = {}

            def take(bank, read_out, count):
                if bank in reader:
                    pe.wait_ge(*reader[bank])
                reader[bank] = (S[read_out], count)

            wq, wk, wo, wv = (tokw[:, 128 * k:128 * k + 128] for k in range(4))
            pe.wait_ge(S["consts"], 1)
            for _ in range(WARM_UP):
                pe.matmul(ps[:, 7, 0:L], ones[:, 0:128], ones[:, :], start=True, stop=True)

            for stage, i in PLAN:
                if stage == "qkv":
                    if i == 0:
                        pe.wait_ge(ld["tokw"], 16)
                    pe.wait_ge(S["conv"], 12 if i < 4 else 24)
                    if i >= 1:
                        pe.wait_ge(S["qk_sb"], i)
                    if i >= 5:
                        pe.wait_ge(S["h0_sb"], i - 4)
                    pe.matmul(ps[:, 0, 0:SI], wq, featf[:, i, :], start=True, stop=True)
                    pe.matmul(ps[:, 0, SI:2 * SI], wk, featf[:, i, :], start=True, stop=True).then_inc(S["qk_mm"], 1)
                    if i >= 1:
                        pe.wait_ge(S["v_sb"], i)
                    if i >= 4:
                        pe.wait_ge(S["mix_sb"], i - 3)
                    for c in range(2):
                        ins = pe.matmul(ps[0:SC, 1, 128 * c:128 * c + 128], featf[:, i, SC * c:SC * c + SC], wv,
                                        start=True, stop=True)
                    ins.then_inc(S["v_mm"], 1)
                elif stage == "scores":
                    pe.wait_ge(S["qk_sb"], i + 1)
                    if i == 0:
                        pe.wait_ge(S["zeros"], 1)
                    if i >= 2:
                        pe.wait_ge(S["pt_v"], i - 1)
                        pe.wait_ge(S["pt_a"], i - 1)
                    for h in range(2):
                        for c in range(2):
                            ins = pe.matmul(ps[0:SC, 2 + 2 * (i % 2) + h, SI * c:SI * c + SI],
                                            qs[:, i, SC * c:SC * c + SC], ks[:, h, i, :], start=True, stop=True)
                    ins.then_inc(S["score_mm"], 1)
                elif stage == "probs_t":
                    pe.wait_ge(S["pnorm"], i + 1)
                    if i == 0:
                        pe.wait_ge(ld["ident"], 16)
                    for h in range(2):
                        for c in range(2):
                            for t in range(2):
                                ins = pe.transpose(ps[0:SC, 2 + 2 * (i % 2) + h, SI * t + SC * c:SI * t + SC * c + SC],
                                                   probs[0:SC, i % 2, 2 * h + c, SC * t:SC * t + SC],
                                                   ident[0:SC, 0:SC])
                    ins.then_inc(S["pt_mm"], 1)
                elif stage == "mix":
                    pe.wait_ge(S["pt_v"], i + 1)
                    pe.wait_ge(S["pt_a"], i + 1)
                    pe.wait_ge(S["v_sb"], min(i + 4, NP))
                    if i >= 1:
                        pe.wait_ge(S["mix_sb"], i)
                    for h in range(2):
                        for t in range(2):
                            k = 2 * t + h
                            ins = pe.matmul(ps[64 * h:64 * h + 64, 1, 0:SI], vs[0:SC, i % 4, 64 * k:64 * k + 64],
                                            probs_t[0:SC, i % 2, h, SI * t:SI * t + SI], start=(t == 0), stop=(t == 1))
                    ins.then_inc(S["mix_mm"], 1)
                elif stage == "tok_out":
                    pe.wait_ge(S["mix_sb"], i + 1)
                    pe.wait_ge(S["qk_sb"], min(i + 5, NP))
                    if i >= 1:
                        pe.wait_ge(S["h0_sb"], i)
                    pe.matmul(ps[:, 0, 0:SI], wo, mixed[:, i % 2, :], start=True, stop=True).then_inc(S["tok_mm"], 1)
                elif stage == "h0_t":
                    pe.wait_ge(S["h0_sb"], LAST_PAIR[i] + 1)
                    if i == 0:
                        pe.wait_ge(ld["txt"], 16)
                    take(6, "h0t", i + 1)
                    for w in range(GW[i]):
                        c = 512 * i + 128 * w
                        ins = pe.transpose(ps[:, 6, 128 * w:128 * w + 128], h0f[:, c:c + 128], ident[:, :])
                    ins.then_inc(S["ht_mm"], 1)
                elif stage in ("xn_t", "xn2_t"):
                    second = stage == "xn2_t"
                    pe.wait_ge(hl_ok[2 if second else 0], i + 1)
                    for s, ws in enumerate(xt_steps(i)):
                        n = (NXT if second else 0) + XT_DONE[i] - len(xt_steps(i)) + s
                        take(7 - s, "xhl_sb", n + 1)
                        for w in ws:
                            for h in range(2):
                                k = 2 * w + h
                                q = 2 * (w - ws[0]) + h
                                ins = pe.transpose(ps[:, 7 - s, 128 * q:128 * q + 128],
                                                   hl[:, i % 2, k, :, :].rearrange("p a d -> p (a d)"), ident[:, :])
                        ins.then_inc(S["xt_mm"], 1)
                elif stage == "mix_gate":
                    if i == 0:
                        pe.wait_ge(S["split"], 2)
                    pe.wait_ge(S["xhl_sb"], XT_DONE[i])
                    take(6, "mg_z", i + 1)
                    for k in range(nb(i)):
                        c = 512 * i + 128 * (k // 2)
                        ins = pe.matmul(ps[:, 6, 32 * k:32 * k + 32], xhl[:, k % 2, c:c + 128],
                                        gate_hl[:, :, 0:16], start=True, stop=True)
                    ins.then_inc(S["mg_mm"], 1)
                elif stage == "hidden":
                    pe.wait_ge(S["xhl_sb"], XT_DONE[LAST_GROUP[i]])
                    if i == 0:
                        pe.wait_ge(S["split"], 1)
                        pe.wait_ge(S["pt_v"], NP - 1)
                        pe.wait_ge(S["pt_a"], NP - 1)
                    else:
                        pe.wait_ge(S["hid_sb"], i)
                    wk1 = (split(spl_h, "kq1"), split(spl_l, "kq1"))
                    for h in range(2):
                        x = xhl[:, h, L * i:L * i + L]
                        ins = exact(ps[:, 2 + h, 0:L], wk1, (x, x))
                    ins.then_inc(S["hid_mm"], 1)
                elif stage == "values":
                    if i == 0:
                        pe.wait_ge(S["h0_sb"], NP)
                        pe.wait_ge(S["mix_sb"], NP)
                    else:
                        pe.wait_ge(S["vp_used"], i)
                        pe.wait_ge(S["vc_sb"], i)
                    for h in range(2):
                        x = xhl[:, h, L * i:L * i + L]
                        wv = tuple(split(p, "vp")[:, 128 * h:128 * h + 128] for p in (spl_h, spl_l))
                        ins = exact(ps[:, 0, 0:L], wv, (x, x), start=(h == 0), stop=(h == 1))
                    ins.then_inc(S["vp_mm"], 1)
                    for k, (m, size) in enumerate(MCH):
                        for h in range(2):
                            x = xhl[:, h, L * i + m:L * i + m + size]
                            o = 128 * k + 64 * h
                            ins = exact(ps[0:size, 1, o:o + 64], (x, x), (split(spl_h, "vc"), split(spl_l, "vc")))
                    ins.then_inc(S["vc_mm"], 1)
                elif stage == "phases":
                    pe.wait_ge(S["hid_sb"], i + 1)
                    if i == 0:
                        pe.wait_ge(ld["attw"], 16)
                        pe.wait_ge(S["pt_v"], NP)
                        pe.wait_ge(S["pt_a"], NP)
                    else:
                        pe.wait_ge(S["ph_sb"], i)
                    for r in range(2):
                        for h in range(2):
                            ins = pe.matmul(ps[64 * h:64 * h + 64, 4 + r, 0:L], attw[:, 64 * r:64 * r + 64],
                                            hid[:, i % 2, h, :], start=True, stop=True)
                    ins.then_inc(S["ph_mm"], 1)
                elif stage == "memory":
                    pe.wait_ge(S["trig_sb"], i + 1)
                    if i == 0:
                        pe.wait_ge(S["hid_sb"], NP)
                    if i == 1:
                        pe.wait_ge(S["ph_sb"], NP)
                    if i >= 2:
                        pe.wait_ge(S["mem_sb"], i - 1)
                    for h in range(2):
                        for k, (m, size) in enumerate(MCH):
                            ins = pe.matmul(ps[0:size, 2 + 2 * (i % 2) + h, MOFF[k]:MOFF[k] + L - m],
                                            keyz[:, i % 2, h, m:m + size], trig[:, 1, L * i + m:L * i + L],
                                            start=True, stop=True)
                    ins.then_inc(S["mem_mm"], 1)
                elif stage == "recall":
                    pe.wait_ge(S["mem_sb"], i + 1)
                    if i == 0:
                        pe.wait_ge(S["vc_sb"], NP)
                        pe.wait_ge(S["vp_used"], NP)
                    if i >= 2:
                        pe.wait_ge(S["rec_sb"], i - 1)
                    for h in range(2):
                        for k, (m, size) in enumerate(MCH):
                            o = 128 * k + 64 * h
                            ins = pe.matmul(ps[64 * h:64 * h + 64, i % 2, m:L], vc[0:size, i, o:o + 64],
                                            mem[0:size, i % 2, h, MOFF[k]:MOFF[k] + L - m],
                                            start=(k == 0), stop=(k == len(MCH) - 1))
                    ins.then_inc(S["rec_mm"], 1)
                elif stage == "combine":
                    pe.wait_ge(S["rec_sb"], LAST_PAIR[i] + 1)
                    pe.wait_ge(S["pos_sb"], LAST_PAIR[i] + 1)
                    take(6, "comb_sb", i + 1)
                    take(7, "comb_sb", i + 1)
                    for bank, src in ((6, h0f), (7, cons)):
                        for w in range(GW[i]):
                            c = 512 * i + 128 * w
                            ins = pe.transpose(ps[:, bank, 128 * w:128 * w + 128], src[:, c:c + 128], ident[:, :])
                    ins.then_inc(S["comb_mm"], 1)
                elif stage == "norm_s":
                    pe.wait_ge(hl_ok[1], i + 1)
                    take(6, "ns_sb", i + 1)
                    for w in range(GW[i]):
                        ins = pe.transpose(ps[:, 6, 128 * w:128 * w + 128], comb[:, i % 2, 128 * w:128 * w + 128],
                                           ident[:, :])
                    ins.then_inc(S["ns_mm"], 1)
                elif stage == "attn_out":
                    pe.wait_ge(S["ns_sb"], i + 1)
                    take(7, "h1_sb", i + 1)
                    for w in range(GW[i]):
                        ins = pe.matmul(ps[:, 7, 128 * w:128 * w + 128], ns[:, i % 2, 128 * w:128 * w + 128],
                                        attw[:, 128:256], start=True, stop=True)
                    ins.then_inc(S["ao_mm"], 1)
                elif stage == "route":
                    pe.wait_ge(S["xhl_sb"], NXT + XT_DONE[i])
                    take(6, "lg_sb", i + 1)
                    for k in range(nb(i)):
                        c = 512 * i + 128 * (k // 2)
                        ins = pe.matmul(ps[:, 6, 16 * k:16 * k + 16], xhl[:, k % 2, c:c + 128],
                                        gate_hl[:, :, 16:24], start=True, stop=True)
                    ins.then_inc(S["lg_mm"], 1)
                elif stage == "weights_t":
                    pe.wait_ge(S["route_w"], i + 1)
                    take(6, "wt_sb", i + 1)
                    for w in range(GW[i]):
                        ins = pe.transpose(ps[0:32, 6, 128 * w:128 * w + 128],
                                           wsp[:, w, :, :].rearrange("p a k -> p (a k)"), ident[:, :])
                    ins.then_inc(S["wt_mm"], 1)
                elif stage == "route_bias":
                    take(7, "rb_sb", i + 1)
                    pe.wait_ge(S["wt_sb"], i + 1)
                    if i == 0:
                        pe.wait_ge(S["small"], 1)
                    x = wt[:, i % 2, 0:128 * GW[i]]
                    exact(ps[:, 7, 0:128 * GW[i]], (b2_h[:, :], b2_l[:, :]), (x, x)).then_inc(S["rb_mm"], 1)
                elif stage == "finish":
                    pe.wait_ge(S["acc_sb"], E * (i + 1))
                    take(7, "out_sb", i + 1)
                    for w in range(GW[i]):
                        ins = pe.transpose(ps[:, 7, 128 * w:128 * w + 128], acc[:, i % 2, 128 * w:128 * w + 128],
                                           ident[:, :])
                    ins.then_inc(S["fin_mm"], 1)
                elif stage == "expert":
                    g = i // E
                    n = 128 * GW[g]
                    if i == 0:
                        pe.wait_ge(S["w1split"], 1)
                        pe.wait_ge(S["rec_sb"], NP)
                        pe.wait_ge(S["mem_sb"], NP)
                    pe.wait_ge(S["xhl_sb"], NXT + XT_DONE[g])
                    for j in range(2):
                        k = 2 * i + j
                        if k >= 2:
                            pe.wait_ge(S["gelu"], k - 1)
                        c = 128 * (2 * (i % E) + j)
                        wts = (w1_h[:, c:c + 128], w1_l[:, c:c + 128])
                        for h in range(2):
                            x = xhl[:, h, 512 * g:512 * g + n]
                            ins = exact(ps[:, 2 * j + h, 0:n], wts, (x, x))
                        ins.then_inc(S["e1_mm"], 1)
                    pe.wait_ge(S["wt_sb"], g + 1)
                    if i >= 2:
                        pe.wait_ge(S["scaled_sb"], i - 1)
                    pe.matmul(ps[:, 4 + i % 2, 0:n], sel[:, i % E, :], wt[:, g % 2, 0:n], start=True, stop=True)\
                        .then_inc(S["wide_mm"], 1)
                elif stage == "expert_out":
                    g = i // E
                    n = 128 * GW[g]
                    pe.wait_ge(S["gelu"], 2 * i + 2)
                    pe.wait_ge(S["wide_sb"], i + 1)
                    if i == 0:
                        pe.wait_ge(ld["w2"], 16)
                    for j in range(2):
                        for h in range(2):
                            ins = pe.matmul(ps[64 * h:64 * h + 64, 4 + i % 2, 0:n], w2[:, 2 * (i % E) + j, :],
                                            hidden_e[:, (2 * i + j) % 4, n * h:n * h + n],
                                            start=(j == 0), stop=(j == 1))
                    ins.then_inc(S["e2_mm"], 1)


def _stack(a):
    return np.concatenate([a, a], axis=0)


def _diagonal(a):
    out = np.zeros((128, 128), np.float32)
    out[0:64, 0:64] = a
    out[64:128, 64:128] = a
    return out


def kernel(**inputs):
    import concourse.bacc as _bacc
    from concourse.bass_utils import run_bass_kernel_spmd as _run

    a = {k: np.ascontiguousarray(v) for k, v in inputs.items()}
    tok = {k[7:]: v for k, v in a.items() if k.startswith("L0_tok_")}
    att = {k[8:]: v for k, v in a.items() if k.startswith("L0_attn_")}
    ffn = {k[7:]: v for k, v in a.items() if k.startswith("L0_ffn_")}

    px = a["x"].reshape(2, 2, 4, IMG // 2, 2, IMG // 2, 2).transpose(0, 1, 4, 6, 2, 3, 5)
    px = px.reshape(2, 2, 4, 4, PATCH, D).transpose(0, 5, 1, 2, 3, 4).reshape(128, 2, 4, 4 * PATCH)
    txt = a["txt"].reshape(2, NP, TXT, D).transpose(0, 3, 1, 2).reshape(128, NP, TXT)

    half = np.arange(128) % 64 < 32
    col = {
        "conv_w": np.broadcast_to(tok["conv_w"].reshape(1, 16), (128, 16)),
        "conv_b": np.broadcast_to(tok["conv_b"].reshape(1, 4), (128, 4)),
        "bq": _stack(tok["bq"]), "bk": _stack(tok["bk"]), "bv": _stack(tok["bv"]), "bo": _stack(tok["bo"]),
        "kq1": np.concatenate([att["bk1"], att["bq1"]]),
        "k2": np.concatenate([att["bk2"]] * 4), "q2": np.concatenate([att["bq2"]] * 4),
        "vp": _stack(att["bvp"]), "ln_g": _stack(att["ln_g"]), "ln_b": _stack(att["ln_b"]),
        "b1": ffn["b1"].reshape(16, 128).T,
        "sign": np.where(half, -1, 1), "sin_scale": np.where(half, -np.pi, np.pi),
        "sin_bias": np.where(half, np.pi / 2, 0), "half_pi": np.full(128, np.pi / 2),
    }
    row = {"bvc": att["bvc"], "bo": att["bo"], "bg1": att["bg1"], "wg2": att["Wg2"].T.reshape(-1),
           "bg2": att["bg2"], "bg": ffn["bg"], "rank": np.arange(8, 0, -1)}
    zero = np.zeros((64, 64), np.float32)
    spl = {"kq1": np.concatenate([att["Wk1"], att["Wq1"]], 1), "vc": att["Wvc"],
           "vp": np.concatenate([att["Wvp"], zero, zero, att["Wvp"]], 1), "g1": att["Wg1"], "gate": ffn["Wg"]}
    pos = np.arange(1, L + 1, dtype=np.float64)
    mask = np.zeros((128, MEND), np.float32)
    for o, (m, size) in zip(MOFF, MCH):
        q = np.arange(m, L)
        k = np.arange(m, m + size)
        mask[0:size, o:o + L - m] = (q[None] >= k[:, None]) / np.sqrt(32 * pos[q])[None]
    b2 = np.zeros((2, 2, E, 2, D), np.float32)
    sel = np.zeros((2, 2, E, E, 2, D), np.float32)
    for h in range(2):
        b2[:, h, :, h, :] = ffn["b2"]
        for e in range(E):
            sel[:, h, e, e, h, :] = 1
    phases = _stack(att["base_phases"][0:L].T)
    arrays = {
        "x_a": px[:, 0], "x_b": px[:, 1],
        "cols": np.concatenate([np.asarray(col[k], np.float32).reshape(128, n) for k, (_, n) in COL.items()], 1),
        "tokw": np.concatenate([_diagonal(tok[k].T) for k in ("wq", "wk", "wo", "wv")], 1),
        "phase": np.stack([phases, np.broadcast_to((1 / np.sqrt(pos)).astype(np.float32), (128, L))], 1),
        "rows": np.broadcast_to(np.concatenate([np.asarray(row[k], np.float32).reshape(-1) for k in ROW]),
                                (128, NROW)),
        "attw": np.concatenate([np.concatenate([att["Wk2"], att["Wk2"], zero], 1),
                                np.concatenate([zero, att["Wq2"], att["Wq2"]], 1),
                                _diagonal(att["Wo"])[0:64], _diagonal(att["Wo"])[64:128]], 0)
        .reshape(2, 2, 64, 128).transpose(1, 2, 0, 3).reshape(128, 256),
        "spl": np.concatenate([_stack(spl[k]) for k in SPL], 1),
        "txt": txt,
        "const": np.concatenate([np.eye(128, dtype=np.float32), mask], 1),
        "w1": _stack(ffn["W1"].transpose(1, 0, 2).reshape(64, E * HID)),
        "w2": ffn["W2"].reshape(16, 128, 64).transpose(1, 0, 2),
        "b2": b2.reshape(32, 128), "sel": sel.reshape(32, E, 128),
    }
    arrays = {f"in_{k}": np.ascontiguousarray(v, dtype=np.float32) for k, v in arrays.items()}

    nc = _bacc.Bacc("TRN2", target_bir_lowering=False, num_devices=1)
    args = [nc.dram_tensor(k, v.shape, F32, kind="ExternalInput").ap() for k, v in arrays.items()]
    out = nc.dram_tensor("out_0", (B * L, D), F32, kind="ExternalOutput").ap()
    fusion_block(nc, *args, out)
    r = _run(nc, [arrays], core_ids=[0])
    return r.results[0]["out_0"].reshape(B, L, D)
```

```python
from contextlib import ExitStack

import numpy as np
import concourse.bass as bass
from concourse import mybir

F32 = mybir.dt.float32
F32R = mybir.dt.float32r
ACT = mybir.ActivationFunctionType
ALU = mybir.AluOpType
AX = mybir.AxisListType

B, IMG, D, TXT = 16, 96, 64, 128
CH = 4
PATCH = (IMG // 2) ** 2 // D
SI = CH * PATCH
SC = SI // 2
L = SI + TXT
NP = B // 2
COLS = NP * L
NWIN = COLS // 128
GW = [3, 4, 4, 4, 2]
NG = len(GW)
GC = [128 * sum(GW[:g]) for g in range(NG)]
assert sum(GW) == NWIN
E, HID = 8, 256
MCH = [(m, min(128, L - m)) for m in range(0, L, 128)]
MOFF = [0, L, 2 * L - 128]
MEND = MOFF[2] + L - 256
EPS = 1e-5
WARM_UP = 10
LAST_PAIR = [(GC[g] + 128 * GW[g] - 1) // L for g in range(NG)]
LAST_GROUP = [sum(c < L * (b + 1) for c in GC) - 1 for b in range(NP)]

TWO_PI_1 = 6.28125
TWO_PI_2 = float(np.float32(np.round((2 * np.pi - TWO_PI_1) * 2 ** 22) / 2 ** 22))
TWO_PI_3 = float(np.float32(2 * np.pi - TWO_PI_1 - TWO_PI_2))
ROUND = 1.5 * 2.0 ** 23
PI32 = 3.1415925

COL = {}
for _name, _n in [("conv_w", 16), ("conv_b", 4), ("bq", 1), ("bk", 1), ("bv", 1), ("bo", 1),
                  ("kq1", 1), ("k2", 1), ("q2", 1), ("vp", 1), ("ln_g", 1), ("ln_b", 1), ("b1", 16),
                  ("sign", 1), ("sin_scale", 1), ("sin_bias", 1), ("half_pi", 1)]:
    COL[_name] = (sum(n for _, n in COL.values()), _n)
NCOL = sum(n for _, n in COL.values())
ROW = {}
for _name, _n in [("bvc", 64), ("bo", 64), ("bg1", 16), ("wg2", 32), ("bg2", 2), ("bg", 8), ("rank", 8)]:
    ROW[_name] = (sum(n for _, n in ROW.values()), _n)
NROW = sum(n for _, n in ROW.values())
SPL = {}
for _name, _n in [("kq1", 128), ("vc", 64), ("vp", 256), ("g1", 16), ("gate", 8)]:
    SPL[_name] = (sum(n for _, n in SPL.values()), _n)
NSPL = sum(n for _, n in SPL.values())


PAIR_AT = {
    "qkv": (0, 0), "scores": (1, 1), "exps": (1, 4.7), "probs_n": (2, 0.5), "probs_t": (2, 4.5),
    "mix": (3, 3), "tok_out": (4, 4), "hidden": (9, 8), "phases": (10, 7.5), "phase_abs": (11, 0.4),
    "content": (11, 8.5), "content_b": (12, 0.5), "values": (15, 8.6), "streams": (16, 0.6),
    "memory": (18, 8), "recall": (20, 7.5),
}
LN1_AT = {
    "h0_t": (5, 2.5), "ln1_stats": (6, 0.2), "ln1_norm": (6, 8.7), "xn_t": (7, 2.7),
    "residual": (7, 6.5), "mix_gate": (8, 6.784), "gate_z": (9, 0.2), "gate_t": (9, 7.6),
    "gate_p": (10, 12.2),
}
FIRST_AT = {
    "combine": (-7, 7.682), "ln2_stats": (-7, 8.2), "ln2_norm": (-6, 9), "norm_s": (-4, 0.7),
    "attn_out": (-4, 8.41), "ln3_stats": (-4, 8.6), "ln3_norm": (-2, 0.7), "xn2_t": (-1, 0.7),
    "route": (-1, 4.204), "route_t": (0, 10.2), "weights_t": (1, 8.5), "route_bias": (1, 10.2),
}
LATER_AT = {
    "combine": (-10, 10.6), "ln2_stats": (-10, 12), "ln2_norm": (-8, 0.05), "norm_s": (-7, 5.5),
    "attn_out": (-7, 10.2), "ln3_stats": (-7, 12), "ln3_norm": (-6, 11.4), "xn2_t": (-4, 10.2),
    "route": (-4, 10.998), "route_t": (-2, 0.3), "weights_t": (-1, 10.1), "route_bias": (0, 10.3),
}
EXPERT_AT = {
    "expert": (0, 10), "wide": (1, 9), "expert_out": (1, 10.5),
}
TRIG_AT = [
    (18, 1), (18, 1.1), (19, 19.372), (19, 20), (20, 20), (21, 20), (22, 20.53), (23, 20),
]
EXPERTS = 28
LN1_SHIFT = [0, 0, 0, 0, 0]
SHIFT = [0, 1, 1, 1, 1]
WARM = [
    (10, 9.5, 2), (12, 9.5, 2), (13, 9.5, 2), (14, 9.5, 2), (15, 9.5, 2), (17, 9.5, 2), (27, 0.5, 4),
    (28, 10.05, 6),
]


def make_plan():
    plan = [(slot, order, "keep_warm", n) for slot, order, n in WARM]
    for b in range(NP):
        plan += [(slot + b, order, stage, b) for stage, (slot, order) in PAIR_AT.items()]
    plan += [(slot, order, "trig", b) for b, (slot, order) in enumerate(TRIG_AT)]
    for g in range(NG):
        plan += [(slot + LAST_PAIR[g] + LN1_SHIFT[g], order, stage, g) for stage, (slot, order) in LN1_AT.items()]
        start = EXPERTS + E * g
        steps = FIRST_AT if g == 0 else LATER_AT
        plan += [(slot + start + SHIFT[g], order, stage, g) for stage, (slot, order) in steps.items()]
        for e in range(E):
            plan += [(slot + start + e, order, stage, E * g + e) for stage, (slot, order) in EXPERT_AT.items()]
        plan.append((start + E + 1, 10.7, "finish", g))
    return [(stage, i) for _, _, stage, i in sorted(plan)]


PLAN = make_plan()


def fusion_block(nc, x_a, x_b, cols_d, tokw_d, phase_d, rows_d, attw_d, spl_d, txt_d, const_d, w1_d,
                 w2_d, b2_d, sel_d, out):
    with ExitStack() as ctx:
        def sb(name, shape, dt=F32):
            return ctx.enter_context(nc.sbuf_tensor(name, shape, dt))

        def sem(name):
            return ctx.enter_context(nc.semaphore(name))

        cols = sb("cols", [128, NCOL])
        rows = sb("rows", [128, NROW])
        tokw = sb("tokw", [128, 512])
        attw = sb("attw", [128, 256])
        ident = sb("ident", [128, 128])
        mask = sb("mask", [128, MEND])
        spl_raw = sb("spl_raw", [128, NSPL])
        spl_h = sb("spl_h", [128, NSPL], F32R)
        spl_l = sb("spl_l", [128, NSPL], F32R)
        w1_h = sb("w1_h", [128, E * HID], F32R)
        w1_l = sb("w1_l", [128, E * HID], F32R)
        w2 = sb("w2", [128, 16, 64])
        b2_raw = sb("b2_raw", [32, 128])
        b2_h = sb("b2_h", [32, 128], F32R)
        b2_l = sb("b2_l", [32, 128], F32R)
        sel = sb("sel", [32, E, 128], F32R)
        gate_hl = sb("gate_hl", [128, 2, 24], F32R)
        minus_half = sb("minus_half", [128, 8])
        phase = sb("phase", [128, 2, L])
        turns = sb("turns", [128, L])
        cos_p = sb("cos_p", [128, L])
        sin_p = sb("sin_p", [128, L])
        cos_n = sb("cos_n", [128, L])
        sin_n = sb("sin_n", [128, L])
        arena = sb("arena", [128, 4, 1024])
        flat = arena[:, :, :].rearrange("p a b -> p (a b)")
        hidden_e = arena
        pix = flat[:, 0:1152].rearrange("p (v t b s) -> p v t (b s)", v=2, t=4, b=4)
        feat = flat[:, 1152:2304].rearrange("p (b c s) -> p b c s", b=NP, c=CH)
        featf = flat[:, 1152:2304].rearrange("p (b s) -> p b s", b=NP)
        w1_raw = sb("w1_raw", [128, E * HID])
        early = sb("early", [128, 3 * NP * SI])
        qs = early[:, 0:NP * SI].rearrange("p (b s) -> p b s", b=NP)
        ks = early[:, NP * SI:].rearrange("p (h b s) -> p h b s", h=2, b=NP)
        y = early[:, 0:4 * L].rearrange("p (n k t) -> p n k t", n=2, k=2)
        cum = early[:, 4 * L:8 * L].rearrange("p (n k t) -> p n k t", n=2, k=2)
        keyz = early[:, 8 * L:12 * L].rearrange("p (n h t) -> p n h t", n=2, h=2)
        vs = sb("vs", [128, 4, 256])
        early_p = sb("early_p", [128, 16 * SI])
        probs = early_p[:, 0:8 * SI].rearrange("p (n k s) -> p n k s", n=2, k=4)
        probs_t = early_p[:, 8 * SI:].rearrange("p (n h s) -> p n h s", n=2, h=2)
        mem = early_p[:, 0:4 * MEND].rearrange("p (n h s) -> p n h s", n=2, h=2)
        negmax = sb("negmax", [128, 2, 4])
        rsum = sb("rsum", [128, 2, 4])
        rinv = sb("rinv", [128, 2, 4])
        mixed = sb("mixed", [128, 2, SI])
        h0s = sb("h0s", [128, NP, L])
        h0f = h0s[:, :, :].rearrange("p b l -> p (b l)")
        res = sb("res", [128, NWIN * 128])
        xn = sb("xn", [128, 2, 512])
        hl = sb("hl", [128, 2, 8, 2, 64])
        xhl = sb("xhl", [128, 2, COLS], F32R)
        stat = sb("stat", [128, 2, 8, 6])
        mean = sb("mean", [128, 2, 8])
        msum = sb("msum", [128, 8])
        mdif = sb("mdif", [128, 8])
        msq = sb("msq", [128, 8])
        mvar = sb("mvar", [128, 8])
        vare = sb("vare", [128, 2, 8])
        rstd = sb("rstd", [128, 2, 8])
        hid = sb("hid", [128, 2, 2, L])
        trig = sb("trig", [128, 2, COLS])
        vc = sb("vc", [128, NP, 384])
        ones = sb("ones", [128, L])
        cons = sb("cons", [128, COLS])
        gu = sb("gu", [128, 8, 16])
        gd = sb("gd", [128, 16])
        gb = sb("gb", [128, 1])
        zg = sb("zg", [128, NG, 8])
        tg = sb("tg", [128, NG, 8])
        p0 = sb("p0", [128, NG, 8])
        p1 = sb("p1", [128, NG, 8])
        c1 = sb("c1", [128, 512])
        c2 = sb("c2", [128, 512])
        comb = sb("comb", [128, 2, 512])
        ns = sb("ns", [128, 2, 512])
        lg = sb("lg", [128, 8, 8])
        eq = sb("eq", [128, 8, 8])
        k1 = sb("k1", [128, 8, 8])
        k2 = sb("k2", [128, 8, 8])
        top = sb("top", [128, 4, 8])
        dl = sb("dl", [128, NG, 8])
        tl = sb("tl", [128, NG, 8])
        wsp = sb("wsp", [128, 4, 2, 16])
        wt = sb("wt", [32, 2, 512], F32R)
        scaled = vs[:, :, :].rearrange("p (n a) c -> p n (a c)", n=2)
        acc = w1_raw[:, 0:1024].rearrange("p (n c) -> p n c", n=2)
        wide = w1_raw[:, 1024:2048].rearrange("p (n c) -> p n c", n=2)
        sel_raw = comb[0:32, :, :].rearrange("p n c -> p (n c)").rearrange("p (e c) -> p e c", e=E)

        ps = ctx.enter_context(nc.psum_tensor("ps", [128, 8, 512], F32))

        ld = {n: sem("ld_" + n) for n in ("pixa", "pixb", "cols", "tokw", "phase", "rows", "attw", "spl",
                                          "txt", "ident", "mask", "w1", "w2", "b2", "sel")}
        S = {n: sem(n) for n in (
            "conv", "qk_mm", "v_mm", "qk_sb", "v_sb", "score_mm", "rowmax", "exps", "rowinv", "pnorm",
            "pt_mm", "pt_v", "pt_a", "mix_mm", "mix_sb", "tok_mm", "h0_sb", "high0",
            "ht_mm", "h0t", "xt_mm", "xhl_sb", "mg_mm", "mg_z", "mg_t", "mg_p", "res_bo", "res_1",
            "split", "w1split", "hid_mm", "hid_sb", "vp_mm", "vp_used", "vc_mm", "vc_sb", "vc_b", "ph_mm", "ph_sb",
            "ph_abs", "trig_sb", "cum_sb", "pos_sb", "reduced", "base_abs", "base_trig", "base_n", "consts",
            "mem_mm", "mem_sb", "rec_mm", "rec_sb", "comb_mm", "comb_sb", "ns_mm", "ns_sb",
            "ao_mm", "h1_sb", "lg_mm", "route_d", "route_t", "route_w", "wt_mm", "wt_sb", "rb_mm", "rb_sb",
            "e1_mm", "gelu", "e2_mm", "scaled_sb", "acc_sb", "stored", "small", "zeros", "key_zeros",
            "tap0", "wide_mm", "wide_sb",
            "fin_mm", "out_sb", "vchain", "pchain", "lg_sb")}
        var_ok = [sem(f"var{k}") for k in range(3)]
        rstd_ok = [sem(f"rstd{k}") for k in range(3)]
        hl_ok = [sem(f"hl{k}") for k in range(3)]

        def col(name, i=0, lo=0, hi=128):
            c = COL[name][0] + i
            return cols[lo:hi, c:c + 1]

        def row(name):
            a, n = ROW[name]
            return rows[:, a:a + n]

        def split(part, name):
            a, n = SPL[name]
            return part[:, a:a + n]

        def blocks(ap, width=64):
            return ap.rearrange("p (k d) -> p k d", d=width)

        def spread(ap, n, width=64):
            return ap.unsqueeze(2).to_broadcast([128, n, width])

        def over(ap, n):
            return ap.unsqueeze(1).to_broadcast([128, n, ap.shape[-1]])

        def nb(g):
            return 2 * GW[g]

        def cut(g):
            return slice(GC[g], GC[g] + 128 * GW[g])

        def xt_steps(g):
            return [range(w, min(w + 2, GW[g])) for w in range(0, GW[g], 2)]

        XT_DONE = [sum(len(xt_steps(k)) for k in range(g + 1)) for g in range(NG)]
        NXT = XT_DONE[-1]
        BLK_BEFORE = [sum(nb(k) for k in range(g)) for g in range(NG)]

        block = ctx.enter_context(nc.Block())

        @block.sync
        def _(sp):
            sp.dma_start(pix[:, 0, :, :], x_a).then_inc(ld["pixa"], 16)
            sp.dma_start(tokw[:, :], tokw_d).then_inc(ld["tokw"], 16)
            sp.dma_start(pix[:, 1, :, :], x_b).then_inc(ld["pixb"], 16)
            sp.dma_start(h0s[:, :, SI:L], txt_d).then_inc(ld["txt"], 16)
            sp.dma_start(spl_raw[:, :], spl_d).then_inc(ld["spl"], 16)
            sp.dma_start(attw[:, :], attw_d).then_inc(ld["attw"], 16)
            sp.dma_start(mask[:, :], const_d[:, 128:]).then_inc(ld["mask"], 16)
            sp.dma_start(w1_raw[:, :], w1_d).then_inc(ld["w1"], 16)
            sp.dma_start(w2[:, :, :], w2_d).then_inc(ld["w2"], 16)
            sp.dma_start(b2_raw[:, :], b2_d).then_inc(ld["b2"], 16)
            sp.dma_start(sel_raw, sel_d).then_inc(ld["sel"], 16)
            for g in range(NG):
                sp.wait_ge(S["out_sb"], g + 1)
                for h in range(2):
                    dst = out[COLS * h + GC[g]:COLS * h + GC[g] + 128 * GW[g], :]
                    src = res[:, cut(g)].rearrange("p (w h d) -> p w h d", h=2, d=64)[:, :, h, :]
                    sp.dma_start(dst.rearrange("(w p) d -> p w d", p=128), src).then_inc(S["stored"], 16)
            sp.wait_ge(S["stored"], 16 * 2 * NG)

        @block.gpsimd
        def _(pool):
            steps = [0]

            def link(ins):
                steps[0] += 1
                ins.then_inc(S["pchain"], 1)
                pool.wait_ge(S["pchain"], steps[0])

            pool.memset(ones[:, :], 1.0).then_inc(S["consts"], 1)
            link(pool.memset(minus_half[:, :], -0.5))
            link(pool.memset(ks[64:128, 0, :, :], 0.0))
            pool.memset(ks[0:64, 1, :, :], 0.0).then_inc(S["zeros"], 1)
            pool.wait_ge(S["zeros"], 1)
            pool.wait_ge(S["base_trig"], 1)
            pool.tensor_tensor(cos_n[:, :], cos_p[:, :], phase[:, 1, :], ALU.mult)
            pool.tensor_tensor(sin_n[:, :], sin_p[:, :], phase[:, 1, :], ALU.mult).then_inc(S["base_n"], 1)
            pool.wait_ge(S["base_n"], 1)
            pool.wait_ge(ld["w1"], 16)
            link(pool.tensor_scalar(w1_h[:, :], w1_raw[:, :], 1.0, None, ALU.mult))
            pool.tensor_tensor(w1_l[:, :], w1_raw[:, :], w1_h[:, :].bitcast(F32), ALU.subtract)\
                .then_inc(S["w1split"], 1)

            def root(kind, g):
                pool.wait_ge(var_ok[kind], g + 1)
                pool.tensor_tensor(rstd[:, g % 2, 0:nb(g)], vare[:, g % 2, 0:nb(g)],
                                   minus_half[:, 0:nb(g)], ALU.pow).then_inc(rstd_ok[kind], 1)

            tail = MCH[2][1]
            for stage, i in PLAN:
                if stage == "ln1_stats":
                    root(0, i)
                elif stage == "ln1_norm":
                    pool.wait_ge(S["high0"], i + 1)
                    x = blocks(xn[:, i % 2, 0:128 * GW[i]])
                    n = nb(i)
                    pool.tensor_tensor(hl[:, i % 2, 0:n, 1, :], x, hl[:, i % 2, 0:n, 0, :], ALU.subtract)\
                        .then_inc(hl_ok[0], 1)
                elif stage == "residual":
                    pool.wait_ge(ld["rows"], 16)
                    pool.tensor_tensor(blocks(res[:, cut(i)]), blocks(res[:, cut(i)]),
                                       over(row("bo"), nb(i)), ALU.add).then_inc(S["res_bo"], 1)
                    pool.wait_ge(S["res_bo"], i + 1)
                    pool.tensor_tensor(res[:, cut(i)], res[:, cut(i)], xn[:, i % 2, 0:128 * GW[i]],
                                       ALU.add).then_inc(S["res_1"], 1)
                elif stage == "content_b":
                    pool.wait_ge(S["vc_sb"], i + 1)
                    pool.tensor_tensor(blocks(vc[:, i, 0:256]), blocks(vc[:, i, 0:256]), over(row("bvc"), 4), ALU.add)
                    pool.tensor_tensor(blocks(vc[0:tail, i, 256:384]), blocks(vc[0:tail, i, 256:384]),
                                       row("bvc")[0:tail, :].unsqueeze(1).to_broadcast([tail, 2, 64]), ALU.add)\
                        .then_inc(S["vc_b"], 1)
                elif stage == "streams":
                    if i == 0:
                        pool.wait_ge(S["score_mm"], NP)
                        pool.memset(keyz[:, :, :, :], 0.0).then_inc(S["key_zeros"], 1)
                    pool.wait_ge(S["cum_sb"], i + 1)
                    link(pool.tensor_tensor(cum[:, i % 2, 0, :], cum[:, i % 2, 0, :], cos_n[:, :], ALU.mult))
                    link(pool.tensor_tensor(cum[:, i % 2, 1, :], cum[:, i % 2, 1, :], sin_n[:, :], ALU.mult))
                    pool.tensor_tensor(h0s[:, i, :], cum[:, i % 2, 0, :], cum[:, i % 2, 1, :],
                                       ALU.add).then_inc(S["pos_sb"], 1)
                elif stage == "ln2_stats":
                    root(1, i)
                elif stage == "ln3_stats":
                    root(2, i)
                elif stage == "expert_out":
                    g = i // E
                    pool.wait_ge(S["scaled_sb"], i + 1)
                    pool.wait_ge(S["rb_sb"], g + 1)
                    if i > 0:
                        pool.wait_ge(S["acc_sb"], i)
                    pool.tensor_tensor(acc[:, g % 2, 0:128 * GW[g]], acc[:, g % 2, 0:128 * GW[g]],
                                       scaled[:, i % 2, 0:128 * GW[g]], ALU.add).then_inc(S["acc_sb"], 1)

        @block.scalar
        def _(act):
            act.dma_start(phase[:, :, :], phase_d).then_inc(ld["phase"], 16)
            act.dma_start(cols[:, :], cols_d).then_inc(ld["cols"], 16)
            act.dma_start(ident[:, :], const_d[:, 0:128]).then_inc(ld["ident"], 16)
            act.dma_start(rows[:, :], rows_d).then_inc(ld["rows"], 16)
            act.wait_ge(ld["cols"], 16)
            for v in range(2):
                act.wait_ge(ld["pixa" if v == 0 else "pixb"], 16)
                for c in range(CH):
                    act.activation(feat[:, 4 * v:4 * v + 4, c, :], pix[:, v, 0, :].rearrange("p (b s) -> p b s", b=4),
                                   ACT.Identity, scale=col("conv_w", 4 * c), bias=col("conv_b", c))\
                        .then_inc(S["tap0"], 1)
                if v == 0:
                    act.wait_ge(S["reduced"], 1)
                    act.activation(sin_p[:, :], phase[:, 0, :], ACT.Sin)
                    act.activation(turns[:, :], phase[:, 0, :], ACT.Abs).then_inc(S["base_abs"], 1)
                    act.wait_ge(S["base_abs"], 1)
                    act.activation(cos_p[:, :], turns[:, :], ACT.Sin, scale=-1.0, bias=col("half_pi"))\
                        .then_inc(S["base_trig"], 1)

            for stage, i in PLAN:
                if stage == "qkv":
                    act.wait_ge(S["v_mm"], i + 1)
                    if i >= 4:
                        act.wait_ge(S["mix_mm"], i - 3)
                    act.activation(vs[0:SC, i % 4, :], ps[0:SC, 1, 0:256], ACT.Copy).then_inc(S["v_sb"], 1)
                elif stage == "exps":
                    act.wait_ge(S["rowmax"], i + 1)
                    for k in range(4):
                        ins = act.activation(probs[0:SC, i % 2, k, :],
                                             ps[0:SC, 2 + 2 * (i % 2) + k // 2, SI * (k % 2):SI * (k % 2) + SI],
                                             ACT.Exp, bias=negmax[0:SC, i % 2, k:k + 1],
                                             accum_out=rsum[0:SC, i % 2, k:k + 1])
                    ins.then_inc(S["exps"], 1)
                elif stage == "probs_t":
                    act.wait_ge(S["pt_mm"], i + 1)
                    act.activation(probs_t[0:SC, i % 2, 1, :], ps[0:SC, 3 + 2 * (i % 2), 0:2 * SI], ACT.Copy)\
                        .then_inc(S["pt_a"], 1)
                elif stage == "mix":
                    act.wait_ge(S["mix_mm"], i + 1)
                    act.activation(mixed[:, i % 2, :], ps[:, 7, 0:SI], ACT.Identity, bias=col("bv"))\
                        .then_inc(S["mix_sb"], 1)
                elif stage == "tok_out":
                    act.wait_ge(S["tok_mm"], i + 1)
                    act.activation(h0s[:, i, 0:SI], ps[:, 6, 0:SI], ACT.Identity, bias=col("bo"))\
                        .then_inc(S["h0_sb"], 1)
                elif stage == "h0_t":
                    act.wait_ge(S["ht_mm"], i + 1)
                    act.activation(res[:, cut(i)], ps[:, 6, 0:128 * GW[i]], ACT.Copy).then_inc(S["h0t"], 1)
                elif stage in ("xn_t", "xn2_t"):
                    base = 0 if stage == "xn_t" else NXT
                    for s, ws in enumerate(xt_steps(i)):
                        n = base + XT_DONE[i] - len(xt_steps(i)) + s
                        act.wait_ge(S["xt_mm"], n + 1)
                        c = GC[i] + 128 * ws[0]
                        act.activation(xhl[:, :, c:c + 128 * len(ws)].rearrange("p h (w t) -> p w h t", t=128),
                                       ps[:, 7 - s, 0:256 * len(ws)].rearrange("p (w h t) -> p w h t", h=2, t=128),
                                       ACT.Copy).then_inc(S["xhl_sb"], 1)
                elif stage == "gate_t":
                    act.wait_ge(S["mg_z"], i + 1)
                    act.activation(tg[:, i, 0:nb(i)], zg[:, i, 0:nb(i)], ACT.Tanh, scale=0.5)\
                        .then_inc(S["mg_t"], 1)
                elif stage == "hidden":
                    act.wait_ge(S["hid_mm"], i + 1)
                    if i >= 2:
                        act.wait_ge(S["ph_mm"], i - 1)
                    act.activation(hid[:, i % 2, :, :], ps[:, 2:4, 0:L], ACT.Tanh, bias=col("kq1"))\
                        .then_inc(S["hid_sb"], 1)
                elif stage == "phases":
                    act.wait_ge(S["ph_mm"], i + 1)
                    act.activation(trig[:, 0, L * i:L * i + L], ps[:, 4, 0:L], ACT.Tanh, bias=col("k2"))
                    act.activation(trig[:, 1, L * i:L * i + L], ps[:, 5, 0:L], ACT.Tanh, bias=col("q2"))\
                        .then_inc(S["ph_sb"], 1)
                elif stage == "content":
                    act.wait_ge(S["vc_mm"], i + 1)
                    tail = MCH[2][1]
                    act.activation(vc[:, i, 0:256], ps[:, 1, 0:256], ACT.Copy)
                    act.activation(vc[0:tail, i, 256:384], ps[0:tail, 1, 256:384], ACT.Copy)\
                        .then_inc(S["vc_sb"], 1)
                elif stage == "trig":
                    act.wait_ge(S["ph_abs"], i + 1)
                    if i == 0:
                        act.wait_ge(S["key_zeros"], 1)
                    else:
                        if i >= 2:
                            act.wait_ge(S["mem_mm"], i - 1)
                    act.activation(trig[:, 1, L * i:L * i + L], trig[:, 1, L * i:L * i + L], ACT.Sin,
                                   scale=col("sin_scale"), bias=col("sin_bias"))
                    for h in range(2):
                        r = slice(64 * h, 64 * h + 64)
                        ins = act.activation(keyz[r, i % 2, h, :], trig[r, 0, L * i:L * i + L], ACT.Sin,
                                             scale=col("sin_scale", 0, 64 * h, 64 * h + 64),
                                             bias=col("sin_bias", 0, 64 * h, 64 * h + 64))
                    ins.then_inc(S["trig_sb"], 1)
                elif stage == "recall":
                    act.wait_ge(S["rec_mm"], i + 1)
                    act.activation(cons[:, L * i:L * i + L], ps[:, 1, 0:L], ACT.Copy)\
                        .then_inc(S["rec_sb"], 1)
                elif stage == "norm_s":
                    act.wait_ge(S["ns_mm"], i + 1)
                    if i >= 2:
                        act.wait_ge(S["ao_mm"], i - 1)
                    act.activation(ns[:, i % 2, 0:128 * GW[i]], ps[:, 6, 0:128 * GW[i]], ACT.Identity,
                                   scale=col("ln_g"), bias=col("ln_b")).then_inc(S["ns_sb"], 1)
                elif stage == "route_t":
                    act.wait_ge(S["route_d"], i + 1)
                    act.activation(tl[:, i, 0:nb(i)], dl[:, i, 0:nb(i)], ACT.Tanh, scale=0.5)\
                        .then_inc(S["route_t"], 1)
                elif stage == "weights_t":
                    act.wait_ge(S["wt_mm"], i + 1)
                    if i >= 2:
                        act.wait_ge(S["wide_mm"], E * (i - 1))
                    act.activation(wt[:, i % 2, 0:128 * GW[i]], ps[0:32, 6, 0:128 * GW[i]], ACT.Copy)\
                        .then_inc(S["wt_sb"], 1)
                elif stage == "expert":
                    g = i // E
                    n = 128 * GW[g]
                    for j in range(2):
                        k = 2 * i + j
                        act.wait_ge(S["e1_mm"], k + 1)
                        if i >= 2:
                            act.wait_ge(S["e2_mm"], i - 1)
                        halves = ps[:, 2 * j:2 * j + 2, 0:n]
                        if GW[g] <= 2:
                            halves = ps[:, 2 * j, 0:2 * n].rearrange("p (h t) -> p h t", h=2)
                        act.activation(hidden_e[:, k % 4, 0:2 * n].rearrange("p (h t) -> p h t", h=2),
                                       halves, ACT.Gelu, bias=col("b1", 2 * (i % E) + j))\
                            .then_inc(S["gelu"], 1)
                elif stage == "wide":
                    n = 128 * GW[i // E]
                    act.wait_ge(S["wide_mm"], i + 1)
                    if i >= 2:
                        act.wait_ge(S["scaled_sb"], i - 1)
                    act.activation(wide[:, i % 2, 0:n], ps[:, 4 + i % 2, 0:n], ACT.Copy).then_inc(S["wide_sb"], 1)

        @block.vector
        def _(dve):
            steps = [0]

            def link(ins):
                steps[0] += 1
                ins.then_inc(S["vchain"], 1)
                dve.wait_ge(S["vchain"], steps[0])

            dve.wait_ge(ld["phase"], 16)
            raw = phase[:, 0, :]
            link(dve.tensor_scalar(turns[:, :], raw, float(1 / (2 * np.pi)), ROUND, ALU.mult, ALU.add))
            link(dve.tensor_scalar(turns[:, :], turns[:, :], ROUND, None, ALU.subtract))
            for part in (TWO_PI_1, TWO_PI_2, TWO_PI_3):
                link(dve.scalar_tensor_tensor(out=raw, in0=turns[:, :], scalar=-part, in1=raw,
                                              op0=ALU.mult, op1=ALU.add))
            dve.tensor_scalar(raw, raw, PI32, -PI32, ALU.min, ALU.max).then_inc(S["reduced"], 1)
            dve.wait_ge(ld["cols"], 16)
            dve.wait_ge(ld["pixa"], 16)

            def conv_tap(v, tap):
                for c in range(CH):
                    if tap == 1:
                        dve.wait_ge(S["tap0"], 4 * v + c + 1)
                    else:
                        dve.wait_ge(S["conv"], 12 * v + 4 * (tap - 2) + c + 1)
                    o = feat[:, 4 * v:4 * v + 4, c, :]
                    dve.scalar_tensor_tensor(out=o, in0=pix[:, v, tap, :].rearrange("p (b s) -> p b s", b=4),
                                             scalar=col("conv_w", 4 * c + tap), in1=o, op0=ALU.mult, op1=ALU.add)\
                        .then_inc(S["conv"], 1)

            for tap in range(1, 4):
                conv_tap(0, tap)

            def mixer_weights():
                dve.wait_ge(ld["spl"], 16)
                link(dve.tensor_copy(spl_h[:, :], spl_raw[:, :]))
                dve.tensor_tensor(spl_l[:, :], spl_raw[:, :], spl_h[:, :].bitcast(F32), ALU.subtract)\
                    .then_inc(S["split"], 1)
                dve.wait_ge(ld["rows"], 16)
                dve.wait_ge(S["split"], 1)
                dve.tensor_copy(gate_hl[:, 0, :], spl_h[:, NSPL - 24:NSPL].bitcast(F32))
                dve.tensor_copy(gate_hl[:, 1, :], spl_l[:, NSPL - 24:NSPL].bitcast(F32)).then_inc(S["split"], 1)
                wg2 = row("wg2").rearrange("p (a k) -> p a k", a=2)
                dve.tensor_tensor(gd[:, :], wg2[:, 0, :], wg2[:, 1, :], ALU.subtract)
                link(dve.tensor_tensor(gb[:, :], row("bg2")[:, 0:1], row("bg2")[:, 1:2], ALU.subtract))

            def small_weights():
                dve.wait_ge(ld["b2"], 16)
                dve.wait_ge(ld["sel"], 16)
                link(dve.tensor_copy(b2_h[:, :], b2_raw[:, :]))
                dve.tensor_tensor(b2_l[:, :], b2_raw[:, :], b2_h[:, :].bitcast(F32), ALU.subtract)
                dve.tensor_copy(sel[:, :, :], sel_raw).then_inc(S["small"], 1)

            def moments(kind, g, src):
                n = nb(g)
                st = stat[:, g % 2, 0:n, :]
                for k in range(n):
                    ins = dve.bn_stats(stat[:, g % 2, k, :], src[:, 64 * k:64 * k + 64])
                link(ins)
                dve.tensor_tensor(msum[:, 0:n], st[:, :, 1], st[:, :, 4], ALU.add)
                dve.tensor_tensor(mvar[:, 0:n], st[:, :, 2], st[:, :, 5], ALU.add)
                link(dve.tensor_tensor(mdif[:, 0:n], st[:, :, 1], st[:, :, 4], ALU.subtract))
                dve.tensor_scalar(mean[:, g % 2, 0:n], msum[:, 0:n], 0.5, None, ALU.mult)
                link(dve.tensor_tensor(msq[:, 0:n], mdif[:, 0:n], mdif[:, 0:n], ALU.mult))
                link(dve.scalar_tensor_tensor(out=mvar[:, 0:n], in0=msq[:, 0:n], scalar=16.0,
                                              in1=mvar[:, 0:n], op0=ALU.mult, op1=ALU.add))
                dve.tensor_scalar(vare[:, g % 2, 0:n], mvar[:, 0:n], 1.0 / 64, EPS, ALU.mult, ALU.add)\
                    .then_inc(var_ok[kind], 1)

            def normalise(kind, g, src, dst):
                dve.wait_ge(rstd_ok[kind], g + 1)
                for k in range(nb(g)):
                    ins = dve.tensor_scalar(dst[:, 64 * k:64 * k + 64], src[:, 64 * k:64 * k + 64],
                                            mean[:, g % 2, k:k + 1], rstd[:, g % 2, k:k + 1],
                                            ALU.subtract, ALU.mult)
                return ins

            def split_tokens(kind, g):
                n = nb(g)
                x = blocks(xn[:, g % 2, 0:64 * n])
                high = dve.tensor_copy(hl[:, g % 2, 0:n, 0, :].bitcast(F32R), x)
                if kind == 0:
                    high.then_inc(S["high0"], 1)
                    return
                link(high)
                dve.tensor_tensor(hl[:, g % 2, 0:n, 1, :], x, hl[:, g % 2, 0:n, 0, :], ALU.subtract)\
                    .then_inc(hl_ok[kind], 1)

            def pick(n, values, one_hot, best):
                link(dve.tensor_reduce(best, values, AX.X, ALU.max))
                link(dve.tensor_tensor(eq[:, 0:n, :], values, spread(best, n, 8), ALU.is_equal))
                link(dve.tensor_tensor(eq[:, 0:n, :], eq[:, 0:n, :], over(row("rank"), n), ALU.mult))
                link(dve.tensor_reduce(top[:, 3, 0:n], eq[:, 0:n, :], AX.X, ALU.max))
                link(dve.tensor_tensor(one_hot, eq[:, 0:n, :], spread(top[:, 3, 0:n], n, 8), ALU.is_equal))

            for stage, i in PLAN:
                if stage == "qkv":
                    dve.wait_ge(S["qk_mm"], i + 1)
                    dve.tensor_scalar(qs[:, i, :], ps[:, 0, 0:SI], col("bq"), float(D) ** -0.5, ALU.add, ALU.mult)
                    for h in range(2):
                        r = slice(64 * h, 64 * h + 64)
                        ins = dve.tensor_scalar(ks[r, h, i, :], ps[r, 0, SI:2 * SI],
                                                col("bk", 0, 64 * h, 64 * h + 64), None, ALU.add)
                    ins.then_inc(S["qk_sb"], 1)
                    if i == 0:
                        mixer_weights()
                        dve.wait_ge(ld["pixb"], 16)
                    if 1 <= i <= 3:
                        conv_tap(1, i)
                elif stage == "scores":
                    dve.wait_ge(S["score_mm"], i + 1)
                    b0 = 2 + 2 * (i % 2)
                    dve.tensor_reduce(negmax[0:SC, i % 2, :].rearrange("p (h c) -> p h c", h=2),
                                      ps[0:SC, b0:b0 + 2, 0:2 * SI].rearrange("p h (c t) -> p h c t", c=2),
                                      AX.X, ALU.max, negate=True).then_inc(S["rowmax"], 1)
                elif stage == "probs_n":
                    dve.wait_ge(S["exps"], i + 1)
                    dve.reciprocal(rinv[0:SC, i % 2, :], rsum[0:SC, i % 2, :]).then_inc(S["rowinv"], 1)
                    dve.wait_ge(S["rowinv"], i + 1)
                    dve.tensor_tensor(probs[0:SC, i % 2, :, :], probs[0:SC, i % 2, :, :],
                                      rinv[0:SC, i % 2, :].unsqueeze(2).to_broadcast([SC, 4, SI]), ALU.mult)\
                        .then_inc(S["pnorm"], 1)
                elif stage == "probs_t":
                    dve.wait_ge(S["pt_mm"], i + 1)
                    dve.tensor_copy(probs_t[0:SC, i % 2, 0, :], ps[0:SC, 2 + 2 * (i % 2), 0:2 * SI])\
                        .then_inc(S["pt_v"], 1)
                elif stage == "ln1_stats":
                    dve.wait_ge(S["h0t"], i + 1)
                    moments(0, i, res[:, cut(i)])
                elif stage == "ln1_norm":
                    if i >= 2:
                        dve.wait_ge(S["res_1"], i - 1)
                        dve.wait_ge(S["xt_mm"], XT_DONE[i - 2])
                    link(normalise(0, i, res[:, cut(i)], xn[:, i % 2, :]))
                    split_tokens(0, i)
                elif stage == "gate_z":
                    n = nb(i)
                    dve.wait_ge(S["mg_mm"], i + 1)
                    link(dve.tensor_reduce(gu[:, 0:n, :],
                                           ps[:, 6, 0:32 * n].rearrange("p (k a j) -> p k j a", a=2, j=16),
                                           AX.X, ALU.add))
                    link(dve.tensor_tensor(gu[:, 0:n, :], gu[:, 0:n, :], over(row("bg1"), n), ALU.add))
                    link(dve.scalar_tensor_tensor(out=gu[:, 0:n, :], in0=gu[:, 0:n, :], scalar=0.0,
                                                  in1=over(gd[:, :], n), op0=ALU.max, op1=ALU.mult))
                    link(dve.tensor_reduce(zg[:, i, 0:n], gu[:, 0:n, :], AX.X, ALU.add))
                    dve.tensor_scalar(zg[:, i, 0:n], zg[:, i, 0:n], gb[:, 0:1], None, ALU.add)\
                        .then_inc(S["mg_z"], 1)
                elif stage == "gate_p":
                    n = nb(i)
                    dve.wait_ge(S["mg_t"], i + 1)
                    dve.tensor_scalar(p0[:, i, 0:n], tg[:, i, 0:n], 0.5, 0.5, ALU.mult, ALU.add)
                    dve.tensor_scalar(p1[:, i, 0:n], tg[:, i, 0:n], -0.5, 0.5, ALU.mult, ALU.add)\
                        .then_inc(S["mg_p"], 1)
                elif stage == "streams":
                    dve.wait_ge(S["vp_mm"], i + 1)
                    if i == 0:
                        dve.wait_ge(S["base_trig"], 1)
                        dve.wait_ge(S["consts"], 1)
                    if i >= 2:
                        dve.wait_ge(S["pos_sb"], i - 1)
                    for k, t in enumerate((cos_p, sin_p)):
                        ins = dve.scalar_tensor_tensor(out=y[:, i % 2, k, :], in0=ps[:, 0, 0:L], scalar=col("vp"),
                                                       in1=t[:, :], op0=ALU.add, op1=ALU.mult)
                    ins.then_inc(S["vp_used"], 1)
                    dve.wait_ge(S["vp_used"], i + 1)
                    for k in range(2):
                        ins = dve.tensor_tensor_scan(cum[:, i % 2, k, :], ones[:, :], y[:, i % 2, k, :], 0.0,
                                                     ALU.mult, ALU.add)
                    ins.then_inc(S["cum_sb"], 1)
                elif stage == "phase_abs":
                    if i == 1:
                        small_weights()
                    dve.wait_ge(S["ph_sb"], i + 1)
                    t = trig[:, :, L * i:L * i + L]
                    dve.scalar_tensor_tensor(out=t, in0=t, scalar=col("sign"), in1=t, op0=ALU.mult, op1=ALU.max)\
                        .then_inc(S["ph_abs"], 1)
                elif stage == "memory":
                    dve.wait_ge(S["mem_mm"], i + 1)
                    if i == 0:
                        dve.wait_ge(ld["mask"], 16)
                    if i >= 2:
                        dve.wait_ge(S["rec_mm"], i - 1)
                    b0, full, tail = 2 + 2 * (i % 2), MOFF[2], MCH[2][1]
                    dve.tensor_tensor(mem[:, i % 2, :, 0:full], ps[:, b0:b0 + 2, 0:full],
                                      over(mask[:, 0:full], 2), ALU.mult)
                    dve.tensor_tensor(mem[0:tail, i % 2, :, full:MEND], ps[0:tail, b0:b0 + 2, full:MEND],
                                      mask[0:tail, full:MEND].unsqueeze(1).to_broadcast([tail, 2, tail]), ALU.mult)\
                        .then_inc(S["mem_sb"], 1)
                elif stage == "combine":
                    n = nb(i)
                    if i >= 2:
                        dve.wait_ge(S["ns_mm"], i - 1)
                    dve.wait_ge(S["comb_mm"], i + 1)
                    dve.wait_ge(S["mg_p"], i + 1)
                    dve.tensor_tensor(blocks(c1[:, 0:64 * n]), blocks(ps[:, 6, 0:64 * n]),
                                      spread(p0[:, i, 0:n], n), ALU.mult)
                    link(dve.tensor_tensor(blocks(c2[:, 0:64 * n]), blocks(ps[:, 7, 0:64 * n]),
                                           spread(p1[:, i, 0:n], n), ALU.mult))
                    dve.tensor_tensor(comb[:, i % 2, 0:64 * n], c1[:, 0:64 * n], c2[:, 0:64 * n], ALU.add)\
                        .then_inc(S["comb_sb"], 1)
                elif stage == "ln2_stats":
                    dve.wait_ge(S["comb_sb"], i + 1)
                    moments(1, i, comb[:, i % 2, :])
                elif stage == "ln2_norm":
                    normalise(1, i, comb[:, i % 2, :], comb[:, i % 2, :]).then_inc(hl_ok[1], 1)
                elif stage == "attn_out":
                    n = 64 * nb(i)
                    dve.wait_ge(S["ao_mm"], i + 1)
                    dve.wait_ge(S["res_1"], i + 1)
                    dve.tensor_tensor(res[:, cut(i)], ps[:, 7, 0:n], res[:, cut(i)], ALU.add).then_inc(S["h1_sb"], 1)
                elif stage == "ln3_stats":
                    dve.wait_ge(S["h1_sb"], i + 1)
                    moments(2, i, res[:, cut(i)])
                elif stage == "ln3_norm":
                    if i == 0:
                        dve.wait_ge(S["res_1"], NG)
                        dve.wait_ge(S["xt_mm"], NXT)
                    if i >= 2:
                        dve.wait_ge(S["xt_mm"], NXT + XT_DONE[i - 2])
                    link(normalise(2, i, res[:, cut(i)], xn[:, i % 2, :]))
                    split_tokens(2, i)
                elif stage == "route":
                    n = nb(i)
                    dve.wait_ge(S["lg_mm"], i + 1)
                    dve.tensor_reduce(lg[:, 0:n, :], ps[:, 6, 0:16 * n].rearrange("p (k a j) -> p k j a", a=2, j=8),
                                      AX.X, ALU.add).then_inc(S["lg_sb"], 1)
                    dve.wait_ge(S["lg_sb"], i + 1)
                    link(dve.tensor_tensor(lg[:, 0:n, :], lg[:, 0:n, :], over(row("bg"), n), ALU.add))
                    pick(n, lg[:, 0:n, :], k1[:, 0:n, :], top[:, 0, 0:n])
                    link(dve.scalar_tensor_tensor(out=lg[:, 0:n, :], in0=k1[:, 0:n, :], scalar=-3.0e38,
                                                  in1=lg[:, 0:n, :], op0=ALU.mult, op1=ALU.add))
                    pick(n, lg[:, 0:n, :], k2[:, 0:n, :], top[:, 1, 0:n])
                    dve.tensor_tensor(dl[:, i, 0:n], top[:, 0, 0:n], top[:, 1, 0:n], ALU.subtract)\
                        .then_inc(S["route_d"], 1)
                elif stage == "route_t":
                    n = nb(i)
                    dve.wait_ge(S["route_t"], i + 1)
                    dve.tensor_scalar(top[:, 0, 0:n], tl[:, i, 0:n], 0.5, 0.5, ALU.mult, ALU.add)
                    link(dve.tensor_scalar(top[:, 1, 0:n], tl[:, i, 0:n], -0.5, 0.5, ALU.mult, ALU.add))
                    dve.tensor_tensor(k1[:, 0:n, :], k1[:, 0:n, :], spread(top[:, 0, 0:n], n, 8), ALU.mult)
                    link(dve.tensor_tensor(k2[:, 0:n, :], k2[:, 0:n, :], spread(top[:, 1, 0:n], n, 8), ALU.mult))
                    link(dve.tensor_tensor(k1[:, 0:n, :], k1[:, 0:n, :], k2[:, 0:n, :], ALU.add))
                    if i >= 1:
                        dve.wait_ge(S["wt_mm"], i)
                    wv = k1[:, 0:n, :].rearrange("p (w h) e -> p w (h e)", h=2)
                    link(dve.tensor_copy(wsp[:, 0:GW[i], 0, :].bitcast(F32R), wv))
                    dve.tensor_tensor(wsp[:, 0:GW[i], 1, :], wv, wsp[:, 0:GW[i], 0, :], ALU.subtract)\
                        .then_inc(S["route_w"], 1)
                elif stage == "route_bias":
                    n = 64 * nb(i)
                    dve.wait_ge(S["rb_mm"], i + 1)
                    if i == 0:
                        dve.wait_ge(S["w1split"], 1)
                    if i >= 2:
                        dve.wait_ge(S["fin_mm"], i - 1)
                    dve.tensor_copy(acc[:, i % 2, 0:n], ps[:, 7, 0:n]).then_inc(S["rb_sb"], 1)
                elif stage == "expert_out":
                    g = i // E
                    n = nb(g)
                    dve.wait_ge(S["e2_mm"], i + 1)
                    dve.wait_ge(S["wide_sb"], i + 1)
                    if i >= 2:
                        dve.wait_ge(S["acc_sb"], i - 1)
                    dve.tensor_tensor(scaled[:, i % 2, 0:64 * n], ps[:, 4 + i % 2, 0:64 * n],
                                      wide[:, i % 2, 0:64 * n], ALU.mult).then_inc(S["scaled_sb"], 1)
                elif stage == "finish":
                    n = 64 * nb(i)
                    dve.wait_ge(S["fin_mm"], i + 1)
                    dve.tensor_tensor(res[:, cut(i)], ps[:, 7, 0:n], res[:, cut(i)], ALU.add).then_inc(S["out_sb"], 1)

        @block.tensor
        def _(pe):
            def exact(outp, lhs_parts, rhs_parts, start=True, stop=True):
                pe.matmul(outp, lhs_parts[0], rhs_parts[0], start=start, stop=False)
                return pe.matmul(outp, lhs_parts[1], rhs_parts[1], start=False, stop=stop)

            reader = {}

            def take(bank, read_out, count):
                if bank in reader:
                    pe.wait_ge(*reader[bank])
                reader[bank] = (S[read_out], count)

            wq, wk, wo, wv = (tokw[:, 128 * k:128 * k + 128] for k in range(4))
            pe.wait_ge(S["consts"], 1)
            for _ in range(WARM_UP):
                pe.matmul(ps[:, 7, 0:L], ones[:, 0:128], ones[:, :], start=True, stop=True)

            for stage, i in PLAN:
                if stage == "keep_warm":
                    if 7 in reader:
                        pe.wait_ge(*reader[7])
                    for _ in range(i):
                        pe.matmul(ps[:, 7, 0:L], ones[:, 0:128], ones[:, :], start=True, stop=True)
                elif stage == "qkv":
                    if i == 0:
                        pe.wait_ge(ld["tokw"], 16)
                    pe.wait_ge(S["conv"], 12 if i < 4 else 24)
                    if i >= 1:
                        pe.wait_ge(S["qk_sb"], i)
                    pe.matmul(ps[:, 0, 0:SI], wq, featf[:, i, :], start=True, stop=True)
                    pe.matmul(ps[:, 0, SI:2 * SI], wk, featf[:, i, :], start=True, stop=True).then_inc(S["qk_mm"], 1)
                    if i >= 1:
                        pe.wait_ge(S["v_sb"], i)
                    for c in range(2):
                        ins = pe.matmul(ps[0:SC, 1, 128 * c:128 * c + 128], featf[:, i, SC * c:SC * c + SC], wv,
                                        start=True, stop=True)
                    ins.then_inc(S["v_mm"], 1)
                elif stage == "scores":
                    pe.wait_ge(S["qk_sb"], i + 1)
                    if i == 0:
                        pe.wait_ge(S["zeros"], 1)
                    if i >= 2:
                        pe.wait_ge(S["pt_v"], i - 1)
                        pe.wait_ge(S["pt_a"], i - 1)
                    for h in range(2):
                        for c in range(2):
                            ins = pe.matmul(ps[0:SC, 2 + 2 * (i % 2) + h, SI * c:SI * c + SI],
                                            qs[:, i, SC * c:SC * c + SC], ks[:, h, i, :], start=True, stop=True)
                    ins.then_inc(S["score_mm"], 1)
                elif stage == "probs_t":
                    pe.wait_ge(S["pnorm"], i + 1)
                    if i == 0:
                        pe.wait_ge(ld["ident"], 16)
                    for h in range(2):
                        for c in range(2):
                            for t in range(2):
                                ins = pe.transpose(ps[0:SC, 2 + 2 * (i % 2) + h, SI * t + SC * c:SI * t + SC * c + SC],
                                                   probs[0:SC, i % 2, 2 * h + c, SC * t:SC * t + SC],
                                                   ident[0:SC, 0:SC])
                    ins.then_inc(S["pt_mm"], 1)
                elif stage == "mix":
                    pe.wait_ge(S["pt_v"], i + 1)
                    pe.wait_ge(S["pt_a"], i + 1)
                    pe.wait_ge(S["v_sb"], i + 1)
                    take(7, "mix_sb", i + 1)
                    for h in range(2):
                        for t in range(2):
                            k = 2 * t + h
                            ins = pe.matmul(ps[64 * h:64 * h + 64, 7, 0:SI], vs[0:SC, i % 4, 64 * k:64 * k + 64],
                                            probs_t[0:SC, i % 2, h, SI * t:SI * t + SI], start=(t == 0), stop=(t == 1))
                    ins.then_inc(S["mix_mm"], 1)
                elif stage == "tok_out":
                    pe.wait_ge(S["mix_sb"], i + 1)
                    take(6, "h0_sb", i + 1)
                    pe.matmul(ps[:, 6, 0:SI], wo, mixed[:, i % 2, :], start=True, stop=True).then_inc(S["tok_mm"], 1)
                elif stage == "h0_t":
                    pe.wait_ge(S["h0_sb"], LAST_PAIR[i] + 1)
                    if i == 0:
                        pe.wait_ge(ld["txt"], 16)
                    take(6, "h0t", i + 1)
                    for w in range(GW[i]):
                        c = GC[i] + 128 * w
                        ins = pe.transpose(ps[:, 6, 128 * w:128 * w + 128], h0f[:, c:c + 128], ident[:, :])
                    ins.then_inc(S["ht_mm"], 1)
                elif stage in ("xn_t", "xn2_t"):
                    second = stage == "xn2_t"
                    pe.wait_ge(hl_ok[2 if second else 0], i + 1)
                    for s, ws in enumerate(xt_steps(i)):
                        n = (NXT if second else 0) + XT_DONE[i] - len(xt_steps(i)) + s
                        take(7 - s, "xhl_sb", n + 1)
                        for w in ws:
                            for h in range(2):
                                k = 2 * w + h
                                q = 2 * (w - ws[0]) + h
                                ins = pe.transpose(ps[:, 7 - s, 128 * q:128 * q + 128],
                                                   hl[:, i % 2, k, :, :].rearrange("p a d -> p (a d)"), ident[:, :])
                        ins.then_inc(S["xt_mm"], 1)
                elif stage == "mix_gate":
                    if i == 0:
                        pe.wait_ge(S["split"], 2)
                    pe.wait_ge(S["xhl_sb"], XT_DONE[i])
                    take(6, "mg_z", i + 1)
                    for k in range(nb(i)):
                        c = GC[i] + 128 * (k // 2)
                        ins = pe.matmul(ps[:, 6, 32 * k:32 * k + 32], xhl[:, k % 2, c:c + 128],
                                        gate_hl[:, :, 0:16], start=True, stop=True)
                    ins.then_inc(S["mg_mm"], 1)
                elif stage == "hidden":
                    pe.wait_ge(S["xhl_sb"], XT_DONE[LAST_GROUP[i]])
                    if i == 0:
                        pe.wait_ge(S["split"], 1)
                        pe.wait_ge(S["pt_v"], NP - 1)
                        pe.wait_ge(S["pt_a"], NP - 1)
                    else:
                        pe.wait_ge(S["hid_sb"], i)
                    wk1 = (split(spl_h, "kq1"), split(spl_l, "kq1"))
                    for h in range(2):
                        x = xhl[:, h, L * i:L * i + L]
                        ins = exact(ps[:, 2 + h, 0:L], wk1, (x, x))
                    ins.then_inc(S["hid_mm"], 1)
                elif stage == "values":
                    if i == 0:
                        pe.wait_ge(S["qk_sb"], NP)
                    else:
                        pe.wait_ge(S["vp_used"], i)
                    for h in range(2):
                        x = xhl[:, h, L * i:L * i + L]
                        wv = tuple(split(p, "vp")[:, 128 * h:128 * h + 128] for p in (spl_h, spl_l))
                        ins = exact(ps[:, 0, 0:L], wv, (x, x), start=(h == 0), stop=(h == 1))
                    ins.then_inc(S["vp_mm"], 1)
                elif stage == "content":
                    if i == 0:
                        pe.wait_ge(S["v_sb"], NP)
                    else:
                        pe.wait_ge(S["vc_sb"], i)
                    for k, (m, size) in enumerate(MCH):
                        for h in range(2):
                            x = xhl[:, h, L * i + m:L * i + m + size]
                            o = 128 * k + 64 * h
                            ins = exact(ps[0:size, 1, o:o + 64], (x, x), (split(spl_h, "vc"), split(spl_l, "vc")))
                    ins.then_inc(S["vc_mm"], 1)
                elif stage == "phases":
                    pe.wait_ge(S["hid_sb"], i + 1)
                    if i == 0:
                        pe.wait_ge(ld["attw"], 16)
                        pe.wait_ge(S["pt_v"], NP)
                        pe.wait_ge(S["pt_a"], NP)
                    else:
                        pe.wait_ge(S["ph_sb"], i)
                    for r in range(2):
                        for h in range(2):
                            ins = pe.matmul(ps[64 * h:64 * h + 64, 4 + r, 0:L], attw[:, 64 * r:64 * r + 64],
                                            hid[:, i % 2, h, :], start=True, stop=True)
                    ins.then_inc(S["ph_mm"], 1)
                elif stage == "memory":
                    pe.wait_ge(S["trig_sb"], i + 1)
                    if i == 0:
                        pe.wait_ge(S["hid_sb"], NP)
                    if i == 1:
                        pe.wait_ge(S["ph_sb"], NP)
                    if i >= 2:
                        pe.wait_ge(S["mem_sb"], i - 1)
                    for h in range(2):
                        for k, (m, size) in enumerate(MCH):
                            ins = pe.matmul(ps[0:size, 2 + 2 * (i % 2) + h, MOFF[k]:MOFF[k] + L - m],
                                            keyz[:, i % 2, h, m:m + size], trig[:, 1, L * i + m:L * i + L],
                                            start=True, stop=True)
                    ins.then_inc(S["mem_mm"], 1)
                elif stage == "recall":
                    pe.wait_ge(S["mem_sb"], i + 1)
                    pe.wait_ge(S["vc_b"], i + 1)
                    if i == 0:
                        pe.wait_ge(S["vc_sb"], NP)
                    else:
                        pe.wait_ge(S["rec_sb"], i)
                    for h in range(2):
                        for k, (m, size) in enumerate(MCH):
                            o = 128 * k + 64 * h
                            ins = pe.matmul(ps[64 * h:64 * h + 64, 1, m:L], vc[0:size, i, o:o + 64],
                                            mem[0:size, i % 2, h, MOFF[k]:MOFF[k] + L - m],
                                            start=(k == 0), stop=(k == len(MCH) - 1))
                    ins.then_inc(S["rec_mm"], 1)
                elif stage == "combine":
                    pe.wait_ge(S["rec_sb"], LAST_PAIR[i] + 1)
                    pe.wait_ge(S["pos_sb"], LAST_PAIR[i] + 1)
                    take(6, "comb_sb", i + 1)
                    take(7, "comb_sb", i + 1)
                    for bank, src in ((6, h0f), (7, cons)):
                        for w in range(GW[i]):
                            c = GC[i] + 128 * w
                            ins = pe.transpose(ps[:, bank, 128 * w:128 * w + 128], src[:, c:c + 128], ident[:, :])
                    ins.then_inc(S["comb_mm"], 1)
                elif stage == "norm_s":
                    pe.wait_ge(hl_ok[1], i + 1)
                    take(6, "ns_sb", i + 1)
                    for w in range(GW[i]):
                        ins = pe.transpose(ps[:, 6, 128 * w:128 * w + 128], comb[:, i % 2, 128 * w:128 * w + 128],
                                           ident[:, :])
                    ins.then_inc(S["ns_mm"], 1)
                elif stage == "attn_out":
                    pe.wait_ge(S["ns_sb"], i + 1)
                    take(7, "h1_sb", i + 1)
                    for w in range(GW[i]):
                        ins = pe.matmul(ps[:, 7, 128 * w:128 * w + 128], ns[:, i % 2, 128 * w:128 * w + 128],
                                        attw[:, 128:256], start=True, stop=True)
                    ins.then_inc(S["ao_mm"], 1)
                elif stage == "route":
                    pe.wait_ge(S["xhl_sb"], NXT + XT_DONE[i])
                    take(6, "lg_sb", i + 1)
                    for k in range(nb(i)):
                        c = GC[i] + 128 * (k // 2)
                        ins = pe.matmul(ps[:, 6, 16 * k:16 * k + 16], xhl[:, k % 2, c:c + 128],
                                        gate_hl[:, :, 16:24], start=True, stop=True)
                    ins.then_inc(S["lg_mm"], 1)
                elif stage == "weights_t":
                    pe.wait_ge(S["route_w"], i + 1)
                    take(6, "wt_sb", i + 1)
                    for w in range(GW[i]):
                        ins = pe.transpose(ps[0:32, 6, 128 * w:128 * w + 128],
                                           wsp[:, w, :, :].rearrange("p a k -> p (a k)"), ident[:, :])
                    ins.then_inc(S["wt_mm"], 1)
                elif stage == "route_bias":
                    take(7, "rb_sb", i + 1)
                    pe.wait_ge(S["wt_sb"], i + 1)
                    if i == 0:
                        pe.wait_ge(S["small"], 1)
                    x = wt[:, i % 2, 0:128 * GW[i]]
                    exact(ps[:, 7, 0:128 * GW[i]], (b2_h[:, :], b2_l[:, :]), (x, x)).then_inc(S["rb_mm"], 1)
                elif stage == "finish":
                    pe.wait_ge(S["acc_sb"], E * (i + 1))
                    take(7, "out_sb", i + 1)
                    for w in range(GW[i]):
                        ins = pe.transpose(ps[:, 7, 128 * w:128 * w + 128], acc[:, i % 2, 128 * w:128 * w + 128],
                                           ident[:, :])
                    ins.then_inc(S["fin_mm"], 1)
                elif stage == "expert":
                    g = i // E
                    n = 128 * GW[g]
                    if i == 0:
                        pe.wait_ge(S["w1split"], 1)
                        pe.wait_ge(S["vp_used"], NP)
                        pe.wait_ge(S["rec_sb"], NP)
                        pe.wait_ge(S["mem_sb"], NP)
                    pe.wait_ge(S["xhl_sb"], NXT + XT_DONE[g])
                    for j in range(2):
                        k = 2 * i + j
                        if k >= 2:
                            pe.wait_ge(S["gelu"], k - 1)
                        c = 128 * (2 * (i % E) + j)
                        wts = (w1_h[:, c:c + 128], w1_l[:, c:c + 128])
                        if GW[g] <= 2:
                            x = xhl[:, :, GC[g]:GC[g] + n]
                            ins = exact(ps[:, 2 * j, 0:2 * n].rearrange("p (h t) -> p h t", h=2), wts, (x, x))
                        else:
                            for h in range(2):
                                x = xhl[:, h, GC[g]:GC[g] + n]
                                ins = exact(ps[:, 2 * j + h, 0:n], wts, (x, x))
                        ins.then_inc(S["e1_mm"], 1)
                elif stage == "wide":
                    g = i // E
                    n = 128 * GW[g]
                    pe.wait_ge(S["wt_sb"], g + 1)
                    if i >= 2:
                        pe.wait_ge(S["scaled_sb"], i - 1)
                    pe.matmul(ps[:, 4 + i % 2, 0:n], sel[:, i % E, :], wt[:, g % 2, 0:n], start=True, stop=True)\
                        .then_inc(S["wide_mm"], 1)
                elif stage == "expert_out":
                    g = i // E
                    n = 128 * GW[g]
                    pe.wait_ge(S["gelu"], 2 * i + 2)
                    pe.wait_ge(S["wide_sb"], i + 1)
                    if i == 0:
                        pe.wait_ge(ld["w2"], 16)
                    for j in range(2):
                        for h in range(2):
                            ins = pe.matmul(ps[64 * h:64 * h + 64, 4 + i % 2, 0:n], w2[:, 2 * (i % E) + j, :],
                                            hidden_e[:, (2 * i + j) % 4, n * h:n * h + n],
                                            start=(j == 0), stop=(j == 1))
                    ins.then_inc(S["e2_mm"], 1)


def _stack(a):
    return np.concatenate([a, a], axis=0)


def _diagonal(a):
    out = np.zeros((128, 128), np.float32)
    out[0:64, 0:64] = a
    out[64:128, 64:128] = a
    return out


def kernel(**inputs):
    import concourse.bacc as _bacc
    from concourse.bass_utils import run_bass_kernel_spmd as _run

    a = {k: np.ascontiguousarray(v) for k, v in inputs.items()}
    tok = {k[7:]: v for k, v in a.items() if k.startswith("L0_tok_")}
    att = {k[8:]: v for k, v in a.items() if k.startswith("L0_attn_")}
    ffn = {k[7:]: v for k, v in a.items() if k.startswith("L0_ffn_")}

    px = a["x"].reshape(2, 2, 4, IMG // 2, 2, IMG // 2, 2).transpose(0, 1, 4, 6, 2, 3, 5)
    px = px.reshape(2, 2, 4, 4, PATCH, D).transpose(0, 5, 1, 2, 3, 4).reshape(128, 2, 4, 4 * PATCH)
    txt = a["txt"].reshape(2, NP, TXT, D).transpose(0, 3, 1, 2).reshape(128, NP, TXT)

    half = np.arange(128) % 64 < 32
    col = {
        "conv_w": np.broadcast_to(tok["conv_w"].reshape(1, 16), (128, 16)),
        "conv_b": np.broadcast_to(tok["conv_b"].reshape(1, 4), (128, 4)),
        "bq": _stack(tok["bq"]), "bk": _stack(tok["bk"]), "bv": _stack(tok["bv"]), "bo": _stack(tok["bo"]),
        "kq1": np.concatenate([att["bk1"], att["bq1"]]),
        "k2": np.concatenate([att["bk2"]] * 4), "q2": np.concatenate([att["bq2"]] * 4),
        "vp": _stack(att["bvp"]), "ln_g": _stack(att["ln_g"]), "ln_b": _stack(att["ln_b"]),
        "b1": ffn["b1"].reshape(16, 128).T,
        "sign": np.where(half, -1, 1), "sin_scale": np.where(half, -np.pi, np.pi),
        "sin_bias": np.where(half, np.pi / 2, 0), "half_pi": np.full(128, np.pi / 2),
    }
    row = {"bvc": att["bvc"], "bo": att["bo"], "bg1": att["bg1"], "wg2": att["Wg2"].T.reshape(-1),
           "bg2": att["bg2"], "bg": ffn["bg"], "rank": np.arange(8, 0, -1)}
    zero = np.zeros((64, 64), np.float32)
    spl = {"kq1": np.concatenate([att["Wk1"], att["Wq1"]], 1), "vc": att["Wvc"],
           "vp": np.concatenate([att["Wvp"], zero, zero, att["Wvp"]], 1), "g1": att["Wg1"], "gate": ffn["Wg"]}
    pos = np.arange(1, L + 1, dtype=np.float64)
    mask = np.zeros((128, MEND), np.float32)
    for o, (m, size) in zip(MOFF, MCH):
        q = np.arange(m, L)
        k = np.arange(m, m + size)
        mask[0:size, o:o + L - m] = (q[None] >= k[:, None]) / np.sqrt(32 * pos[q])[None]
    b2 = np.zeros((2, 2, E, 2, D), np.float32)
    sel = np.zeros((2, 2, E, E, 2, D), np.float32)
    for h in range(2):
        b2[:, h, :, h, :] = ffn["b2"]
        for e in range(E):
            sel[:, h, e, e, h, :] = 1
    phases = _stack(att["base_phases"][0:L].T)
    arrays = {
        "x_a": px[:, 0], "x_b": px[:, 1],
        "cols": np.concatenate([np.asarray(col[k], np.float32).reshape(128, n) for k, (_, n) in COL.items()], 1),
        "tokw": np.concatenate([_diagonal(tok[k].T) for k in ("wq", "wk", "wo", "wv")], 1),
        "phase": np.stack([phases, np.broadcast_to((1 / np.sqrt(pos)).astype(np.float32), (128, L))], 1),
        "rows": np.broadcast_to(np.concatenate([np.asarray(row[k], np.float32).reshape(-1) for k in ROW]),
                                (128, NROW)),
        "attw": np.concatenate([np.concatenate([att["Wk2"], att["Wk2"], zero], 1),
                                np.concatenate([zero, att["Wq2"], att["Wq2"]], 1),
                                _diagonal(att["Wo"])[0:64], _diagonal(att["Wo"])[64:128]], 0)
        .reshape(2, 2, 64, 128).transpose(1, 2, 0, 3).reshape(128, 256),
        "spl": np.concatenate([_stack(spl[k]) for k in SPL], 1),
        "txt": txt,
        "const": np.concatenate([np.eye(128, dtype=np.float32), mask], 1),
        "w1": _stack(ffn["W1"].transpose(1, 0, 2).reshape(64, E * HID)),
        "w2": ffn["W2"].reshape(16, 128, 64).transpose(1, 0, 2),
        "b2": b2.reshape(32, 128), "sel": sel.reshape(32, E, 128),
    }
    arrays = {f"in_{k}": np.ascontiguousarray(v, dtype=np.float32) for k, v in arrays.items()}

    nc = _bacc.Bacc("TRN2", target_bir_lowering=False, num_devices=1)
    args = [nc.dram_tensor(k, v.shape, F32, kind="ExternalInput").ap() for k, v in arrays.items()]
    out = nc.dram_tensor("out_0", (B * L, D), F32, kind="ExternalOutput").ap()
    fusion_block(nc, *args, out)
    r = _run(nc, [arrays], core_ids=[0])
    return r.results[0]["out_0"].reshape(B, L, D)
```
